# Optimizing a Trainium2 kernel written in Bass

```python
import numpy as np
import jax
import jax.numpy as jnp

def _softmax(x, axis=-1):
    return jax.nn.softmax(x, axis=axis)

def _gelu(x):
    return jax.nn.gelu(x, approximate=True)

def _silu(x):
    return jax.nn.silu(x)

def _sigmoid(x):
    return jax.nn.sigmoid(x)

def _layernorm(x, axis=-1, eps=1e-05):
    m = jnp.mean(x, axis=axis, keepdims=True)
    v = jnp.var(x, axis=axis, keepdims=True)
    return (x - m) / jnp.sqrt(v + eps)

def _scatter_add(tgt, idx, src, axis=0):
    return tgt.at[idx].add(src)

def _segment_sum(src, seg, n):
    return jax.ops.segment_sum(src, seg, n)
kernel_name = 'mk_xattn_seq_d4_seqx_r4_2c7aa2'

def setup_inputs(seed: int=0):
    np.random.seed(seed)
    _w = jnp.asarray

    def _rec_inputs():
        import jax
        import jax.numpy as jnp
        _rk = jax.random.key(seed)
        x = -0.000125 + 0.9999 * jax.random.normal(jax.random.fold_in(_rk, 1), (4, 1024, 256), jnp.float32)
        _lenS = 1024 - jax.random.randint(jax.random.fold_in(_rk, 7), (4,), 0, max(1, 1024 // 4) + 1, jnp.int32)
        _lenS2 = 154 - jax.random.randint(jax.random.fold_in(_rk, 8), (4,), 0, max(1, 154 // 4) + 1, jnp.int32)
        _ctx_2048P = jax.random.normal(jax.random.fold_in(_rk, 11), (4, 16, 512), jnp.float32)
        _ctx_2048c = jax.random.dirichlet(jax.random.fold_in(_rk, 511), 0.3 * jnp.ones((16,), jnp.float32), (4, 154))
        _ctx_2048t = jnp.einsum('bsk,bkd->bsd', _ctx_2048c, _ctx_2048P)
        _ctx_2048t = _ctx_2048t * jax.lax.rsqrt(jnp.mean(jnp.square(_ctx_2048t)) + 1e-12) * 0.953939
        ctx_2048 = 5.36139e-06 + 1.00015 * (_ctx_2048t + 0.3 * jax.random.normal(jax.random.fold_in(_rk, 611), (4, 154, 512), jnp.float32))
        _validS = jnp.arange(1024)[None, :] < _lenS[:, None]
        _validS2 = jnp.arange(154)[None, :] < _lenS2[:, None]
        _causal = jnp.tril(jnp.ones((1024, 1024), dtype=bool))
        mask_S_fk1 = jnp.where(_validS[0], 1.0, 0.0).astype(jnp.float32)
        mask_S_fk0 = jnp.where(_validS[0], 0.0, 1.0).astype(jnp.float32)
        return (x, ctx_2048, mask_S_fk1, mask_S_fk0)
    x, ctx_2048, mask_S_fk1, mask_S_fk0 = _rec_inputs()

    def _L0_xattn_setup():
        import jax, jax.numpy as jnp
        import numpy as np
        HEADS = 16
        HEAD_DIM = 64
        SUPPRESS = 20.0
        key = jax.random.key(seed)
        ks = jax.random.split(key, 8)
        B, HW, C, T, CT = (8, 1024, 256, 77, 512)
        inner = HEADS * HEAD_DIM
        scale = 0.02
        return {'hidden_states': jax.random.normal(ks[0], (B, HW, C), jnp.float32), 'encoder_hidden_states': jax.random.normal(ks[1], (B, T, CT), jnp.float32), 'mask_A': (jax.random.uniform(ks[2], (HW,)) > 0.5).astype(jnp.float32), 'mask_B': (jax.random.uniform(ks[3], (HW,)) > 0.5).astype(jnp.float32), 'Wq': jax.random.normal(ks[4], (C, inner), jnp.float32) * scale, 'Wk': jax.random.normal(ks[5], (CT, inner), jnp.float32) * scale, 'Wv': jax.random.normal(ks[6], (CT, inner), jnp.float32) * scale, 'Wo': jax.random.normal(ks[7], (inner, C), jnp.float32) * scale, 'bo': jnp.zeros((C,), jnp.float32), 'token_indices_A': jnp.array([2, 3], dtype=jnp.int64), 'token_indices_B': jnp.array([5, 6], dtype=jnp.int64)}
    _L0_xattn_all = _L0_xattn_setup()
    _L0_xattn_in = {k: v for k, v in _L0_xattn_all.items() if k in ('Wq', 'Wk', 'Wv', 'Wo', 'bo', 'token_indices_A', 'token_indices_B')}
    del _L0_xattn_all

    def _L1_xattn_setup():
        import jax, jax.numpy as jnp
        import numpy as np
        D_MODEL = 256
        N_HEADS = 16
        N_KV_HEADS = 4
        HEAD_DIM = D_MODEL // N_HEADS
        SPEAKER_DIM = 512
        EPS = 1e-05

        def rmsnorm(x, w, eps=EPS):
            xf = x.astype(jnp.float32)
            inv = jax.lax.rsqrt(jnp.mean(xf * xf, axis=-1, keepdims=True) + eps)
            return (xf * inv).astype(x.dtype) * w
        key = jax.random.key(seed)
        ks = jax.random.split(key, 7)
        B, T, S = (4, 512, 128)
        x = jax.random.normal(ks[0], (B, T, D_MODEL), dtype=jnp.float32)
        cond = jax.random.normal(ks[1], (B, S, SPEAKER_DIM), dtype=jnp.float32)
        sq = 0.02
        wq = jax.random.normal(ks[2], (D_MODEL, N_HEADS * HEAD_DIM), dtype=jnp.float32) * sq
        wk = jax.random.normal(ks[3], (SPEAKER_DIM, N_KV_HEADS * HEAD_DIM), dtype=jnp.float32) * sq
        wv = jax.random.normal(ks[4], (SPEAKER_DIM, N_KV_HEADS * HEAD_DIM), dtype=jnp.float32) * sq
        wo = jax.random.normal(ks[5], (N_HEADS * HEAD_DIM, D_MODEL), dtype=jnp.float32) * sq
        norm_w = jnp.ones((D_MODEL,), dtype=jnp.float32)
        return {'x': x, 'cond': cond, 'wq': wq, 'wk': wk, 'wv': wv, 'wo': wo, 'norm_w': norm_w}
    _L1_xattn_all = _L1_xattn_setup()
    _L1_xattn_in = {k: v for k, v in _L1_xattn_all.items() if k in ('wq', 'wk', 'wv', 'wo', 'norm_w')}
    del _L1_xattn_all

    def _L2_xattn_setup():
        import jax, jax.numpy as jnp
        import numpy as np
        HEADS = 16
        HEAD_DIM = 64
        SUPPRESS = 20.0
        key = jax.random.key(seed)
        ks = jax.random.split(key, 8)
        B, HW, C, T, CT = (8, 1024, 256, 77, 512)
        inner = HEADS * HEAD_DIM
        scale = 0.02
        return {'hidden_states': jax.random.normal(ks[0], (B, HW, C), jnp.float32), 'encoder_hidden_states': jax.random.normal(ks[1], (B, T, CT), jnp.float32), 'mask_A': (jax.random.uniform(ks[2], (HW,)) > 0.5).astype(jnp.float32), 'mask_B': (jax.random.uniform(ks[3], (HW,)) > 0.5).astype(jnp.float32), 'Wq': jax.random.normal(ks[4], (C, inner), jnp.float32) * scale, 'Wk': jax.random.normal(ks[5], (CT, inner), jnp.float32) * scale, 'Wv': jax.random.normal(ks[6], (CT, inner), jnp.float32) * scale, 'Wo': jax.random.normal(ks[7], (inner, C), jnp.float32) * scale, 'bo': jnp.zeros((C,), jnp.float32), 'token_indices_A': jnp.array([2, 3], dtype=jnp.int64), 'token_indices_B': jnp.array([5, 6], dtype=jnp.int64)}
    _L2_xattn_all = _L2_xattn_setup()
    _L2_xattn_in = {k: v for k, v in _L2_xattn_all.items() if k in ('Wq', 'Wk', 'Wv', 'Wo', 'bo', 'token_indices_A', 'token_indices_B')}
    del _L2_xattn_all

    def _L3_xattn_setup():
        import jax, jax.numpy as jnp
        import numpy as np
        D_MODEL = 256
        N_HEADS = 16
        N_KV_HEADS = 4
        HEAD_DIM = D_MODEL // N_HEADS
        SPEAKER_DIM = 512
        EPS = 1e-05

        def rmsnorm(x, w, eps=EPS):
            xf = x.astype(jnp.float32)
            inv = jax.lax.rsqrt(jnp.mean(xf * xf, axis=-1, keepdims=True) + eps)
            return (xf * inv).astype(x.dtype) * w
        key = jax.random.key(seed)
        ks = jax.random.split(key, 7)
        B, T, S = (4, 512, 128)
        x = jax.random.normal(ks[0], (B, T, D_MODEL), dtype=jnp.float32)
        cond = jax.random.normal(ks[1], (B, S, SPEAKER_DIM), dtype=jnp.float32)
        sq = 0.02
        wq = jax.random.normal(ks[2], (D_MODEL, N_HEADS * HEAD_DIM), dtype=jnp.float32) * sq
        wk = jax.random.normal(ks[3], (SPEAKER_DIM, N_KV_HEADS * HEAD_DIM), dtype=jnp.float32) * sq
        wv = jax.random.normal(ks[4], (SPEAKER_DIM, N_KV_HEADS * HEAD_DIM), dtype=jnp.float32) * sq
        wo = jax.random.normal(ks[5], (N_HEADS * HEAD_DIM, D_MODEL), dtype=jnp.float32) * sq
        norm_w = jnp.ones((D_MODEL,), dtype=jnp.float32)
        return {'x': x, 'cond': cond, 'wq': wq, 'wk': wk, 'wv': wv, 'wo': wo, 'norm_w': norm_w}
    _L3_xattn_all = _L3_xattn_setup()
    _L3_xattn_in = {k: v for k, v in _L3_xattn_all.items() if k in ('wq', 'wk', 'wv', 'wo', 'norm_w')}
    del _L3_xattn_all
    return {'x': x, 'ctx_2048': ctx_2048, 'mask_S_fk1': mask_S_fk1, 'mask_S_fk0': mask_S_fk0, 'L0_xattn_Wq': _L0_xattn_in['Wq'], 'L0_xattn_Wk': _L0_xattn_in['Wk'], 'L0_xattn_Wv': _L0_xattn_in['Wv'], 'L0_xattn_Wo': _L0_xattn_in['Wo'], 'L0_xattn_bo': _L0_xattn_in['bo'], 'L0_xattn_token_indices_A': _L0_xattn_in['token_indices_A'], 'L0_xattn_token_indices_B': _L0_xattn_in['token_indices_B'], 'L1_xattn_wq': _L1_xattn_in['wq'], 'L1_xattn_wk': _L1_xattn_in['wk'], 'L1_xattn_wv': _L1_xattn_in['wv'], 'L1_xattn_wo': _L1_xattn_in['wo'], 'L1_xattn_norm_w': _L1_xattn_in['norm_w'], 'L2_xattn_Wq': _L2_xattn_in['Wq'], 'L2_xattn_Wk': _L2_xattn_in['Wk'], 'L2_xattn_Wv': _L2_xattn_in['Wv'], 'L2_xattn_Wo': _L2_xattn_in['Wo'], 'L2_xattn_bo': _L2_xattn_in['bo'], 'L2_xattn_token_indices_A': _L2_xattn_in['token_indices_A'], 'L2_xattn_token_indices_B': _L2_xattn_in['token_indices_B'], 'L3_xattn_wq': _L3_xattn_in['wq'], 'L3_xattn_wk': _L3_xattn_in['wk'], 'L3_xattn_wv': _L3_xattn_in['wv'], 'L3_xattn_wo': _L3_xattn_in['wo'], 'L3_xattn_norm_w': _L3_xattn_in['norm_w']}

def reference(x, ctx_2048, mask_S_fk1, mask_S_fk0, L0_xattn_Wq, L0_xattn_Wk, L0_xattn_Wv, L0_xattn_Wo, L0_xattn_bo, L0_xattn_token_indices_A, L0_xattn_token_indices_B, L1_xattn_wq, L1_xattn_wk, L1_xattn_wv, L1_xattn_wo, L1_xattn_norm_w, L2_xattn_Wq, L2_xattn_Wk, L2_xattn_Wv, L2_xattn_Wo, L2_xattn_bo, L2_xattn_token_indices_A, L2_xattn_token_indices_B, L3_xattn_wq, L3_xattn_wk, L3_xattn_wv, L3_xattn_wo, L3_xattn_norm_w):
    import jax
    import jax.numpy as jnp

    def _L0_xattn_ref(hidden_states, encoder_hidden_states, mask_A, mask_B, Wq, Wk, Wv, Wo, bo, token_indices_A, token_indices_B):
        import jax, jax.numpy as jnp
        import numpy as np
        HEADS = 16
        HEAD_DIM = 64
        SUPPRESS = 20.0
        B, HW, C = hidden_states.shape
        T = encoder_hidden_states.shape[1]
        residual = hidden_states
        q = hidden_states @ Wq
        k = encoder_hidden_states @ Wk
        v = encoder_hidden_states @ Wv
        q = q.reshape(B, HW, HEADS, HEAD_DIM).transpose(0, 2, 1, 3)
        k = k.reshape(B, T, HEADS, HEAD_DIM).transpose(0, 2, 1, 3)
        v = v.reshape(B, T, HEADS, HEAD_DIM).transpose(0, 2, 1, 3)
        scale = HEAD_DIM ** (-0.5)
        logits = jnp.einsum('bhqd,bhkd->bhqk', q, k) * scale
        suppress_A_in = 1.0 - mask_A
        suppress_B_in = 1.0 - mask_B
        col_bias = jnp.zeros((HW, T), logits.dtype)
        col_bias = col_bias.at[:, token_indices_A].set((-SUPPRESS * suppress_A_in)[:, None])
        col_bias = col_bias.at[:, token_indices_B].set((-SUPPRESS * suppress_B_in)[:, None])
        logits = logits + col_bias[None, None, :, :]
        probs = jax.nn.softmax(logits, axis=-1)
        out = jnp.einsum('bhqk,bhkd->bhqd', probs, v)
        out = out.transpose(0, 2, 1, 3).reshape(B, HW, HEADS * HEAD_DIM)
        out = out @ Wo + bo
        out = out + residual
        return out

    def _L1_xattn_ref(x, cond, wq, wk, wv, wo, norm_w):
        import jax, jax.numpy as jnp
        import numpy as np
        D_MODEL = 256
        N_HEADS = 16
        N_KV_HEADS = 4
        HEAD_DIM = D_MODEL // N_HEADS
        SPEAKER_DIM = 512
        EPS = 1e-05

        def rmsnorm(x, w, eps=EPS):
            xf = x.astype(jnp.float32)
            inv = jax.lax.rsqrt(jnp.mean(xf * xf, axis=-1, keepdims=True) + eps)
            return (xf * inv).astype(x.dtype) * w
        B, T, _ = x.shape
        S = cond.shape[1]
        n_rep = N_HEADS // N_KV_HEADS
        residual = x
        xn = rmsnorm(x, norm_w)
        q = (xn @ wq).reshape(B, T, N_HEADS, HEAD_DIM)
        k = (cond @ wk).reshape(B, S, N_KV_HEADS, HEAD_DIM)
        v = (cond @ wv).reshape(B, S, N_KV_HEADS, HEAD_DIM)
        qg = q.reshape(B, T, N_KV_HEADS, n_rep, HEAD_DIM)
        scale = 1.0 / np.sqrt(HEAD_DIM).astype(np.float32)
        scores = jnp.einsum('btgrd,bsgd->bgrts', qg, k) * scale
        attn = jax.nn.softmax(scores.astype(jnp.float32), axis=-1).astype(q.dtype)
        out = jnp.einsum('bgrts,bsgd->btgrd', attn, v).reshape(B, T, N_HEADS * HEAD_DIM)
        return residual + out @ wo

    def _L2_xattn_ref(hidden_states, encoder_hidden_states, mask_A, mask_B, Wq, Wk, Wv, Wo, bo, token_indices_A, token_indices_B):
        import jax, jax.numpy as jnp
        import numpy as np
        HEADS = 16
        HEAD_DIM = 64
        SUPPRESS = 20.0
        B, HW, C = hidden_states.shape
        T = encoder_hidden_states.shape[1]
        residual = hidden_states
        q = hidden_states @ Wq
        k = encoder_hidden_states @ Wk
        v = encoder_hidden_states @ Wv
        q = q.reshape(B, HW, HEADS, HEAD_DIM).transpose(0, 2, 1, 3)
        k = k.reshape(B, T, HEADS, HEAD_DIM).transpose(0, 2, 1, 3)
        v = v.reshape(B, T, HEADS, HEAD_DIM).transpose(0, 2, 1, 3)
        scale = HEAD_DIM ** (-0.5)
        logits = jnp.einsum('bhqd,bhkd->bhqk', q, k) * scale
        suppress_A_in = 1.0 - mask_A
        suppress_B_in = 1.0 - mask_B
        col_bias = jnp.zeros((HW, T), logits.dtype)
        col_bias = col_bias.at[:, token_indices_A].set((-SUPPRESS * suppress_A_in)[:, None])
        col_bias = col_bias.at[:, token_indices_B].set((-SUPPRESS * suppress_B_in)[:, None])
        logits = logits + col_bias[None, None, :, :]
        probs = jax.nn.softmax(logits, axis=-1)
        out = jnp.einsum('bhqk,bhkd->bhqd', probs, v)
        out = out.transpose(0, 2, 1, 3).reshape(B, HW, HEADS * HEAD_DIM)
        out = out @ Wo + bo
        out = out + residual
        return out

    def _L3_xattn_ref(x, cond, wq, wk, wv, wo, norm_w):
        import jax, jax.numpy as jnp
        import numpy as np
        D_MODEL = 256
        N_HEADS = 16
        N_KV_HEADS = 4
        HEAD_DIM = D_MODEL // N_HEADS
        SPEAKER_DIM = 512
        EPS = 1e-05

        def rmsnorm(x, w, eps=EPS):
            xf = x.astype(jnp.float32)
            inv = jax.lax.rsqrt(jnp.mean(xf * xf, axis=-1, keepdims=True) + eps)
            return (xf * inv).astype(x.dtype) * w
        B, T, _ = x.shape
        S = cond.shape[1]
        n_rep = N_HEADS // N_KV_HEADS
        residual = x
        xn = rmsnorm(x, norm_w)
        q = (xn @ wq).reshape(B, T, N_HEADS, HEAD_DIM)
        k = (cond @ wk).reshape(B, S, N_KV_HEADS, HEAD_DIM)
        v = (cond @ wv).reshape(B, S, N_KV_HEADS, HEAD_DIM)
        qg = q.reshape(B, T, N_KV_HEADS, n_rep, HEAD_DIM)
        scale = 1.0 / np.sqrt(HEAD_DIM).astype(np.float32)
        scores = jnp.einsum('btgrd,bsgd->bgrts', qg, k) * scale
        attn = jax.nn.softmax(scores.astype(jnp.float32), axis=-1).astype(q.dtype)
        out = jnp.einsum('bgrts,bsgd->btgrd', attn, v).reshape(B, T, N_HEADS * HEAD_DIM)
        return residual + out @ wo
    x = _L0_xattn_ref(x, ctx_2048, mask_S_fk1, mask_S_fk0, L0_xattn_Wq, L0_xattn_Wk, L0_xattn_Wv, L0_xattn_Wo, L0_xattn_bo, L0_xattn_token_indices_A, L0_xattn_token_indices_B)
    x = _L1_xattn_ref(x, ctx_2048, L1_xattn_wq, L1_xattn_wk, L1_xattn_wv, L1_xattn_wo, L1_xattn_norm_w)
    x = _L2_xattn_ref(x, ctx_2048, mask_S_fk1, mask_S_fk0, L2_xattn_Wq, L2_xattn_Wk, L2_xattn_Wv, L2_xattn_Wo, L2_xattn_bo, L2_xattn_token_indices_A, L2_xattn_token_indices_B)
    x = _L3_xattn_ref(x, ctx_2048, L3_xattn_wq, L3_xattn_wk, L3_xattn_wv, L3_xattn_wo, L3_xattn_norm_w)
    return x

_drawn_inputs = setup_inputs


def setup_inputs(seed=0):
    import zlib

    import numpy as np

    out = dict(_drawn_inputs(seed))
    spreads = {'L0_xattn_bo': (0.0, 0.1),
     'L1_xattn_norm_w': (1.0, 0.6),
     'L2_xattn_bo': (0.0, 0.1),
     'L3_xattn_norm_w': (1.0, 0.6)}
    factors = {'mask_S_fk1': 8.0,
     'mask_S_fk0': 8.0,
     'L0_xattn_Wq': 7.799,
     'L0_xattn_Wk': 7.78,
     'L1_xattn_wq': 8.0,
     'L1_xattn_wk': 8.0,
     'L2_xattn_Wq': 7.672,
     'L2_xattn_Wk': 7.642,
     'L3_xattn_wq': 8.0,
     'L3_xattn_wk': 8.0}
    for name, (base, spread) in spreads.items():
        noise = np.random.default_rng([zlib.crc32(name.encode()), seed]).standard_normal(out[name].shape)
        drawn = base * np.exp(spread * noise) if base else spread * noise
        out[name] = jnp.asarray(drawn.astype(out[name].dtype))
    for name, factor in factors.items():
        out[name] = (out[name] * factor).astype(out[name].dtype)
    return out
```

```python
from contextlib import ExitStack

import concourse.bass as bass
from concourse import mybir

F32 = mybir.dt.float32
F32R = mybir.dt.float32r
BF16 = mybir.dt.bfloat16
I32 = mybir.dt.int32
ALU = mybir.AluOpType
ACT = mybir.ActivationFunctionType
AX_X = mybir.AxisListType.X

P = 128
B, S, C = 4, 1024, 256
KEYS, CT = 154, 512
REST = KEYS - P
H = 16
DW, DN = 64, 16
KVN = 4
TOK = 512
KC, KCT = C // P, CT // P
ALLK = B * KEYS
WI = H * DW
EPS = 1e-5
SUPPRESS = 20.0
ROW_M = 32
WSTEPS, STEPS = 8, 16


def split3(lhs_hi, lhs_lo, rhs_hi, rhs_lo):
    return ((lhs_hi, rhs_hi), (lhs_hi, rhs_lo), (lhs_lo, rhs_hi))


def scratch_tensors(nc):
    def d(name, shape, dt):
        return nc.dram_tensor("scratch_" + name, shape, dt).ap()

    return dict(
        stream=d("stream", (B, 2, P, KC, TOK), F32),
        maskrows=d("maskrows", (2, 6, TOK), BF16),
        keyrows=d("keyrows", (2, 6, KEYS), BF16),
        wq_hi=d("wq_hi", (2, P, KC, WI), F32), wq_lo=d("wq_lo", (2, P, KC, WI), F32),
        wo_hi=d("wo_hi", (2, P, H // 2, C), F32), wo_lo=d("wo_lo", (2, P, H // 2, C), F32),
        nq_hi=d("nq_hi", (2, P, KC, C), F32), nq_lo=d("nq_lo", (2, P, KC, C), F32),
        no_hi=d("no_hi", (2, P, KC, C), F32), no_lo=d("no_lo", (2, P, KC, C), F32),
        wk_hi=d("wk_hi", (2, P, H // 2, ALLK), F32),
        wk_lob=d("wk_lob", (2, P, H // 2, ALLK), BF16), wk_hib=d("wk_hib", (2, P, H // 2, ALLK), BF16),
        nk_hi=d("nk_hi", (2, KVN * DN, ALLK), F32),
        nk_lob=d("nk_lob", (2, KVN * DN, ALLK), BF16), nk_hib=d("nk_hib", (2, KVN * DN, ALLK), BF16),
        wv=d("wv", (2, B, P, WI), F32), wv_rest=d("wv_rest", (2, B * REST, WI), F32),
        nv=d("nv", (2, B, P, KVN, 32), F32), nv_rest=d("nv_rest", (2, B * REST, KVN, 32), F32),
        sums=d("sums", (P, TOK), F32),
    )


def prepare(nc, ins, dr):
    ctx = ExitStack()
    with ctx:
        def sb(name, shape, dt=F32):
            return ctx.enter_context(nc.sbuf_tensor(name, shape, dt))

        def sem(name):
            return ctx.enter_context(nc.semaphore(name))

        ident = sb("p_ident", [P, P])
        tokens_in = sb("p_tokens_in", [P, 2, 4, C])
        tokens_t = sb("p_tokens_t", [P, 2, KC, TOK])
        ctx_in = sb("p_ctx_in", [P, 5, CT])
        ctx_hi = sb("p_ctx_hi", [P, KCT, ALLK], F32R)
        ctx_lo = sb("p_ctx_lo", [P, KCT, ALLK], F32R)
        raw = sb("p_raw", [P, 4096])
        hi = sb("p_hi", [P, 4096], F32R)
        lo = sb("p_lo", [P, 4096], F32R)
        normw = sb("p_normw", [P, KC])
        kout_hi = sb("p_kout_hi", [P, 2, ALLK], F32R)
        kout_hib = sb("p_kout_hib", [P, 2, ALLK], BF16)
        kout_lob = sb("p_kout_lob", [P, 2, ALLK], BF16)
        vout = sb("p_vout", [P, 2, 512])
        nvout = sb("p_nvout", [P, 2, KVN, 32])
        idx = sb("p_idx", [1, 8], I32)
        idxf = sb("p_idxf", [1, 3, 8])
        keyno = sb("p_keyno", [1, KEYS], I32)
        keynof = sb("p_keynof", [1, KEYS])
        onehot = sb("p_onehot", [1, 5, KEYS])
        keyrow = sb("p_keyrow", [1, 2, 6, KEYS], BF16)
        mrow = sb("p_mrow", [1, 2, S])
        mtmp = sb("p_mtmp", [1, 2, S])
        mpart = sb("p_mpart", [1, 2, 3, S], BF16)
        ps = ctx.enter_context(nc.psum_tensor("p_ps", [P, 8, 512], F32))

        s_ident = sem("p_ident_ready")
        s_x = [sem(f"p_tokens_loaded{i}") for i in range(2)]
        s_xt = sem("p_tokens_transposed")
        s_xc = sem("p_tokens_copied")
        s_xs = [sem(f"p_tokens_stored{i}") for i in range(2)]
        s_c = sem("p_context_loaded")
        s_ct = sem("p_context_transposed")
        s_cs = sem("p_context_split")
        s_w = [sem(f"p_weights_loaded{i}") for i in range(2)]
        s_nw = sem("p_norm_weights_loaded")
        s_hi = sem("p_weights_hi")
        s_lo = sem("p_weights_lo")
        s_wst = [sem(f"p_weights_stored{i}") for i in range(4)]
        s_mm = sem("p_product_made")
        s_ev = sem("p_product_taken")
        s_evh = sem("p_hi_taken")
        s_st = [sem(f"p_product_stored{i}") for i in range(2)]
        s_ones = sem("p_ones_ready")
        s_small = sem("p_small_loaded")
        s_rows = sem("p_rows_chain")
        s_rowst = sem("p_rows_stored")
        s_pool = sem("p_pool_chain")

        block = ctx.enter_context(nc.Block())
        NX = 2 * B

        def weight_pieces(p):
            wq, wk, wv, wo = ins[f"L{2 * p}_xattn_Wq"], ins[f"L{2 * p}_xattn_Wk"], ins[f"L{2 * p}_xattn_Wv"], ins[f"L{2 * p}_xattn_Wo"]
            nq, nk, nv, no = (ins[f"L{2 * p + 1}_xattn_{w}"] for w in ("wq", "wk", "wv", "wo"))
            r = lambda w: w.rearrange("(k p) n -> p k n", p=P)
            return [("wk0", r(wk)[:, :, 0:512], None), ("wk1", r(wk)[:, :, 512:1024], None),
                    ("nk", r(nk), None), ("nv", r(nv), None),
                    ("wv0", r(wv)[:, :, 0:512], None), ("wv1", r(wv)[:, :, 512:1024], None),
                    ("wq", r(wq), (dr["wq_hi"][p], dr["wq_lo"][p])),
                    ("wo", r(wo), (dr["wo_hi"][p], dr["wo_lo"][p])),
                    ("nq", r(nq), (dr["nq_hi"][p], dr["nq_lo"][p])),
                    ("no", r(no), (dr["no_hi"][p], dr["no_lo"][p]))]

        pieces = [(p, *x) for p in range(2) for x in weight_pieces(p)]
        size = lambda ap: ap.shape[1] * ap.shape[2]
        used = lambda i: pieces[i][3] is None

        def view(buf, i):
            k, n = pieces[i][2].shape[1:]
            return buf[:, (i % 2) * 2048:(i % 2) * 2048 + k * n].rearrange("p (k n) -> p k n", k=k)

        jobs = []
        for i, (p, name, src, st) in enumerate(pieces):
            if name in ("wk0", "wk1"):
                jobs += [(i, "k", 4 * int(name[2]) + m) for m in range(4)]
            elif name == "nk":
                jobs += [(i, "nk", 0)]
            elif name in ("wv0", "wv1"):
                jobs += [(i, "v", (int(name[2]), t)) for t in range(B + 1)]
            elif name == "nv":
                jobs += [(i, "nv", t) for t in range(B + 1)]
        last_job = {i: max(n for n, j in enumerate(jobs) if j[0] == i) for i in range(len(pieces)) if used(i)}

        def wait_piece_free(eng, i):
            j = i - 2
            if j < 0:
                return
            if used(j):
                eng.wait_ge(s_mm, last_job[j] + 1)
            else:
                stored = sum(not used(k) for k in range(j))
                eng.wait_ge(s_wst[stored % 4], 32 * (stored // 4 + 1))

        def store_job(sp, n):
            i, kind, what = jobs[n]
            p, stored = pieces[i][0], s_st[n % 2]
            sp.wait_ge(s_ev, n + 1)
            if kind in ("k", "nk"):
                m = P if kind == "k" else KVN * DN
                for name, buf in (("hi", kout_hi), ("hib", kout_hib), ("lob", kout_lob)):
                    to = dr["wk_" + name][p, :, what, :] if kind == "k" else dr["nk_" + name][p]
                    of = buf[0:m, n % 2, :]
                    sp.dma_start(to, of.bitcast(F32) if name == "hi" else of).then_inc(stored, 16)
            elif kind == "v":
                half, t = what
                cols = slice(half * 512, half * 512 + 512)
                to = dr["wv"][p, t, :, cols] if t < B else dr["wv_rest"][p, :, cols]
                sp.dma_start(to, vout[0:P if t < B else B * REST, n % 2, :]).then_inc(stored, 48)
            else:
                to = dr["nv"][p, what] if what < B else dr["nv_rest"][p]
                sp.dma_start(to, nvout[0:P if what < B else B * REST, n % 2]).then_inc(stored, 48)

        rows_ready = []

        @block.vector
        def _(dve):
            ins_done = [0]
            for k in range(KCT):
                dve.wait_ge(s_ct, k + 1)
                for half, (a, z) in enumerate(((0, 512), (512, ALLK))):
                    bank = (k % 2) * 2 + half
                    nc.vector.tensor_copy(ctx_hi[:, k, a:z], ps[:, bank, 0:z - a]).then_inc(s_cs, 1)
                dve.wait_ge(s_cs, 4 * k + 2)
                for half, (a, z) in enumerate(((0, 512), (512, ALLK))):
                    bank = (k % 2) * 2 + half
                    nc.vector.tensor_tensor(ctx_lo[:, k, a:z], ps[:, bank, 0:z - a], ctx_hi[:, k, a:z], ALU.subtract).then_inc(s_cs, 1)
            for x in range(NX):
                dve.wait_ge(s_xt, x + 1)
                if x >= 2:
                    dve.wait_ge(s_xs[x % 2], 16 * (x // 2))
                for k in range(KC):
                    nc.vector.tensor_copy(tokens_t[:, x % 2, k, :], ps[:, 4 + 2 * (x % 2) + k, :]).then_inc(s_xc, 1)

            chain = [0]

            def link(instruction):
                chain[0] += 1
                instruction.then_inc(s_rows, 1)
                dve.wait_ge(s_rows, chain[0])

            dve.wait_ge(s_small, 16 * 6)
            link(nc.vector.tensor_scalar(mtmp[:], mrow[:], -1.0, 1.0, ALU.mult, ALU.add))
            link(nc.vector.tensor_scalar(mrow[:], mtmp[:], -SUPPRESS * DW ** 0.5, None, ALU.mult))
            for part in range(3):
                link(nc.vector.tensor_copy(mpart[:, :, part], mrow[:]))
                if part < 2:
                    link(nc.vector.tensor_tensor(mrow[:], mrow[:], mpart[:, :, part], ALU.subtract))
            dve.wait_ge(s_ones, 1)
            link(nc.vector.tensor_copy(keynof[:], keyno[:]))
            link(nc.vector.tensor_copy(idxf[:, 0, :], idx[:]))
            link(nc.vector.tensor_scalar(idxf[:, 1, :], idxf[:, 0, :], 0.0, float(KEYS), ALU.is_lt, ALU.mult))
            link(nc.vector.tensor_tensor(idxf[:, 2, :], idxf[:, 0, :], idxf[:, 1, :], ALU.add))
            for p in range(2):
                for j in range(4):
                    link(nc.vector.tensor_scalar(onehot[:, j, :], keynof[:], idxf[:, 2, 4 * p + j:4 * p + j + 1], None, ALU.is_equal))
                link(nc.vector.tensor_tensor(onehot[:, 0, :], onehot[:, 0, :], onehot[:, 1, :], ALU.max))
                link(nc.vector.tensor_tensor(onehot[:, 2, :], onehot[:, 2, :], onehot[:, 3, :], ALU.max))
                link(nc.vector.tensor_scalar(onehot[:, 4, :], onehot[:, 2, :], -1.0, 1.0, ALU.mult, ALU.add))
                link(nc.vector.tensor_tensor(onehot[:, 1, :], onehot[:, 0, :], onehot[:, 4, :], ALU.mult))
                for r in range(6):
                    link(nc.vector.tensor_copy(keyrow[:, p, r, :], onehot[:, 1 if r < 3 else 2, :]))
            rows_ready.append(chain[0])
            for n, (i, kind, what) in enumerate(jobs):
                dve.wait_ge(s_mm, n + 1)
                if n >= 2:
                    dve.wait_ge(s_st[n % 2], 48 * (n // 2))
                bank = 2 * (n % 4)
                if kind in ("k", "nk"):
                    m = P if kind == "k" else KVN * DN
                    parts = [(ps[0:m, bank + half, 0:z - a], a, z) for half, (a, z) in enumerate(((0, 512), (512, ALLK)))]
                    for src, a, z in parts:
                        nc.vector.tensor_copy(kout_hi[0:m, n % 2, a:z], src)
                        last = nc.vector.tensor_copy(kout_hib[0:m, n % 2, a:z], src)
                    link(last)
                    for src, a, z in parts:
                        last = nc.vector.tensor_tensor(kout_lob[0:m, n % 2, a:z], src, kout_hi[0:m, n % 2, a:z], ALU.subtract)
                elif kind == "v":
                    m = P if what[1] < B else B * REST
                    last = nc.vector.tensor_copy(vout[0:m, n % 2, :], ps[0:m, bank, :])
                else:
                    dve.wait_ge(s_ones, 1)
                    m = P if what < B else B * REST
                    last = nc.vector.tensor_copy(nvout[0:m, n % 2, :, 0:DN], ps[0:m, bank, 0:KVN * DN].rearrange("p (g d) -> p g d", g=KVN))
                last.then_inc(s_ev, 1)

        @block.sync
        def _(sp):
            def load_piece(i):
                if i >= 2:
                    sp.wait_ge(s_lo, i - 1)
                p, name, src, st = pieces[i]
                sp.dma_start(view(raw, i), src).then_inc(s_w[i % 2], 16)
                if name == "nq":
                    if p:
                        sp.wait_ge(s_hi, len(pieces) // 2)
                    sp.dma_start(normw[:, :], ins[f"L{2 * p + 1}_xattn_norm_w"].rearrange("(k p) -> p k", p=P)).then_inc(s_nw, 16)

            with nc.allow_non_contiguous_dma(reason="columns of norm weights"):
                sp.dma_start(ctx_in[:, 0:B, :], ins["ctx_2048"][:, 0:P].rearrange("b p d -> p b d")).then_inc(s_c, 16)
                for b in range(B):
                    sp.dma_start(ctx_in[b * REST:(b + 1) * REST, B, :], ins["ctx_2048"][b, P:KEYS]).then_inc(s_c, 16)
                load_piece(0)
                load_piece(1)
                for a, name in enumerate(("mask_S_fk1", "mask_S_fk0")):
                    sp.dma_start(mrow[:, a, :], ins[name].rearrange("(a n) -> a n", a=1)).then_inc(s_small, 16)
                for p in range(2):
                    for a, name in enumerate("AB"):
                        at = 4 * p + 2 * a
                        sp.dma_start(idx[:, at:at + 2], ins[f"L{2 * p}_xattn_token_indices_{name}"].rearrange("(a n) -> a n", a=1)).then_inc(s_small, 16)
                for x in range(NX + 1):
                    if x < NX:
                        if x >= 2:
                            sp.wait_ge(s_xt, x - 1)
                        sp.dma_start(tokens_in[:, x % 2], ins["x"].rearrange("b (c t p) d -> (b c) p t d", t=4, p=P)[x]).then_inc(s_x[x % 2], 16)
                    if x >= 1:
                        y = x - 1
                        sp.wait_ge(s_xc, KC * (y + 1))
                        sp.dma_start(dr["stream"][y // 2, y % 2], tokens_t[:, y % 2]).then_inc(s_xs[y % 2], 16)
                for i in range(len(pieces)):
                    if i + 2 < len(pieces):
                        load_piece(i + 2)
                    for n, j in enumerate(jobs):
                        if j[0] == i:
                            store_job(sp, n)
                sp.wait_ge(s_rows, rows_ready[0])
                for t in range(2):
                    sp.dma_start(dr["maskrows"][t:t + 1].rearrange("o (a r) n -> o a r n", a=2),
                                 mpart[:, :, :, t * TOK:(t + 1) * TOK]).then_inc(s_rowst, 16)
                sp.dma_start(dr["keyrows"].rearrange("(o p) r n -> o p r n", o=1), keyrow[:]).then_inc(s_rowst, 16)
                sp.wait_ge(s_rowst, 48)
                for h in range(2):
                    sp.wait_ge(s_xs[h], 16 * (NX // 2))
                    sp.wait_ge(s_st[h], 48 * len(range(h, len(jobs), 2)))

        @block.scalar
        def _(act):
            for i, (p, name, src, st) in enumerate(pieces):
                act.wait_ge(s_w[i % 2], 16 * (i // 2 + 1))
                wait_piece_free(act, i)
                if name == "nq":
                    act.wait_ge(s_nw, 16 * (p + 1))
                    for k in range(KC):
                        nc.scalar.activation(view(raw, i)[:, k], view(raw, i)[:, k], ACT.Copy,
                                             scale=normw[:, k:k + 1]).then_inc(s_evh, 1)
                    act.wait_ge(s_evh, KC * (p + 1))
                nc.scalar.activation(view(hi, i), view(raw, i), ACT.Copy).then_inc(s_hi, 1)
                if st is not None:
                    act.wait_ge(s_lo, i + 1)
                    stored = s_wst[sum(not used(k) for k in range(i)) % 4]
                    act.dma_start(st[0], view(hi, i).bitcast(F32)).then_inc(stored, 16)
                    act.dma_start(st[1], view(lo, i).bitcast(F32)).then_inc(stored, 16)
            for k in range(4):
                act.wait_ge(s_wst[k], 32 * 2)

        @block.gpsimd
        def _(pool):
            nc.gpsimd.memset(ident[:], 0.0).then_inc(s_pool, 1)
            pool.wait_ge(s_pool, 1)
            nc.gpsimd.affine_select(out=ident[:], in_=ident[:], compare_op=ALU.not_equal, fill=1.0, base=0,
                                    pattern=[[-1, P]], channel_multiplier=1).then_inc(s_ident, 1)
            nc.gpsimd.memset(nvout[:], 0.0)
            nc.gpsimd.iota(keyno[:], pattern=[[1, KEYS]], base=0, channel_multiplier=0).then_inc(s_ones, 1)
            for i, (p, name, src, st) in enumerate(pieces):
                pool.wait_ge(s_hi, i + 1)
                wait_piece_free(pool, i)
                nc.gpsimd.tensor_tensor(view(lo, i), view(raw, i), view(hi, i), ALU.subtract).then_inc(s_lo, 1)

        @block.tensor
        def _(pe):
            pe.wait_ge(s_ident, 1)
            pe.wait_ge(s_c, 16 * (B + 1))
            for k in range(KCT):
                if k >= 1:
                    pe.wait_ge(s_cs, 4 * k)
                for t in range(5):
                    n = P if t < 4 else ALLK - 512
                    bank, col = (k % 2) * 2 + (t // 4), (t % 4) * P
                    last = nc.tensor.transpose(ps[:, bank, col:col + n], ctx_in[0:n, t, k * P:(k + 1) * P], ident[0:n, 0:n])
                last.then_inc(s_ct, 1)
            for x in range(NX):
                pe.wait_ge(s_x[x % 2], 16 * (x // 2 + 1))
                if x >= 2:
                    pe.wait_ge(s_xc, 2 * (x - 1))
                for k in range(KC):
                    for t in range(4):
                        last = nc.tensor.transpose(ps[:, 4 + 2 * (x % 2) + k, t * P:(t + 1) * P],
                                                   tokens_in[:, x % 2, t, k * P:(k + 1) * P], ident[:])
                last.then_inc(s_xt, 1)
            pe.wait_ge(s_cs, 4 * KCT)
            pe.wait_ge(s_xc, 2 * NX)
            for n, (i, kind, what) in enumerate(jobs):
                pe.wait_ge(s_lo, i + 1)
                if n >= 4:
                    pe.wait_ge(s_ev, n - 3)
                bank = 2 * (n % 4)
                wh, wl = view(hi, i), view(lo, i)
                if kind in ("k", "nk"):
                    cols = slice((what % 4) * P, (what % 4) * P + P) if kind == "k" else slice(0, KVN * DN)
                    m = P if kind == "k" else KVN * DN
                    for half, (a, z) in enumerate(((0, 512), (512, ALLK))):
                        pairs = [q for k in range(KCT) for q in split3(wh[:, k, cols], wl[:, k, cols], ctx_hi[:, k, a:z], ctx_lo[:, k, a:z])]
                        for j, (l, r) in enumerate(pairs):
                            last = nc.tensor.matmul(ps[0:m, bank + half, 0:z - a], l, r, start=(j == 0), stop=(j == len(pairs) - 1))
                else:
                    t = what[1] if kind == "v" else what
                    n_cols = 512 if kind == "v" else KVN * DN
                    m = P if t < B else B * REST

                    def tok(c, k):
                        return c[:, k, t * P:t * P + m]

                    pairs = [q for k in range(KCT) for q in split3(tok(ctx_hi, k), tok(ctx_lo, k), wh[:, k, :], wl[:, k, :])]
                    for j, (l, r) in enumerate(pairs):
                        last = nc.tensor.matmul(ps[0:m, bank, 0:n_cols], l, r, start=(j == 0), stop=(j == len(pairs) - 1))
                last.then_inc(s_mm, 1)


GB = 3
KEPT = 10
LAST = 3
OUT_BATCHES = (4, 4, 2, 2)


def wide(n):
    return n < WSTEPS


def half_of(n):
    return (n // 4) % 2


def slot(n):
    return n % 2 if wide(n) else ((n - WSTEPS) // 2) % 2


def first_tile(n):
    return 2 * n if wide(n) else 2 * WSTEPS + (n - WSTEPS)


def chunk_tile(c, k):
    return first_tile(4 * c) + k


def iteration_order():
    order = [("split", 0, 0)]

    def queries(n, part):
        if wide(n) or (part == 0 and n % 2 == 0):
            order.append(("query", n, part))
        if n == 3 and part == 1:
            order.append(("split", 1, 0))

    def norm(c, k):
        if c >= 0 and k < OUT_BATCHES[c]:
            order.append(("norm", c, k))

    def output(c, k):
        if c >= 0 and k < OUT_BATCHES[c]:
            order.append(("output", c, k))

    queries(0, 0)
    queries(0, 1)
    order.extend(("max", 0, i) for i in range(8))
    order.append(("turn", 0, 0))
    for n in range(STEPS):
        c, g, more = n // 4, n % 4, n + 1 < STEPS
        fresh = more and not wide(n + 1) and (n + 1) % 4 == 0
        order.append(("rest", n, 0))
        if more and not fresh:
            queries(n + 1, 0)
        order.extend(("score", n, j) for j in (0, 1))
        if g:
            output(c - 1, (None, 0, 1, 3)[g])
        if g == 2:
            norm(c - 1, 2)
        if more and not fresh:
            queries(n + 1, 1)
        if wide(n):
            order.append(("value", n, 0))
        if more and not fresh:
            order.extend(("max", n + 1, i) for i in range(4))
        order.extend(("score", n, j) for j in (2, 3))
        if g < 2:
            norm(c - 1, g)
        if fresh:
            order.append(("square", c + 1, 0))
        elif more:
            order.extend(("max", n + 1, i) for i in range(4, 8))
        if g == 2:
            output(c - 1, 2)
            norm(c - 1, 3)
        order.append(("value", n, 1))
        if g == 3:
            order.append(("invert", c, 0))
        if fresh:
            order.append(("rate", c + 1, 0))
            queries(n + 1, 0)
            order.extend(("max", n + 1, i) for i in range(8))
        if more:
            order.append(("turn", n + 1, 0))
    for k in range(2):
        norm(LAST, k)
        output(LAST, k)
    return order


ORDER = iteration_order()


class Signal:

    def __init__(self, sem, kinds, times=1):
        self.sem, self.times = sem, times
        self.number = {}
        for x in ORDER:
            if x[0] in kinds:
                self.number[x] = len(self.number) + 1
        self.per = len(self.number) * times

    def after(self, it, *key):
        return it * self.per + self.number[key] * self.times

    def before(self, it, number):
        return it * self.per + max(number, 0) * self.times


def general_uses():
    return [(*x, m) for x in ORDER if x[0] in ("query", "max", "turn", "output", "square", "rate")
            for m in range(KC if x[0] == "output" else 1)]


GENERAL = general_uses()
BANK = {use: i % GB for i, use in enumerate(GENERAL)}


def run_layers(nc, ins, dr):
    ctx = ExitStack()
    with ctx:
        def sb(name, shape, dt=F32):
            return ctx.enter_context(nc.sbuf_tensor(name, shape, dt))

        def sem(name):
            return ctx.enter_context(nc.semaphore(name))

        def signal(name, *kinds, times=1):
            return Signal(sem(name), kinds, times)

        x = sb("x", [P, 2, KC, TOK])
        wq = [sb(f"wq_{a}", [P, KC, WI], F32R) for a in ("hi", "lo")]
        wo = [sb(f"wo_{a}", [P, H // 2, C], F32R) for a in ("hi", "lo")]
        nq = [sb(f"nq_{a}", [P, KC, C], F32R) for a in ("hi", "lo")]
        no = [sb(f"no_{a}", [P, KVN, C], F32R) for a in ("hi", "lo")]
        bias = sb("bias", [P, KC])
        w_pair, n_pair = (sb(a + "_pair", [P, H, P], F32R) for a in "wn")
        w_aux, n_aux = (sb(a + "_aux", [P, H, P], BF16) for a in "wn")
        w_top, n_top = (sb(a + "_top", [P, H, KEYS], BF16) for a in "wn")
        w_pair_rest, w_aux_rest = sb("w_pair_rest", [P, H, P], F32R), sb("w_aux_rest", [P, H, P], BF16)
        n_pair_rest, n_aux_rest = sb("n_pair_rest", [P, KVN, P], F32R), sb("n_aux_rest", [P, KVN, P], BF16)
        w_val, w_val_rest = sb("w_val", [P, WI]), sb("w_val_rest", [P, WI])
        n_val, n_val_rest = sb("n_val", [P, KVN, 32]), sb("n_val_rest", [P, KVN, P])
        x_hi, x_lo = sb("x_hi", [P, KC, TOK], F32R), sb("x_lo", [P, KC, TOK], F32R)
        xn = sb("xn", [P, KC, TOK])
        q_pair = sb("q_pair", [P, 2, 4, TOK], F32R)
        q_aux = sb("q_aux", [P, 2, 2, 4, TOK], BF16)
        probs = sb("probs", [P, 4, TOK])
        probs_rest = sb("probs_rest", [P, 2, TOK])
        kept = sb("kept", [P, KEPT, TOK])
        inv = sb("inv", [P, TOK])
        inv_b = sb("inv_b", [P, 2, TOK])
        a_hi, a_lo = sb("a_hi", [P, 2, TOK], F32R), sb("a_lo", [P, 2, TOK], F32R)
        tops = sb("tops", [P, 4, 4])
        meansq, rate, power = sb("meansq", [P, 4]), sb("rate", [P, 4]), sb("power", [P, 4])
        ident, ones = sb("ident", [P, P]), sb("ones", [P, 1])
        ones_row = sb("ones_row", [1, 4, P], BF16)
        sel, sel_rest = sb("sel", [P, 4, 32]), sb("sel_rest", [P, 4, P])

        general = ctx.enter_context(nc.psum_tensor("general", [P, GB, 512], F32))
        score_ps = ctx.enter_context(nc.psum_tensor("score_ps", [P, 2, 512], F32))
        out_ps = ctx.enter_context(nc.psum_tensor("out_ps", [P, 2, 512], F32))
        sum_ps = ctx.enter_context(nc.psum_tensor("sum_ps", [P, 512], F32))

        CLEARED, STATIC = 17, 56
        WIDE, NARROW = 16 * 13, 16 * 18
        WKEYS, NKEYS = 16 * 27, 16 * 53

        cleared = sem("cleared")
        filled = sem("filled")
        ident_ready = sem("ident_ready")
        static_loaded = sem("static_loaded")
        wide_loaded, narrow_loaded = sem("wide_loaded"), sem("narrow_loaded")
        wkeys_loaded, nkeys_loaded = sem("wkeys_loaded"), sem("nkeys_loaded")
        x_loaded, x_stored = [sem(f"x_loaded{t}") for t in range(2)], [sem(f"x_stored{t}") for t in range(2)]
        sums_stored, inv_loaded = signal("sums_stored", "invert", times=16), signal("inv_loaded", "norm", times=64)
        pe_query, pe_max, pe_turn = signal("pe_query", "query"), signal("pe_max", "max"), signal("pe_turn", "turn")
        pe_score, pe_value = signal("pe_score", "rest", "score"), signal("pe_value", "value")
        pe_output, pe_square, pe_rate = signal("pe_output", "output"), signal("pe_square", "square"), signal("pe_rate", "rate")
        act_split, act_query, act_exp = signal("act_split", "split", "rate"), signal("act_query", "query"), signal("act_exp", "rest", "score")
        act_turn, act_keep, act_norm = signal("act_turn", "turn"), signal("act_keep", "value"), signal("act_norm", "norm")
        act_square = signal("act_square", "square")
        dve_query, dve_max, dve_invert = signal("dve_query", "query"), signal("dve_max", "max"), signal("dve_invert", "invert")
        dve_norm, dve_output = signal("dve_norm", "norm"), signal("dve_output", "output", times=KC)
        dve_square, dve_rate = signal("dve_square", "square"), signal("dve_rate", "rate")
        pool_split, pool_norm, pool_rate = signal("pool_split", "split", "rate"), signal("pool_norm", "norm"), signal("pool_rate", "square")
        reader = {"query": dve_query, "max": dve_max, "turn": act_turn, "output": dve_output,
                  "square": dve_square, "rate": dve_rate}

        block = ctx.enter_context(nc.Block())

        def each_iteration(eng, body):
            with eng.Fori(0, 2) as p:
                with eng.Fori(0, B) as b:
                    body(eng.snap(p * B + b), eng.snap(p))

        def bank_of(use):
            return general[:, BANK[use], :]

        @block.sync
        def _(sp):
            sp.wait_ge(cleared, CLEARED)
            count = [0]

            def static(dst, src):
                sp.dma_start(dst, src).then_inc(static_loaded, 16)
                count[0] += 1

            for t in range(2):
                for s in range(2):
                    for j in range(4):
                        a = 64 * (1 - j % 2)
                        static(q_aux[a:a + 6, t, s, j, :], dr["maskrows"][t])
            sp.wait_ge(filled, 1)
            for j in range(4):
                a = 64 * (1 - j % 2) + ROW_M + j
                heads = w_aux[a:a + 1].rearrange("p (g j) k -> p g j k", j=4)
                static(heads[:, :, j, :], ones_row[:])
                rests = w_aux_rest[a:a + 1].rearrange("p (g j) k -> p g j k", j=4)
                static(rests[:, :, j, 32 * j:32 * j + REST], ones_row[:, :, 0:REST])
                for u in range(KVN):
                    a = 64 * (1 - u % 2) + ROW_M + j
                    static(n_aux[a:a + 1, 4 * u + j, :], ones_row[:, 0, :])
                    static(n_aux_rest[a:a + 1, u, 32 * j:32 * j + REST], ones_row[:, 0, 0:REST])
            assert count[0] == STATIC

            def load_wide(p):
                for i, a in enumerate(("hi", "lo")):
                    sp.dma_start(wq[i][:].bitcast(F32), dr["wq_" + a][p]).then_inc(wide_loaded, 16)
                    sp.dma_start(wo[i][:].bitcast(F32), dr["wo_" + a][p]).then_inc(wide_loaded, 16)
                sp.dma_start(bias[:], ins[f"L{2 * p}_xattn_bo"].rearrange("(k p) -> p k", p=P),
                             allow_slow_non_contiguous=True).then_inc(wide_loaded, 16)
                for par in range(2):
                    a = 64 * (1 - par)
                    def every(buf):
                        return buf[a:a + 6].rearrange("p (h two) k -> p h two k", two=2)[:, :, par, :]
                    rows = dr["keyrows"][p]
                    sp.dma_start(every(w_aux), rows[:, None, 0:P].to_broadcast([6, 8, P])).then_inc(wide_loaded, 16)
                    sp.dma_start(every(w_top), rows[:, None, :].to_broadcast([6, 8, KEYS])).then_inc(wide_loaded, 16)
                for j in range(4):
                    a = 64 * (1 - j % 2)
                    rests = w_aux_rest[a:a + 6].rearrange("p (g j) k -> p g j k", j=4)
                    sp.dma_start(rests[:, :, j, 32 * j:32 * j + REST],
                                 dr["keyrows"][p][:, None, P:KEYS].to_broadcast([6, 4, REST])).then_inc(wide_loaded, 16)

            def load_narrow(p):
                for i, a in enumerate(("hi", "lo")):
                    sp.dma_start(nq[i][:].bitcast(F32), dr["nq_" + a][p]).then_inc(narrow_loaded, 16)
                    for j in range(4):
                        src = dr["no_" + a][p].rearrange("(v j i) k n -> v j i k n", j=4, i=DN)
                        for v in range(2):
                            dst = no[i][32 * j:32 * j + DN].rearrange("p (k v) n -> p k v n", v=2)
                            sp.dma_start(dst[:, :, v, :].bitcast(F32), src[v, j]).then_inc(narrow_loaded, 16)

            def cols(src, b):
                return src[..., bass.ds(b * P, P)], src[..., bass.ds(b * REST + B * P, REST)]

            def load_wide_keys(p, b):
                def go(dst, src):
                    sp.dma_start(dst, src).then_inc(wkeys_loaded, 16)

                for par in range(2):
                    rows = slice(64 * par, 64 * par + 64)
                    every = lambda buf: buf.rearrange("p (h two) k -> p h two k", two=2)[:, :, par, :]
                    main, rest = cols(dr["wk_hi"][p, rows], b)
                    for half in range(2):
                        to = slice(64 * half, 64 * half + 64)
                        go(every(w_pair[to]).bitcast(F32), main)
                        for jj in (par, par + 2):
                            heads = w_pair_rest[to].rearrange("p (g j) k -> p g j k", j=4)
                            go(heads[:, :, jj, 32 * jj:32 * jj + REST].bitcast(F32),
                               rest.rearrange("p (g two) k -> p g two k", two=2)[:, :, jj // 2, :])
                    main, rest = cols(dr["wk_lob"][p, rows], b)
                    go(every(w_aux[rows]), main)
                    for jj in (par, par + 2):
                        heads = w_aux_rest[rows].rearrange("p (g j) k -> p g j k", j=4)
                        go(heads[:, :, jj, 32 * jj:32 * jj + REST],
                           rest.rearrange("p (g two) k -> p g two k", two=2)[:, :, jj // 2, :])
                    main, rest = cols(dr["wk_hib"][p, rows], b)
                    go(every(w_top[rows])[:, :, 0:P], main)
                    go(every(w_top[rows])[:, :, P:KEYS], rest)
                go(w_val[:], dr["wv"][p, bass.ds(b, 1)].rearrange("o p n -> p (o n)"))
                for j in range(4):
                    dst = w_val_rest[32 * j:32 * j + REST].rearrange("p (g j d) -> p g j d", j=4, d=DW)
                    src = dr["wv_rest"][p, bass.ds(b * REST, REST)].rearrange("p (g j d) -> p g j d", j=4, d=DW)
                    go(dst[:, :, j, :], src[:, :, j, :])

            def load_narrow_keys(p, b):
                def go(dst, src):
                    sp.dma_start(dst, src).then_inc(nkeys_loaded, 16)

                def by_unit(src, w):
                    return src.rearrange("(u i) k -> i u k", i=DN)

                for j in range(4):
                    heads = lambda buf: buf.rearrange("p (u j) k -> p u j k", j=4)[:, :, j, :]
                    main, rest = cols(dr["nk_hi"][p], b)
                    for half in range(2):
                        to = slice(64 * half + DN * j, 64 * half + DN * j + DN)
                        go(heads(n_pair[to]).bitcast(F32), by_unit(main, P))
                        go(n_pair_rest[to, :, 32 * j:32 * j + REST].bitcast(F32), by_unit(rest, REST))
                    lo, lo_rest = cols(dr["nk_lob"][p], b)
                    hi, hi_rest = cols(dr["nk_hib"][p], b)
                    for par in range(2):
                        to = slice(64 * par + DN * j, 64 * par + DN * j + DN)
                        odd = lambda ap: ap.rearrange("p (v two) k -> p v two k", two=2)[:, :, par, :]
                        go(odd(heads(n_aux[to])), odd(by_unit(lo, P)))
                        go(odd(n_aux_rest[to, :, 32 * j:32 * j + REST]), odd(by_unit(lo_rest, REST)))
                        go(odd(heads(n_top[to]))[:, :, 0:P], odd(by_unit(hi, P)))
                        go(odd(heads(n_top[to]))[:, :, P:KEYS], odd(by_unit(hi_rest, REST)))
                    go(n_val_rest[32 * j:32 * j + REST, :, 32 * j:32 * j + 32], dr["nv_rest"][p, bass.ds(b * REST, REST)])
                go(n_val[:], dr["nv"][p, bass.ds(b, 1)].rearrange("o p g d -> p (o g) d"))

            def load_x(t, b):
                sp.dma_start(x[:, t], dr["stream"][bass.ds(b, 1), t].rearrange("o p k n -> p (o k) n")).then_inc(x_loaded[t], 16)

            def store_x(t, it, b):
                sp.wait_ge(dve_output.sem, dve_output.after(it, "output", 2 + t, 1))
                sp.dma_start(dr["stream"][bass.ds(b, 1), t].rearrange("o p k n -> p (o k) n"), x[:, t]).then_inc(x_stored[t], 16)
                sp.wait_ge(x_stored[t], 16 * it + 16)

            def body(p, b, last_of_pair):
                it = sp.snap(b + B * p) if not isinstance(b, int) else b + B * p
                last = last_of_pair and p == 1
                next_p, next_b = (p, b + 1) if not last_of_pair else (p + 1, 0)
                for what, c, k in ORDER:
                    if what == "invert":
                        sp.wait_ge(dve_invert.sem, dve_invert.after(it, what, c, 0))
                        sp.dma_start(dr["sums"], inv[:]).then_inc(sums_stored.sem, 16)
                        sp.wait_ge(sums_stored.sem, sums_stored.after(it, what, c, 0))
                        batch = 0
                    elif what == "norm" and k + 1 < OUT_BATCHES[c]:
                        sp.wait_ge(dve_norm.sem, dve_norm.after(it, what, c, k))
                        batch = k + 1
                    elif what == "output" and (c, k) == (1, 3) and last_of_pair and p == 0:
                        sp.wait_ge(pe_output.sem, pe_output.after(it, what, c, k))
                        load_wide(1)
                        continue
                    elif what == "turn" and c == WSTEPS and not last:
                        sp.wait_ge(pe_value.sem, pe_value.after(it, "value", WSTEPS - 1, 1))
                        load_wide_keys(next_p, next_b)
                        continue
                    elif what == "output" and (c, k) == (2, 1):
                        store_x(0, it, b)
                        if not last:
                            load_x(0, next_b)
                        continue
                    else:
                        continue
                    if what == "invert" or what == "norm":
                        for q in range(4):
                            if c < 2:
                                dst = inv_b[64 * (q % 2):64 * (q % 2) + 64, q // 2, :]
                                row = 32 * q + 8 * batch
                                src = dr["sums"][row:row + 1, :].to_broadcast([64, TOK])
                            else:
                                dst = inv_b[32 * q:32 * q + 32, :, :]
                                src = dr["sums"][32 * q + 16 * batch:32 * q + 16 * batch + 16, :].rearrange(
                                    "(u r) n -> r u n", r=8)[0:1].to_broadcast([32, 2, TOK])
                            sp.dma_start(dst, src).then_inc(inv_loaded.sem, 16)
                if not last:
                    sp.wait_ge(pe_value.sem, pe_value.after(it, "value", STEPS - 1, 1))
                    load_narrow_keys(next_p, next_b)
                store_x(1, it, b)
                if not last:
                    load_x(1, next_b)
                if last_of_pair and p == 0:
                    sp.wait_ge(pe_output.sem, pe_output.after(it, "output", LAST, 1))
                    load_narrow(1)

            load_x(0, 0)
            load_x(1, 0)
            load_wide(0)
            load_wide_keys(0, 0)
            load_narrow(0)
            load_narrow_keys(0, 0)
            for p in range(2):
                with sp.Fori(0, B - 1) as b:
                    body(p, sp.snap(b), False)
                body(p, B - 1, True)

        @block.scalar
        def _(act):
            act.wait_ge(cleared, CLEARED)

            def body(it, p):
                for what, n, k in ORDER:
                    if what == "split":
                        t = n
                        act.wait_ge(x_loaded[t], it * 16 + 16)
                        act.wait_ge(pe_query.sem, pe_query.before(it, 8 * t))
                        nc.scalar.activation(x_hi[:], x[:, t], ACT.Copy).then_inc(act_split.sem, 1)
                    elif what == "square":
                        act.wait_ge(dve_output.sem, dve_output.after(it, "output", n - 2, 3))
                        act.wait_ge(act_split.sem, act_split.before(it, n))
                        act.wait_ge(pool_split.sem, pool_split.before(it, n))
                        nc.scalar.activation(xn[:], x[:, n - 2], ACT.Square).then_inc(act_square.sem, 1)
                    elif what == "rate":
                        act.wait_ge(dve_rate.sem, dve_rate.after(it, what, n, k))
                        act.wait_ge(pe_query.sem, pe_query.before(it, 16 + 2 * (n - 2)))
                        nc.scalar.activation(x_hi[:], xn[:], ACT.Copy).then_inc(act_split.sem, 1)
                    elif what == "query":
                        act.wait_ge(pe_query.sem, pe_query.after(it, what, n, k))
                        ps = bank_of((what, n, k, 0))
                        t, s, j = half_of(n), slot(n), 2 * k
                        nc.scalar.activation(q_pair[0:64, s, j, :], ps[0:64], ACT.Copy)
                        nc.scalar.activation(q_pair[64:P, s, j + 1, :], ps[64:P], ACT.Copy)
                        nc.scalar.activation(q_aux[0:64, t, s, j, :], ps[0:64], ACT.Copy)
                        nc.scalar.activation(q_aux[64:P, t, s, j + 1, :], ps[64:P], ACT.Copy).then_inc(act_query.sem, 1)
                    elif what in ("rest", "score"):
                        act.wait_ge(pe_score.sem, pe_score.after(it, what, n, k))
                        number = pe_score.number[(what, n, k)]
                        if what == "rest":
                            act.wait_ge(pe_value.sem, pe_value.before(it, pe_value.number[("value", n - 2, 1)] if n >= 2 else 0))
                            dst = probs_rest[:, n % 2, :]
                        else:
                            half = k // 2 if wide(n - 1) or n == 0 else 1
                            act.wait_ge(pe_value.sem, pe_value.before(it, pe_value.number[("value", n - 1, half)] if n else 0))
                            dst = probs[:, k, :]
                        scale = (DW if wide(n) else DN) ** -0.5
                        nc.scalar.activation(dst, score_ps[:, number % 2, :], ACT.Exp, scale=scale).then_inc(act_exp.sem, 1)
                    elif what == "turn":
                        act.wait_ge(pe_turn.sem, pe_turn.after(it, what, n, k))
                        ps = bank_of((what, n, k, 0))
                        units = range(4) if wide(n) else (n % 2,)
                        for j in units:
                            a = 64 * (1 - j % 2) + ROW_M
                            last = nc.scalar.activation(q_aux[a:a + 4, half_of(n), slot(n), j, :], ps[0:4], ACT.Copy, scale=-1.0)
                        last.then_inc(act_turn.sem, 1)
                    elif what == "value":
                        act.wait_ge(pe_value.sem, pe_value.after(it, what, n, k))
                        tile = first_tile(n) + (k if wide(n) else 0)
                        act.wait_ge(pool_norm.sem, pool_norm.before(it, freed_by(tile)))
                        act.wait_ge(act_norm.sem, act_norm.before(it, freed_by(tile)))
                        nc.scalar.activation(kept[:, tile % KEPT, :], out_ps[:, tile % 2, :], ACT.Copy).then_inc(act_keep.sem, 1)
                    elif what == "norm":
                        act.wait_ge(dve_norm.sem, dve_norm.after(it, what, n, k))
                        act.wait_ge(pe_output.sem, pe_output.before(it, pe_output_before(n, k)))
                        for i in range(2):
                            tile = chunk_tile(n, 2 * k + i)
                            last = nc.scalar.activation(a_hi[:, i, :], kept[:, tile % KEPT, :], ACT.Copy)
                        last.then_inc(act_norm.sem, 1)

            def pe_output_before(c, k):
                return pe_output.number[("output", c, k)] - 1

            def freed_by(tile):
                if tile < KEPT:
                    return 0
                old = tile - KEPT
                c = next(c for c in reversed(range(4)) if chunk_tile(c, 0) <= old)
                return dve_norm.number[("norm", c, (old - chunk_tile(c, 0)) // 2)]

            each_iteration(act, body)

        @block.gpsimd
        def _(pool):
            for buf in (w_pair, n_pair, w_pair_rest, n_pair_rest):
                nc.gpsimd.memset(buf[:].bitcast(F32), 0.0).then_inc(cleared, 1)
            nc.gpsimd.memset(ident[:], 0.0).then_inc(ident_ready, 1)
            pool.wait_ge(ident_ready, 1)
            nc.gpsimd.affine_select(out=ident[:], in_=ident[:], compare_op=ALU.not_equal, fill=1.0, base=0,
                                    pattern=[[-1, P]], channel_multiplier=1).then_inc(ident_ready, 1)
            nc.gpsimd.memset(power[:], -0.5).then_inc(ident_ready, 1)
            pool.wait_ge(ident_ready, 3)
            pool.wait_ge(cleared, CLEARED)

            def body(it, p):
                for what, n, k in ORDER:
                    if what in ("split", "rate"):
                        pool.wait_ge(act_split.sem, act_split.after(it, what, n, k))
                        src = x[:, n] if what == "split" else xn[:]
                        nc.gpsimd.tensor_tensor(x_lo[:], src, x_hi[:], ALU.subtract).then_inc(pool_split.sem, 1)
                    elif what == "square":
                        pool.wait_ge(dve_square.sem, dve_square.after(it, what, n, k))
                        nc.gpsimd.tensor_tensor(rate[:], meansq[:], power[:], ALU.pow).then_inc(pool_rate.sem, 1)
                    elif what == "norm":
                        pool.wait_ge(act_norm.sem, act_norm.after(it, what, n, k))
                        for i in range(2):
                            tile = chunk_tile(n, 2 * k + i)
                            last = nc.gpsimd.tensor_tensor(a_lo[:, i, :], kept[:, tile % KEPT, :], a_hi[:, i, :], ALU.subtract)
                        last.then_inc(pool_norm.sem, 1)

            each_iteration(pool, body)

        @block.vector
        def _(dve):
            for buf in (w_aux, n_aux, w_top, n_top, w_aux_rest, n_aux_rest, w_val_rest, n_val_rest, q_aux, sel, sel_rest):
                nc.vector.memset(buf[:], 0.0).then_inc(cleared, 1)
            for i in range(2):
                nc.vector.memset(no[i][:].bitcast(F32), 0.0).then_inc(cleared, 1)
            dve.wait_ge(cleared, CLEARED)
            nc.vector.memset(ones[:], 1.0)
            nc.vector.memset(ones_row[:], 1.0)
            for g in range(4):
                nc.vector.memset(sel[:, g, 8 * g:8 * g + 8], 1.0)
                for j in range(4):
                    last = nc.vector.memset(sel_rest[32 * j:32 * j + REST, g, 32 * j + 8 * g:32 * j + 8 * g + 8], 1.0)
            last.then_inc(filled, 1)

            def body(it, p):
                dve.wait_ge(wide_loaded, p * WIDE + WIDE)
                for what, n, k in ORDER:
                    if what == "query":
                        dve.wait_ge(act_query.sem, act_query.after(it, what, n, k))
                        ps = bank_of((what, n, k, 0))
                        s, j = slot(n), 2 * k
                        nc.vector.tensor_tensor(q_pair[64:P, s, j, :], ps[0:64], q_pair[0:64, s, j, :], ALU.subtract)
                        last = nc.vector.tensor_tensor(q_pair[0:64, s, j + 1, :], ps[64:P], q_pair[64:P, s, j + 1, :], ALU.subtract)
                        last.then_inc(dve_query.sem, 1)
                    elif what == "max":
                        dve.wait_ge(pe_max.sem, pe_max.after(it, what, n, k))
                        if k == 0:
                            dve.wait_ge(pe_turn.sem, pe_turn.before(it, n))
                        sub, pair = k // 2, k % 2
                        src = bank_of((what, n, k, 0))[:, 0:2 * KEYS].rearrange("p (h k) -> p h k", h=2)
                        last = nc.vector.tensor_reduce(tops[:, sub, 2 * pair:2 * pair + 2], src, AX_X, ALU.max)
                        last.then_inc(dve_max.sem, 1)
                    elif what == "invert":
                        dve.wait_ge(pe_value.sem, pe_value.after(it, "value", 4 * n + 3, 1))
                        dve.wait_ge(sums_stored.sem, sums_stored.before(it, n))
                        nc.vector.reciprocal(inv[:], sum_ps[:]).then_inc(dve_invert.sem, 1)
                    elif what == "norm":
                        dve.wait_ge(inv_loaded.sem, inv_loaded.after(it, what, n, k))
                        tile = chunk_tile(n, 2 * k + 1)
                        dve.wait_ge(act_keep.sem, act_keep.before(it, tile + 1))
                        for i in range(2):
                            place = kept[:, chunk_tile(n, 2 * k + i) % KEPT, :]
                            last = nc.vector.tensor_tensor(place, place, inv_b[:, i, :], ALU.mult)
                        last.then_inc(dve_norm.sem, 1)
                    elif what == "output":
                        dve.wait_ge(pe_output.sem, pe_output.after(it, what, n, k))
                        t = n % 2
                        if k == 0 and n < 2:
                            dve.wait_ge(pool_split.sem, pool_split.after(it, "split", t, 0))
                            dve.wait_ge(x_loaded[t], it * 16 + 16)
                        else:
                            dve.wait_ge(dve_output.sem, dve_output.after(it, what, *((n, k - 1) if k else (n - 2, 3))))
                            if k == 0:
                                dve.wait_ge(dve_rate.sem, dve_rate.after(it, "rate", n, 0))
                        for m in range(KC):
                            dst, ps = x[:, t, m, :], bank_of((what, n, k, m))
                            if n < 2 and k == 0:
                                last = nc.vector.scalar_tensor_tensor(out=dst, in0=ps, scalar=bias[:, m:m + 1], in1=dst, op0=ALU.add, op1=ALU.add)
                            else:
                                last = nc.vector.tensor_tensor(dst, ps, dst, ALU.add)
                            last.then_inc(dve_output.sem, 1)
                    elif what == "square":
                        dve.wait_ge(pe_square.sem, pe_square.after(it, what, n, k))
                        last = nc.vector.tensor_scalar(meansq[:], bank_of((what, n, k, 0))[:, 0:4], 1.0 / C, EPS, ALU.mult, ALU.add)
                        last.then_inc(dve_square.sem, 1)
                    elif what == "rate":
                        dve.wait_ge(pe_rate.sem, pe_rate.after(it, what, n, k))
                        ps = bank_of((what, n, k, 0))
                        for m in range(KC):
                            last = nc.vector.tensor_tensor(xn[:, m, :], ps, x[:, n - 2, m, :], ALU.mult)
                        last.then_inc(dve_rate.sem, 1)


            each_iteration(dve, body)

        @block.tensor
        def _(pe):
            pe.wait_ge(ident_ready, 3)
            pe.wait_ge(filled, 1)
            pe.wait_ge(static_loaded, 16 * STATIC)

            def bank(it, use):
                i = GENERAL.index(use)
                if i < GB:
                    pe.wait_ge(dve_output.sem, dve_output.before(it, 0))
                else:
                    *key, m = GENERAL[i - GB]
                    read = reader[key[0]]
                    pe.wait_ge(read.sem, read.after(it, *key) - (read.times - 1 - m))
                return general[:, BANK[use], :]

            def body(it, p):
                pe.wait_ge(wide_loaded, p * WIDE + WIDE)
                pe.wait_ge(narrow_loaded, p * NARROW + NARROW)
                pe.wait_ge(wkeys_loaded, it * WKEYS + WKEYS)
                pe.wait_ge(nkeys_loaded, it * NKEYS + NKEYS)
                for what, n, k in ORDER:
                    if what == "query":
                        if n % 4 == 0 and k == 0:
                            key = ("split", n // 4, 0) if wide(n) else ("rate", n // 4, 0)
                            pe.wait_ge(pool_split.sem, pool_split.after(it, *key))
                        ps = bank(it, (what, n, k, 0))
                        w, at = (wq, 2 * (n % 4) + k) if wide(n) else (nq, (n % 4) // 2)
                        at = slice(at * P, at * P + P)
                        pairs = [q for c in range(KC) for q in split3(w[0][:, c, at], w[1][:, c, at], x_hi[:, c, :], x_lo[:, c, :])]
                        for i, (l, r) in enumerate(pairs):
                            last = nc.tensor.matmul(ps, l, r, start=(i == 0), stop=(i == len(pairs) - 1))
                        last.then_inc(pe_query.sem, 1)
                    elif what == "max":
                        if k == 0:
                            pe.wait_ge(act_query.sem, act_query.before(it, queries_for(n)))
                        ps = bank(it, (what, n, k, 0))
                        sub, pair = slice(k // 2 * P, k // 2 * P + P), k % 2
                        q = q_aux[:, half_of(n), slot(n)]
                        if wide(n):
                            for i in range(2):
                                last = nc.tensor.matmul(ps[:, i * KEYS:(i + 1) * KEYS], q[:, 2 * pair + i, sub],
                                                        w_top[:, 4 * (n % 4) + 2 * pair + i, :], start=True, stop=True)
                        else:
                            h = 4 * (n % 4) + 2 * pair
                            last = nc.tensor.matmul(ps[:, 0:2 * KEYS], q[:, n % 2, sub],
                                                    n_top[:, h:h + 2, :].rearrange("p h k -> p (h k)"), start=True, stop=True)
                        last.then_inc(pe_max.sem, 1)
                    elif what == "turn":
                        pe.wait_ge(dve_max.sem, dve_max.after(it, "max", n, 7))
                        ps = bank(it, (what, n, k, 0))
                        for sub in range(4):
                            last = nc.tensor.transpose(ps[0:4, sub * P:(sub + 1) * P], tops[:, sub, :], ident[:])
                        last.then_inc(pe_turn.sem, 1)
                    elif what in ("rest", "score"):
                        number = pe_score.number[(what, n, k)]
                        ps = score_ps[:, number % 2, :]
                        pe.wait_ge(act_exp.sem, act_exp.before(it, number - 2))
                        if what == "rest":
                            pe.wait_ge(dve_query.sem, dve_query.before(it, queries_for(n)))
                            pe.wait_ge(act_turn.sem, act_turn.after(it, "turn", n, 0))
                        s, t, g = slot(n), half_of(n), n % 4
                        pairs = []
                        for j in (range(4) if what == "rest" else (k,)):
                            h = 4 * g + j
                            unit = j if wide(n) else n % 2
                            if what == "score":
                                keys = (w_pair[:, h], w_aux[:, h]) if wide(n) else (n_pair[:, h], n_aux[:, h])
                            elif wide(n):
                                keys = (w_pair_rest[:, h], w_aux_rest[:, h])
                            elif j == 0:
                                keys = (n_pair_rest[:, g], n_aux_rest[:, g])
                            else:
                                continue
                            pairs += [(keys[0], q_pair[:, s, unit, :]), (keys[1], q_aux[:, t, s, unit, :])]
                        for i, (l, r) in enumerate(pairs):
                            last = nc.tensor.matmul(ps, l, r, start=(i == 0), stop=(i == len(pairs) - 1))
                        last.then_inc(pe_score.sem, 1)
                    elif what == "value":
                        pe.wait_ge(act_exp.sem, act_exp.after(it, "score", n, 2 * k + 1))
                        tile, g = first_tile(n) + (k if wide(n) else 0), n % 4
                        pe.wait_ge(act_keep.sem, act_keep.before(it, tile - 1))
                        if g == 0 and (k == 0 or not wide(n)):
                            pe.wait_ge(dve_invert.sem, dve_invert.before(it, n // 4))
                        out = out_ps[:, tile % 2, :]
                        rest = probs_rest[:, n % 2, :]
                        heads = (2 * k, 2 * k + 1) if wide(n) else range(4)
                        for i, j in enumerate(heads):
                            h = 4 * g + j
                            if wide(n):
                                nc.tensor.matmul(out[64 * i:64 * i + 64], w_val[:, h * DW:(h + 1) * DW], probs[:, j, :],
                                                 start=True, stop=False, skip_group_check=True)
                            else:
                                nc.tensor.matmul(out[32 * j:32 * j + 32], n_val[:, g, :], probs[:, j, :],
                                                 start=True, stop=False, skip_group_check=True)
                        if wide(n):
                            for i, j in enumerate(heads):
                                h = 4 * g + j
                                nc.tensor.matmul(out[64 * i:64 * i + 64], w_val_rest[:, h * DW:(h + 1) * DW], rest,
                                                 start=False, stop=True, skip_group_check=True)
                        else:
                            nc.tensor.matmul(out, n_val_rest[:, g, :], rest, start=False, stop=True, skip_group_check=True)
                        for j in heads:
                            last = nc.tensor.matmul(sum_ps[32 * j:32 * j + 32, :], sel[:, g, :], probs[:, j, :],
                                                    start=(g == 0), stop=False, skip_group_check=True)
                        if k == 1:
                            last = nc.tensor.matmul(sum_ps[:], sel_rest[:, g, :], rest, start=False, stop=(g == 3), skip_group_check=True)
                        last.then_inc(pe_value.sem, 1)
                    elif what == "output":
                        pe.wait_ge(pool_norm.sem, pool_norm.after(it, "norm", n, k))
                        w = wo if n < 2 else no
                        for m in range(KC):
                            ps = bank(it, (what, n, k, m))
                            rows = slice(m * P, m * P + P)
                            pairs = [q for i in range(2) for q in split3(w[0][:, 2 * k + i, rows], w[1][:, 2 * k + i, rows], a_hi[:, i, :], a_lo[:, i, :])]
                            for i, (l, r) in enumerate(pairs):
                                last = nc.tensor.matmul(ps, l, r, start=(i == 0), stop=(i == len(pairs) - 1))
                        last.then_inc(pe_output.sem, 1)
                    elif what == "square":
                        pe.wait_ge(act_square.sem, act_square.after(it, what, n, k))
                        ps = bank(it, (what, n, k, 0))
                        for sub in range(4):
                            for c in range(KC):
                                last = nc.tensor.matmul(ps[:, sub:sub + 1], xn[:, c, sub * P:(sub + 1) * P], ones[:],
                                                        start=(c == 0), stop=(c == KC - 1))
                        last.then_inc(pe_square.sem, 1)
                    elif what == "rate":
                        pe.wait_ge(pool_rate.sem, pool_rate.after(it, "square", n, k))
                        ps = bank(it, (what, n, k, 0))
                        for sub in range(4):
                            last = nc.tensor.transpose(ps[:, sub * P:(sub + 1) * P], rate[:, sub:sub + 1].to_broadcast([P, P]), ident[:])
                        last.then_inc(pe_rate.sem, 1)

            def queries_for(n):
                return 2 * (n + 1) if wide(n) else 2 * WSTEPS + (n - WSTEPS) // 2 + 1

            each_iteration(pe, body)


def store_outputs(nc, dr, out):
    ctx = ExitStack()
    with ctx:
        def sem(name):
            return ctx.enter_context(nc.semaphore(name))

        ident = ctx.enter_context(nc.sbuf_tensor("o_ident", [P, P], F32))
        xt = ctx.enter_context(nc.sbuf_tensor("o_xt", [P, 2 * B, KC, TOK], F32))
        tokens = ctx.enter_context(nc.sbuf_tensor("o_tokens", [P, 2 * B, 4, C], F32))
        ps = ctx.enter_context(nc.psum_tensor("o_ps", [P, 8, 512], F32))
        ident_ready, made = sem("o_ident_ready"), sem("o_transposed")
        loaded = [sem(f"o_loaded{i}") for i in range(2 * B)]
        taken = [sem("o_taken_dve"), sem("o_taken_act")]
        stored = sem("o_stored")
        block = ctx.enter_context(nc.Block())

        @block.sync
        def _(sp):
            for i in range(2 * B):
                sp.dma_start(xt[:, i], dr["stream"][i // 2, i % 2]).then_inc(loaded[i], 16)
            for i in range(2 * B):
                for e in range(2):
                    sp.wait_ge(taken[e], i + 1)
                sp.dma_start(out.rearrange("b (c t p) d -> (b c) p t d", t=4, p=P)[i], tokens[:, i]).then_inc(stored, 16)
            sp.wait_ge(stored, 16 * 2 * B)

        @block.gpsimd
        def _(pool):
            nc.gpsimd.memset(ident[:], 0.0).then_inc(ident_ready, 1)
            pool.wait_ge(ident_ready, 1)
            nc.gpsimd.affine_select(out=ident[:], in_=ident[:], compare_op=ALU.not_equal, fill=1.0, base=0,
                                    pattern=[[-1, P]], channel_multiplier=1).then_inc(ident_ready, 1)

        @block.tensor
        def _(pe):
            pe.wait_ge(ident_ready, 2)
            for i in range(2 * B):
                pe.wait_ge(loaded[i], 16)
                if i >= 4:
                    for e in range(2):
                        pe.wait_ge(taken[e], i - 3)
                for t in range(4):
                    for k in range(KC):
                        col = (t % 2) * C + k * P
                        last = nc.tensor.transpose(ps[:, 2 * (i % 4) + t // 2, col:col + P], xt[:, i, k, t * P:(t + 1) * P], ident[:])
                last.then_inc(made, 1)

        def take(eng, copy, e):
            for i in range(2 * B):
                eng.wait_ge(made, i + 1)
                copy(tokens[:, i, 2 * e:2 * e + 2, :].rearrange("p t d -> p (t d)"), ps[:, 2 * (i % 4) + e, :]).then_inc(taken[e], 1)

        @block.vector
        def _(dve):
            take(dve, nc.vector.tensor_copy, 0)

        @block.scalar
        def _(act):
            take(act, lambda dst, src: nc.scalar.activation(dst, src, ACT.Copy), 1)


_INS = ["x", "ctx_2048", "mask_S_fk1", "mask_S_fk0"]
for _p in range(2):
    _INS += [f"L{2 * _p}_xattn_{_w}" for _w in ("Wq", "Wk", "Wv", "Wo", "bo", "token_indices_A", "token_indices_B")]
    _INS += [f"L{2 * _p + 1}_xattn_{_w}" for _w in ("wq", "wk", "wv", "wo", "norm_w")]


def build(nc, ins, out):
    dr = scratch_tensors(nc)
    prepare(nc, ins, dr)
    run_layers(nc, ins, dr)
    store_outputs(nc, dr, out)


def kernel(**inputs):
    import numpy as _np
    import concourse.bacc as _bacc
    from concourse import mybir as _mybir
    from concourse.bass_utils import run_bass_kernel_spmd as _run

    nc = _bacc.Bacc("TRN2", target_bir_lowering=False, num_devices=1)
    arrays, ins = {}, {}
    for name in _INS:
        a = _np.ascontiguousarray(inputs[name])
        arrays[f"in_{name}_dram"] = a
        ins[name] = nc.dram_tensor(f"in_{name}_dram", a.shape, _mybir.dt.from_np(a.dtype), kind="ExternalInput").ap()
    out = nc.dram_tensor("out_0_dram", (B, S, C), _mybir.dt.float32, kind="ExternalOutput").ap()
    build(nc, ins, out)
    r = _run(nc, [arrays], core_ids=[0])
    return r.results[0]["out_0_dram"]
```

```python
from contextlib import ExitStack

import concourse.bass as bass
from concourse import mybir

F32 = mybir.dt.float32
F32R = mybir.dt.float32r
BF16 = mybir.dt.bfloat16
I32 = mybir.dt.int32
ALU = mybir.AluOpType
ACT = mybir.ActivationFunctionType
AX_X = mybir.AxisListType.X

P = 128
B, S, C = 4, 1024, 256
KEYS, CT = 154, 512
REST = KEYS - P
H = 16
DW, DN = 64, 16
KVN = 4
TOK = 512
KC, KCT = C // P, CT // P
ALLK = B * KEYS
WI = H * DW
EPS = 1e-5
SUPPRESS = 20.0
ROW_M = 32
WSTEPS, STEPS = 8, 16


def split3(lhs_hi, lhs_lo, rhs_hi, rhs_lo):
    return ((lhs_hi, rhs_hi), (lhs_hi, rhs_lo), (lhs_lo, rhs_hi))


def scratch_tensors(nc):
    def d(name, shape, dt):
        return nc.dram_tensor("scratch_" + name, shape, dt).ap()

    return dict(
        stream=d("stream", (B, 2, P, KC, TOK), F32),
        maskrows=d("maskrows", (2, 6, TOK), BF16),
        keyrows=d("keyrows", (2, 6, KEYS), BF16),
        wq_hi=d("wq_hi", (2, P, KC, WI), F32), wq_lo=d("wq_lo", (2, P, KC, WI), F32),
        wo_hi=d("wo_hi", (2, P, H // 2, C), F32), wo_lo=d("wo_lo", (2, P, H // 2, C), F32),
        nq_hi=d("nq_hi", (2, P, KC, C), F32), nq_lo=d("nq_lo", (2, P, KC, C), F32),
        no_hi=d("no_hi", (2, P, KC, C), F32), no_lo=d("no_lo", (2, P, KC, C), F32),
        wk_hi=d("wk_hi", (2, P, H // 2, ALLK), F32),
        wk_lob=d("wk_lob", (2, P, H // 2, ALLK), BF16), wk_hib=d("wk_hib", (2, P, H // 2, ALLK), BF16),
        nk_hi=d("nk_hi", (2, KVN * DN, ALLK), F32),
        nk_lob=d("nk_lob", (2, KVN * DN, ALLK), BF16), nk_hib=d("nk_hib", (2, KVN * DN, ALLK), BF16),
        wv=d("wv", (2, B, P, WI), F32), wv_rest=d("wv_rest", (2, B * REST, WI), F32),
        nv=d("nv", (2, B, P, KVN, 32), F32), nv_rest=d("nv_rest", (2, B * REST, KVN, 32), F32),
        sums=d("sums", (P, TOK), F32),
    )


def prepare(nc, ins, dr):
    ctx = ExitStack()
    with ctx:
        def sb(name, shape, dt=F32):
            return ctx.enter_context(nc.sbuf_tensor(name, shape, dt))

        def sem(name):
            return ctx.enter_context(nc.semaphore(name))

        ident = sb("p_ident", [P, P])
        tokens_in = sb("p_tokens_in", [P, 2, 4, C])
        tokens_t = sb("p_tokens_t", [P, 2, KC, TOK])
        ctx_in = sb("p_ctx_in", [P, 5, CT])
        ctx_hi = sb("p_ctx_hi", [P, KCT, ALLK], F32R)
        ctx_lo = sb("p_ctx_lo", [P, KCT, ALLK], F32R)
        SETS, OUTS = 3, 4
        raw = sb("p_raw", [P, SETS * 2048])
        hi = sb("p_hi", [P, SETS * 2048], F32R)
        lo = sb("p_lo", [P, SETS * 2048], F32R)
        normw = sb("p_normw", [P, KC])
        kout_hi = sb("p_kout_hi", [P, OUTS, ALLK], F32R)
        kout_hib = sb("p_kout_hib", [P, OUTS, ALLK], BF16)
        kout_lob = sb("p_kout_lob", [P, OUTS, ALLK], BF16)
        vout = sb("p_vout", [P, OUTS, 512])
        nvout = sb("p_nvout", [P, OUTS, KVN, 32])
        idx = sb("p_idx", [1, 8], I32)
        idxf = sb("p_idxf", [1, 3, 8])
        keyno = sb("p_keyno", [1, KEYS], I32)
        keynof = sb("p_keynof", [1, KEYS])
        onehot = sb("p_onehot", [1, 5, KEYS])
        keyrow = sb("p_keyrow", [1, 2, 6, KEYS], BF16)
        mrow = sb("p_mrow", [1, 2, S])
        mtmp = sb("p_mtmp", [1, 2, S])
        mpart = sb("p_mpart", [1, 2, 3, S], BF16)
        ps = ctx.enter_context(nc.psum_tensor("p_ps", [P, 8, 512], F32))

        s_ident = sem("p_ident_ready")
        s_x = [sem(f"p_tokens_loaded{i}") for i in range(2)]
        s_xt = sem("p_tokens_transposed")
        s_xc = sem("p_tokens_copied")
        s_xs = [sem(f"p_tokens_stored{i}") for i in range(2)]
        s_c = sem("p_context_loaded")
        s_ct = sem("p_context_transposed")
        s_cs = sem("p_context_split")
        s_w = [sem(f"p_weights_loaded{i}") for i in range(SETS)]
        s_nw = sem("p_norm_weights_loaded")
        s_hi = sem("p_weights_hi")
        s_lo = sem("p_weights_lo")
        s_wst = [sem(f"p_weights_stored{i}") for i in range(4)]
        s_mm = sem("p_product_made")
        s_ev = sem("p_product_taken")
        s_evh = sem("p_hi_taken")
        s_st = [sem(f"p_product_stored{i}") for i in range(OUTS)]
        s_ones = sem("p_ones_ready")
        s_small = sem("p_small_loaded")
        s_rows = sem("p_rows_chain")
        s_rowst = sem("p_rows_stored")
        s_pool = sem("p_pool_chain")

        block = ctx.enter_context(nc.Block())
        NX = 2 * B

        def weight_pieces(p):
            wq, wk, wv, wo = ins[f"L{2 * p}_xattn_Wq"], ins[f"L{2 * p}_xattn_Wk"], ins[f"L{2 * p}_xattn_Wv"], ins[f"L{2 * p}_xattn_Wo"]
            nq, nk, nv, no = (ins[f"L{2 * p + 1}_xattn_{w}"] for w in ("wq", "wk", "wv", "wo"))
            r = lambda w: w.rearrange("(k p) n -> p k n", p=P)
            return [("wk0", r(wk)[:, :, 0:512], None),
                    ("wq", r(wq), (dr["wq_hi"][p], dr["wq_lo"][p])),
                    ("wk1", r(wk)[:, :, 512:1024], None), ("nk", r(nk), None),
                    ("wo", r(wo), (dr["wo_hi"][p], dr["wo_lo"][p])),
                    ("wv0", r(wv)[:, :, 0:512], None), ("nv", r(nv), None),
                    ("nq", r(nq), (dr["nq_hi"][p], dr["nq_lo"][p])),
                    ("wv1", r(wv)[:, :, 512:1024], None),
                    ("no", r(no), (dr["no_hi"][p], dr["no_lo"][p]))]

        pieces = [(p, *x) for p in range(2) for x in weight_pieces(p)]
        used = lambda i: pieces[i][3] is None

        def view(buf, i):
            k, n = pieces[i][2].shape[1:]
            return buf[:, (i % SETS) * 2048:(i % SETS) * 2048 + k * n].rearrange("p (k n) -> p k n", k=k)

        jobs = []
        for i, (p, name, src, st) in enumerate(pieces):
            if name in ("wk0", "wk1"):
                jobs += [(i, "k", 4 * int(name[2]) + m) for m in range(4)]
            elif name == "nk":
                jobs += [(i, "nk", 0)]
            elif name in ("wv0", "wv1"):
                jobs += [(i, "v", (int(name[2]), t)) for t in range(B + 1)]
            elif name == "nv":
                jobs += [(i, "nv", t) for t in range(B + 1)]
        last_job = {i: max(n for n, j in enumerate(jobs) if j[0] == i) for i in range(len(pieces)) if used(i)}

        def wait_piece_free(eng, i):
            j = i - SETS
            if j < 0:
                return
            if used(j):
                eng.wait_ge(s_mm, last_job[j] + 1)
            else:
                stored = sum(not used(k) for k in range(j))
                eng.wait_ge(s_wst[stored % 4], 32 * (stored // 4 + 1))

        def store_job(sp, n):
            i, kind, what = jobs[n]
            p, stored = pieces[i][0], s_st[n % OUTS]
            sp.wait_ge(s_ev, n + 1)
            if kind in ("k", "nk"):
                m = P if kind == "k" else KVN * DN
                for name, buf in (("hi", kout_hi), ("hib", kout_hib), ("lob", kout_lob)):
                    to = dr["wk_" + name][p, :, what, :] if kind == "k" else dr["nk_" + name][p]
                    of = buf[0:m, n % OUTS, :]
                    sp.dma_start(to, of.bitcast(F32) if name == "hi" else of).then_inc(stored, 16)
            elif kind == "v":
                half, t = what
                cols = slice(half * 512, half * 512 + 512)
                to = dr["wv"][p, t, :, cols] if t < B else dr["wv_rest"][p, :, cols]
                sp.dma_start(to, vout[0:P if t < B else B * REST, n % OUTS, :]).then_inc(stored, 48)
            else:
                to = dr["nv"][p, what] if what < B else dr["nv_rest"][p]
                sp.dma_start(to, nvout[0:P if what < B else B * REST, n % OUTS]).then_inc(stored, 48)

        rows_ready = []

        @block.vector
        def _(dve):
            for k in range(KCT):
                dve.wait_ge(s_ct, k + 1)
                for half, (a, z) in enumerate(((0, 512), (512, ALLK))):
                    bank = (k % 2) * 2 + half
                    nc.vector.tensor_copy(ctx_hi[:, k, a:z], ps[:, bank, 0:z - a]).then_inc(s_cs, 1)
                dve.wait_ge(s_cs, 4 * k + 2)
                for half, (a, z) in enumerate(((0, 512), (512, ALLK))):
                    bank = (k % 2) * 2 + half
                    nc.vector.tensor_tensor(ctx_lo[:, k, a:z], ps[:, bank, 0:z - a], ctx_hi[:, k, a:z], ALU.subtract).then_inc(s_cs, 1)
            def take_stream(x):
                dve.wait_ge(s_xt, x + 1)
                if x >= 2:
                    dve.wait_ge(s_xs[x % 2], 16 * (x // 2))
                for k in range(KC):
                    nc.vector.tensor_copy(tokens_t[:, x % 2, k, :], ps[:, 6 + k, :]).then_inc(s_xc, 1)

            chain = [0]

            def link(instruction):
                chain[0] += 1
                instruction.then_inc(s_rows, 1)
                dve.wait_ge(s_rows, chain[0])

            def make_rows():
                dve.wait_ge(s_small, 16 * 6)
                link(nc.vector.tensor_scalar(mtmp[:], mrow[:], -1.0, 1.0, ALU.mult, ALU.add))
                link(nc.vector.tensor_scalar(mrow[:], mtmp[:], -SUPPRESS * DW ** 0.5, None, ALU.mult))
                for part in range(3):
                    link(nc.vector.tensor_copy(mpart[:, :, part], mrow[:]))
                    if part < 2:
                        link(nc.vector.tensor_tensor(mrow[:], mrow[:], mpart[:, :, part], ALU.subtract))
                dve.wait_ge(s_ones, 1)
                link(nc.vector.tensor_copy(keynof[:], keyno[:]))
                link(nc.vector.tensor_copy(idxf[:, 0, :], idx[:]))
                link(nc.vector.tensor_scalar(idxf[:, 1, :], idxf[:, 0, :], 0.0, float(KEYS), ALU.is_lt, ALU.mult))
                link(nc.vector.tensor_tensor(idxf[:, 2, :], idxf[:, 0, :], idxf[:, 1, :], ALU.add))
                for p in range(2):
                    for j in range(4):
                        link(nc.vector.tensor_scalar(onehot[:, j, :], keynof[:], idxf[:, 2, 4 * p + j:4 * p + j + 1], None, ALU.is_equal))
                    link(nc.vector.tensor_tensor(onehot[:, 0, :], onehot[:, 0, :], onehot[:, 1, :], ALU.max))
                    link(nc.vector.tensor_tensor(onehot[:, 2, :], onehot[:, 2, :], onehot[:, 3, :], ALU.max))
                    link(nc.vector.tensor_scalar(onehot[:, 4, :], onehot[:, 2, :], -1.0, 1.0, ALU.mult, ALU.add))
                    link(nc.vector.tensor_tensor(onehot[:, 1, :], onehot[:, 0, :], onehot[:, 4, :], ALU.mult))
                    for r in range(6):
                        link(nc.vector.tensor_copy(keyrow[:, p, r, :], onehot[:, 1 if r < 3 else 2, :]))
                rows_ready.append(chain[0])

            def take_product(n, i, kind, what):
                dve.wait_ge(s_mm, n + 1)
                if n >= OUTS:
                    dve.wait_ge(s_st[n % OUTS], 48 * (n // OUTS))
                bank = 2 * (n % 3)
                if kind in ("k", "nk"):
                    m = P if kind == "k" else KVN * DN
                    parts = [(ps[0:m, bank + half, 0:z - a], a, z) for half, (a, z) in enumerate(((0, 512), (512, ALLK)))]
                    for src, a, z in parts:
                        nc.vector.tensor_copy(kout_hi[0:m, n % OUTS, a:z], src)
                        last = nc.vector.tensor_copy(kout_hib[0:m, n % OUTS, a:z], src)
                    link(last)
                    for src, a, z in parts:
                        last = nc.vector.tensor_tensor(kout_lob[0:m, n % OUTS, a:z], src, kout_hi[0:m, n % OUTS, a:z], ALU.subtract)
                elif kind == "v":
                    m = P if what[1] < B else B * REST
                    last = nc.vector.tensor_copy(vout[0:m, n % OUTS, :], ps[0:m, bank, :])
                else:
                    dve.wait_ge(s_ones, 1)
                    m = P if what < B else B * REST
                    last = nc.vector.tensor_copy(nvout[0:m, n % OUTS, :, 0:DN], ps[0:m, bank, 0:KVN * DN].rearrange("p (g d) -> p g d", g=KVN))
                last.then_inc(s_ev, 1)

            for i in range(len(pieces)):
                if i < NX:
                    take_stream(i)
                for n, job in enumerate(jobs):
                    if job[0] == i:
                        take_product(n, *job)
                if i == 4:
                    make_rows()

        @block.sync
        def _(sp):
            def load_piece(i):
                if i >= SETS:
                    sp.wait_ge(s_lo, i - SETS + 1)
                p, name, src, st = pieces[i]
                sp.dma_start(view(raw, i), src).then_inc(s_w[i % SETS], 16)
                if name == "nq":
                    if p:
                        sp.wait_ge(s_hi, len(pieces) // 2)
                    sp.dma_start(normw[:, :], ins[f"L{2 * p + 1}_xattn_norm_w"].rearrange("(k p) -> p k", p=P)).then_inc(s_nw, 16)

            with nc.allow_non_contiguous_dma(reason="columns of norm weights"):
                sp.dma_start(ctx_in[:, 0:B, :], ins["ctx_2048"][:, 0:P].rearrange("b p d -> p b d")).then_inc(s_c, 16)
                for b in range(B):
                    sp.dma_start(ctx_in[b * REST:(b + 1) * REST, B, :], ins["ctx_2048"][b, P:KEYS]).then_inc(s_c, 16)
                def load_stream(x):
                    if x >= 2:
                        sp.wait_ge(s_xt, x - 1)
                    sp.dma_start(tokens_in[:, x % 2], ins["x"].rearrange("b (c t p) d -> (b c) p t d", t=4, p=P)[x]).then_inc(s_x[x % 2], 16)

                load_piece(0)
                load_stream(0)
                load_piece(1)
                load_piece(2)
                load_stream(1)
                for a, name in enumerate(("mask_S_fk1", "mask_S_fk0")):
                    sp.dma_start(mrow[:, a, :], ins[name].rearrange("(a n) -> a n", a=1)).then_inc(s_small, 16)
                for p in range(2):
                    for a, name in enumerate("AB"):
                        at = 4 * p + 2 * a
                        sp.dma_start(idx[:, at:at + 2], ins[f"L{2 * p}_xattn_token_indices_{name}"].rearrange("(a n) -> a n", a=1)).then_inc(s_small, 16)
                for i in range(len(pieces)):
                    if i + SETS < len(pieces):
                        load_piece(i + SETS)
                    if i < NX:
                        if i + 2 < NX:
                            load_stream(i + 2)
                        sp.wait_ge(s_xc, KC * (i + 1))
                        sp.dma_start(dr["stream"][i // 2, i % 2], tokens_t[:, i % 2]).then_inc(s_xs[i % 2], 16)
                    for n, j in enumerate(jobs):
                        if j[0] == i:
                            store_job(sp, n)
                sp.wait_ge(s_rows, rows_ready[0])
                for t in range(2):
                    sp.dma_start(dr["maskrows"][t:t + 1].rearrange("o (a r) n -> o a r n", a=2),
                                 mpart[:, :, :, t * TOK:(t + 1) * TOK]).then_inc(s_rowst, 16)
                sp.dma_start(dr["keyrows"].rearrange("(o p) r n -> o p r n", o=1), keyrow[:]).then_inc(s_rowst, 16)
                sp.wait_ge(s_rowst, 48)
                for h in range(2):
                    sp.wait_ge(s_xs[h], 16 * (NX // 2))
                for h in range(OUTS):
                    sp.wait_ge(s_st[h], 48 * len(range(h, len(jobs), OUTS)))

        @block.scalar
        def _(act):
            for i, (p, name, src, st) in enumerate(pieces):
                act.wait_ge(s_w[i % SETS], 16 * (i // SETS + 1))
                wait_piece_free(act, i)
                if name == "nq":
                    act.wait_ge(s_nw, 16 * (p + 1))
                    for k in range(KC):
                        nc.scalar.activation(view(raw, i)[:, k], view(raw, i)[:, k], ACT.Copy,
                                             scale=normw[:, k:k + 1]).then_inc(s_evh, 1)
                    act.wait_ge(s_evh, KC * (p + 1))
                nc.scalar.activation(view(hi, i), view(raw, i), ACT.Copy).then_inc(s_hi, 1)
                if st is not None:
                    act.wait_ge(s_lo, i + 1)
                    stored = s_wst[sum(not used(k) for k in range(i)) % 4]
                    act.dma_start(st[0], view(hi, i).bitcast(F32)).then_inc(stored, 16)
                    act.dma_start(st[1], view(lo, i).bitcast(F32)).then_inc(stored, 16)
            for k in range(4):
                act.wait_ge(s_wst[k], 32 * 2)

        @block.gpsimd
        def _(pool):
            nc.gpsimd.memset(ident[:], 0.0).then_inc(s_pool, 1)
            pool.wait_ge(s_pool, 1)
            nc.gpsimd.affine_select(out=ident[:], in_=ident[:], compare_op=ALU.not_equal, fill=1.0, base=0,
                                    pattern=[[-1, P]], channel_multiplier=1).then_inc(s_ident, 1)
            nc.gpsimd.memset(nvout[:], 0.0).then_inc(s_pool, 1)
            pool.wait_ge(s_pool, 2)
            for u in range(KVN):
                nc.gpsimd.memset(nvout[:, :, u, DN + 4 * u:DN + 4 * u + 4], 1.0)
            nc.gpsimd.iota(keyno[:], pattern=[[1, KEYS]], base=0, channel_multiplier=0).then_inc(s_ones, 1)
            for i, (p, name, src, st) in enumerate(pieces):
                pool.wait_ge(s_hi, i + 1)
                wait_piece_free(pool, i)
                nc.gpsimd.tensor_tensor(view(lo, i), view(raw, i), view(hi, i), ALU.subtract).then_inc(s_lo, 1)

        @block.tensor
        def _(pe):
            pe.wait_ge(s_ident, 1)
            pe.wait_ge(s_c, 16 * (B + 1))
            for k in range(KCT):
                if k >= 1:
                    pe.wait_ge(s_cs, 4 * k)
                for t in range(5):
                    n = P if t < 4 else ALLK - 512
                    bank, col = (k % 2) * 2 + (t // 4), (t % 4) * P
                    last = nc.tensor.transpose(ps[:, bank, col:col + n], ctx_in[0:n, t, k * P:(k + 1) * P], ident[0:n, 0:n])
                last.then_inc(s_ct, 1)
            def turn_stream(x):
                pe.wait_ge(s_x[x % 2], 16 * (x // 2 + 1))
                if x:
                    pe.wait_ge(s_xc, KC * x)
                for k in range(KC):
                    for t in range(4):
                        last = nc.tensor.transpose(ps[:, 6 + k, t * P:(t + 1) * P], tokens_in[:, x % 2, t, k * P:(k + 1) * P], ident[:])
                last.then_inc(s_xt, 1)

            def make_product(n, i, kind, what):
                pe.wait_ge(s_lo, i + 1)
                if n >= 3:
                    pe.wait_ge(s_ev, n - 2)
                bank = 2 * (n % 3)
                wh, wl = view(hi, i), view(lo, i)
                if kind in ("k", "nk"):
                    cols = slice((what % 4) * P, (what % 4) * P + P) if kind == "k" else slice(0, KVN * DN)
                    m = P if kind == "k" else KVN * DN
                    for half, (a, z) in enumerate(((0, 512), (512, ALLK))):
                        pairs = [q for k in range(KCT) for q in split3(wh[:, k, cols], wl[:, k, cols], ctx_hi[:, k, a:z], ctx_lo[:, k, a:z])]
                        for j, (l, r) in enumerate(pairs):
                            last = nc.tensor.matmul(ps[0:m, bank + half, 0:z - a], l, r, start=(j == 0), stop=(j == len(pairs) - 1))
                else:
                    t = what[1] if kind == "v" else what
                    n_cols = 512 if kind == "v" else KVN * DN
                    m = P if t < B else B * REST

                    def tok(c, k):
                        return c[:, k, t * P:t * P + m]

                    pairs = [q for k in range(KCT) for q in split3(tok(ctx_hi, k), tok(ctx_lo, k), wh[:, k, :], wl[:, k, :])]
                    for j, (l, r) in enumerate(pairs):
                        last = nc.tensor.matmul(ps[0:m, bank, 0:n_cols], l, r, start=(j == 0), stop=(j == len(pairs) - 1))
                last.then_inc(s_mm, 1)

            pe.wait_ge(s_cs, 4 * KCT)
            for i in range(len(pieces)):
                if i < NX:
                    turn_stream(i)
                for n, job in enumerate(jobs):
                    if job[0] == i:
                        make_product(n, *job)


GB = 3
OUT_BATCHES = (4, 4, 2, 2)
KEPT = 10
PLACES = ((0, 1, 2, 3, 4, 5, 6, 7), (8, 9, 0, 1, 2, 3, 4, 5), (6, 7, 8, 9), (4, 5, 6, 7))
ITER = 2 * B
TINY = 1e-37
NARROW_KEYS_AT, WIDE_KEYS_AT = (2, 3, 4, 7), (9, 10, 11)


def wide(n):
    return n < WSTEPS


def half_of(n):
    return (n // 4) % 2


def slot(n):
    return n % 2 if wide(n) else ((n - WSTEPS) // 2) % 2


def first_tile(n):
    return 2 * n if wide(n) else 2 * WSTEPS + (n - WSTEPS)


def chunk_tile(c, k):
    return first_tile(4 * c) + k


def chunk_of(tile):
    c = max(c for c in range(4) if chunk_tile(c, 0) <= tile)
    return c, tile - chunk_tile(c, 0)


def place(tile):
    c, k = chunk_of(tile)
    return PLACES[c][k]


def last_in_place(tile):
    for back in range(1, 25):
        old, ago = (tile - back) % 24, int(tile - back < 0)
        if place(old) == place(tile):
            return old, ago


def window():
    order = []

    def queries(n, part):
        if wide(n % STEPS) or (part == 0 and n % 2 == 0 and n < STEPS):
            order.append(("query", n % STEPS, part, n // STEPS))

    def maxima(n, parts):
        order.extend(("max", n % STEPS, i, n // STEPS) for i in parts)

    def finish(what, c, k):
        if k < OUT_BATCHES[c - 1]:
            order.append((what, (c - 1) % 4, k, -1 if c == 0 else 0))

    usual = {(0, "c"): (("scale", 0),), (0, "e"): (("norm", 0), ("low", 0)),
             (1, "a"): (("output", 0), ("scale", 1), ("norm", 1)), (1, "b"): (("low", 1),),
             (1, "c"): (("output", 1), ("scale", 2), ("norm", 2)), (1, "e"): (("low", 2),),
             (2, "a"): (("output", 2), ("scale", 3), ("norm", 3)), (2, "b"): (("low", 3),),
             (2, "c"): (("output", 3),)}
    slower = {(0, "e"): (("scale", 0),), (1, "a"): (("norm", 0),), (1, "b"): (("low", 0),),
              (1, "c"): (("output", 0), ("scale", 1)), (1, "e"): (("norm", 1),),
              (2, "a"): (("low", 1), ("output", 1), ("scale", 2)), (2, "c"): (("norm", 2),),
              (2, "e"): (("low", 2), ("output", 2), ("scale", 3)),
              (3, "a"): (("norm", 3),), (3, "b"): (("low", 3),), (3, "c"): (("output", 3),)}

    def last_chunk(c, g, where):
        for what, k in (slower if c >= 2 else usual).get((g, where), ()):
            finish(what, c, k)

    def invert(c):
        if c >= 2:
            order.append(("guard", c, 0, 0))
        order.append(("invert", c, 0, 0))

    def inverse(c):
        order.append(("inverse", c % 4, 0, -1 if c < 0 else 0))

    for n in range(STEPS):
        c, g = n // 4, n % 4
        to_narrow = n in (7, 11)
        order.append(("rest", n, 0, 0))
        if not to_narrow:
            maxima(n + 1, (2, 3))
            if g == 0:
                inverse(c - 1)
            queries(n + 1, 1)
        order.extend(("score", n, j, 0) for j in (0, 1))
        if n == 2:
            order.append(("split", 1, 0, 0))
        elif n == 7:
            order.append(("rate", c + 1, 0, 0))
        elif n == 13:
            order.append(("split", 0, 0, 1))
        if wide(n):
            last_chunk(c, g, "a")
        if not to_narrow:
            maxima(n + 1, (4, 5))
        if wide(n):
            order.append(("value", n, 0, 0))
            last_chunk(c, g, "b")
        else:
            last_chunk(c, g, "a")
        if n == 7:
            queries(n + 1, 0)
        if not to_narrow:
            maxima(n + 1, (6,))
        order.append(("score", n, 2, 0))
        if not to_narrow:
            maxima(n + 1, (7,))
        if not wide(n):
            last_chunk(c, g, "b")
        order.append(("score", n, 3, 0))
        last_chunk(c, g, "c")
        if n == 11:
            order.extend((("squares", c + 1, 0, 0), ("value", n, 1, 0), ("square", c + 1, 0, 0)))
            order.extend((("rate", c + 1, 0, 0), ("add", n, 0, 0)))
            queries(n + 1, 0)
        if to_narrow:
            maxima(n + 1, range(8))
        if n + 2 not in (8, 12):
            queries(n + 2, 0)
        order.append(("turn", (n + 1) % STEPS, 0, (n + 1) // STEPS))
        if n == 6:
            order.append(("squares", c + 1, 0, 0))
        if n != 11:
            order.append(("value", n, 1, 0))
            if g and not wide(n):
                order.append(("add", n, 0, 0))
        last_chunk(c, g, "e")
        if n == 6:
            order.append(("square", c + 1, 0, 0))
        if n + 2 not in (8, 12):
            maxima(n + 2, (0, 1))
        if g == 3:
            invert(c)
    return order


WINDOW = window()


def present(it, turn):
    return not isinstance(it, int) or 0 <= it + turn < ITER


class Signal:

    def __init__(self, sem, kinds, times=1):
        self.sem, self.times = sem, times
        mine = [x for x in WINDOW if x[0] in kinds]
        mine = [x for t in (1, 0, -1) for x in mine if x[3] == t]
        self.number = {x[:3]: i + 1 for i, x in enumerate(mine)}
        self.per = len(self.number) * times

    def after(self, it, *key):
        return it * self.per + self.number[key] * self.times

    def before(self, it, number):
        return it * self.per + max(number, 0) * self.times


def wait(eng, sem, value):
    if not isinstance(value, int) or value > 0:
        eng.wait_ge(sem, value)


GENERAL = [(*x, m) for x in WINDOW if x[0] in ("query", "max", "turn", "output", "square", "rate")
           for m in range(KC if x[0] == "output" else 1)]
assert len(GENERAL) % GB == 0
BANK = {(*use[:3], use[4]): i % GB for i, use in enumerate(GENERAL)}


def run_layers(nc, ins, dr):
    ctx = ExitStack()
    with ctx:
        def sb(name, shape, dt=F32):
            return ctx.enter_context(nc.sbuf_tensor(name, shape, dt))

        def sem(name):
            return ctx.enter_context(nc.semaphore(name))

        def signal(name, *kinds, times=1):
            return Signal(sem(name), kinds, times)

        x = sb("x", [P, 2, KC, TOK])
        wq = [sb(f"wq_{a}", [P, KC, WI], F32R) for a in ("hi", "lo")]
        wo = [sb(f"wo_{a}", [P, H // 2, C], F32R) for a in ("hi", "lo")]
        nq = [sb(f"nq_{a}", [P, KC, C], F32R) for a in ("hi", "lo")]
        no = [sb(f"no_{a}", [P, KVN, C], F32R) for a in ("hi", "lo")]
        bias = sb("bias", [P, KC])
        w_pair, n_pair = (sb(a + "_pair", [P, H, P], F32R) for a in "wn")
        w_aux, n_aux = (sb(a + "_aux", [P, H, P], BF16) for a in "wn")
        w_top, n_top = (sb(a + "_top", [P, H, KEYS], BF16) for a in "wn")
        w_pair_rest, w_aux_rest = sb("w_pair_rest", [P, H, P], F32R), sb("w_aux_rest", [P, H, P], BF16)
        n_pair_rest, n_aux_rest = sb("n_pair_rest", [P, KVN, P], F32R), sb("n_aux_rest", [P, KVN, P], BF16)
        w_val, w_val_rest = sb("w_val", [P, WI]), sb("w_val_rest", [P, WI])
        n_val, n_val_rest = sb("n_val", [P, KVN, 32]), sb("n_val_rest", [P, KVN, P])
        x_hi, x_lo = sb("x_hi", [P, KC, TOK], F32R), sb("x_lo", [P, KC, TOK], F32R)
        xn = sb("xn", [P, KC, TOK])
        q_pair = sb("q_pair", [P, 2, 4, TOK], F32R)
        q_aux = sb("q_aux", [P, 2, 2, 4, TOK], BF16)
        probs = sb("probs", [P, 4, TOK])
        probs_rest = sb("probs_rest", [P, 2, TOK])
        kept = sb("kept", [P, KEPT, TOK])
        total = sb("total", [P, TOK])
        inv = sb("inv", [P, TOK])
        inv_b = sb("inv_b", [P, 2, TOK])
        a_hi, a_lo = sb("a_hi", [P, 2, TOK], F32R), sb("a_lo", [P, 2, TOK], F32R)
        tops = sb("tops", [P, 4, 4], BF16)
        meansq, rate, power = sb("meansq", [P, 4]), sb("rate", [P, 4]), sb("power", [P, 4])
        ident, ident_bf, ones = sb("ident", [P, P]), sb("ident_bf", [P, P], BF16), sb("ones", [P, 1])
        sel, sel_rest = sb("sel", [P, 4, 32]), sb("sel_rest", [P, 4, P])

        general = ctx.enter_context(nc.psum_tensor("general", [P, GB, 512], F32))
        score_ps = ctx.enter_context(nc.psum_tensor("score_ps", [P, 2, 512], F32))
        out_ps = ctx.enter_context(nc.psum_tensor("out_ps", [P, 2, 512], F32))
        sum_ps = ctx.enter_context(nc.psum_tensor("sum_ps", [P, 512], F32))

        CLEARED = 17
        WIDE, NARROW = 16 * 13, 16 * 18
        WKEYS, NKEYS = 16 * 27, 16 * 53

        cleared = sem("cleared")
        filled, rows_filled = sem("filled"), sem("rows_filled")
        ident_ready = sem("ident_ready")
        masks_loaded = sem("masks_loaded")
        wide_loaded, narrow_loaded = sem("wide_loaded"), sem("narrow_loaded")
        wkeys_loaded, nkeys_loaded = sem("wkeys_loaded"), sem("nkeys_loaded")
        early_loaded = signal("early_loaded", "split", times=16)
        x_loaded, x_stored = [sem(f"x_loaded{t}") for t in range(2)], [sem(f"x_stored{t}") for t in range(2)]
        sums_stored, inv_loaded = signal("sums_stored", "inverse", times=16), signal("inv_loaded", "scale", times=64)
        pe_query, pe_max, pe_turn = signal("pe_query", "query"), signal("pe_max", "max"), signal("pe_turn", "turn")
        pe_score, pe_value = signal("pe_score", "rest", "score"), signal("pe_value", "value")
        pe_output, pe_square, pe_rate = signal("pe_output", "output", times=KC), signal("pe_square", "square"), signal("pe_rate", "rate")
        act_split, act_query, act_exp = signal("act_split", "split", "rate"), signal("act_query", "query"), signal("act_exp", "rest", "score")
        act_turn, act_keep, act_norm = signal("act_turn", "turn"), signal("act_keep", "value"), signal("act_norm", "norm")
        act_square = signal("act_square", "squares")
        dve_aux, dve_query = signal("dve_aux", "query"), signal("dve_query", "query")
        dve_guard = signal("dve_guard", "guard")
        dve_max, dve_invert = signal("dve_max", "max"), signal("dve_invert", "invert", "inverse")
        dve_output = signal("dve_output", "output", times=KC)
        dve_square, dve_rate = signal("dve_square", "square"), signal("dve_rate", "rate")
        pool_split, pool_rate = signal("pool_split", "split", "rate"), signal("pool_rate", "square")
        pool_scale, dve_low = signal("pool_scale", "scale"), signal("dve_low", "low")
        pool_add = signal("pool_add", "add")
        reader = {"query": dve_query, "max": dve_max, "turn": act_turn, "output": dve_output,
                  "square": dve_square, "rate": dve_rate}

        block = ctx.enter_context(nc.Block())

        def each_batch(eng, do):
            def one_turn(it):
                loop = not isinstance(it, int)
                batch = {turn: eng.snap(it + turn) if loop else it + turn for turn in (-1, 0, 1)}
                for what, n, k, turn in WINDOW:
                    if present(it, turn):
                        do(batch[turn], what, n, k)

            one_turn(-1)
            one_turn(0)
            with eng.Fori(1, ITER - 1) as it:
                one_turn(it)
            one_turn(ITER - 1)
            one_turn(ITER)

        def bank_of(use):
            return general[:, BANK[use], :]

        @block.sync
        def _(sp):
            def load_wide(p):
                for i, a in enumerate(("hi", "lo")):
                    sp.dma_start(wq[i][:].bitcast(F32), dr["wq_" + a][p]).then_inc(wide_loaded, 16)
                for i, a in enumerate(("hi", "lo")):
                    sp.dma_start(wo[i][:].bitcast(F32), dr["wo_" + a][p]).then_inc(wide_loaded, 16)
                sp.dma_start(bias[:], ins[f"L{2 * p}_xattn_bo"].rearrange("(k p) -> p k", p=P),
                             allow_slow_non_contiguous=True).then_inc(wide_loaded, 16)
                if p == 0:
                    sp.wait_ge(cleared, CLEARED)
                for par in range(2):
                    a = 64 * (1 - par)
                    def every(buf):
                        return buf[a:a + 6].rearrange("p (h two) k -> p h two k", two=2)[:, :, par, :]
                    rows = dr["keyrows"][p]
                    sp.dma_start(every(w_aux), rows[:, None, 0:P].to_broadcast([6, 8, P])).then_inc(wide_loaded, 16)
                    sp.dma_start(every(w_top), rows[:, None, :].to_broadcast([6, 8, KEYS])).then_inc(wide_loaded, 16)
                for j in range(4):
                    a = 64 * (1 - j % 2)
                    rests = w_aux_rest[a:a + 6].rearrange("p (g j) k -> p g j k", j=4)
                    sp.dma_start(rests[:, :, j, 32 * j:32 * j + REST],
                                 dr["keyrows"][p][:, None, P:KEYS].to_broadcast([6, 4, REST])).then_inc(wide_loaded, 16)

            def load_narrow(p):
                for i, a in enumerate(("hi", "lo")):
                    sp.dma_start(nq[i][:].bitcast(F32), dr["nq_" + a][p]).then_inc(narrow_loaded, 16)
                    for j in range(4):
                        src = dr["no_" + a][p].rearrange("(v j i) k n -> v j i k n", j=4, i=DN)
                        for v in range(2):
                            dst = no[i][32 * j:32 * j + DN].rearrange("p (k v) n -> p k v n", v=2)
                            sp.dma_start(dst[:, :, v, :].bitcast(F32), src[v, j]).then_inc(narrow_loaded, 16)
                sp.wait_ge(narrow_loaded, p * NARROW + NARROW)

            def cols(src, b):
                return src[..., bass.ds(b * P, P)], src[..., bass.ds(b * REST + B * P, REST)]

            def load_wide_keys(p, b, part):
                def go(dst, src):
                    sp.dma_start(dst, src).then_inc(wkeys_loaded, 16)

                if part < 2:
                    par = part
                    rows = slice(64 * par, 64 * par + 64)
                    every = lambda buf: buf.rearrange("p (h two) k -> p h two k", two=2)[:, :, par, :]
                    main, rest = cols(dr["wk_hi"][p, rows], b)
                    for half in range(2):
                        to = slice(64 * half, 64 * half + 64)
                        go(every(w_pair[to]).bitcast(F32), main)
                        for jj in (par, par + 2):
                            heads = w_pair_rest[to].rearrange("p (g j) k -> p g j k", j=4)
                            go(heads[:, :, jj, 32 * jj:32 * jj + REST].bitcast(F32),
                               rest.rearrange("p (g two) k -> p g two k", two=2)[:, :, jj // 2, :])
                    main, rest = cols(dr["wk_lob"][p, rows], b)
                    go(every(w_aux[rows]), main)
                    for jj in (par, par + 2):
                        heads = w_aux_rest[rows].rearrange("p (g j) k -> p g j k", j=4)
                        go(heads[:, :, jj, 32 * jj:32 * jj + REST],
                           rest.rearrange("p (g two) k -> p g two k", two=2)[:, :, jj // 2, :])
                    main, rest = cols(dr["wk_hib"][p, rows], b)
                    go(every(w_top[rows])[:, :, 0:P], main)
                    go(every(w_top[rows])[:, :, P:KEYS], rest)
                else:
                    go(w_val[:], dr["wv"][p, bass.ds(b, 1)].rearrange("o p n -> p (o n)"))
                    for j in range(4):
                        dst = w_val_rest[32 * j:32 * j + REST].rearrange("p (g j d) -> p g j d", j=4, d=DW)
                        src = dr["wv_rest"][p, bass.ds(b * REST, REST)].rearrange("p (g j d) -> p g j d", j=4, d=DW)
                        go(dst[:, :, j, :], src[:, :, j, :])

            def load_narrow_keys(p, b, j):
                def go(dst, src):
                    sp.dma_start(dst, src).then_inc(nkeys_loaded, 16)

                def by_unit(src, w):
                    return src.rearrange("(u i) k -> i u k", i=DN)

                heads = lambda buf: buf.rearrange("p (u j) k -> p u j k", j=4)[:, :, j, :]
                main, rest = cols(dr["nk_hi"][p], b)
                for half in range(2):
                    to = slice(64 * half + DN * j, 64 * half + DN * j + DN)
                    go(heads(n_pair[to]).bitcast(F32), by_unit(main, P))
                    go(n_pair_rest[to, :, 32 * j:32 * j + REST].bitcast(F32), by_unit(rest, REST))
                lo, lo_rest = cols(dr["nk_lob"][p], b)
                hi, hi_rest = cols(dr["nk_hib"][p], b)
                for par in range(2):
                    to = slice(64 * par + DN * j, 64 * par + DN * j + DN)
                    odd = lambda ap: ap.rearrange("p (v two) k -> p v two k", two=2)[:, :, par, :]
                    go(odd(heads(n_aux[to])), odd(by_unit(lo, P)))
                    go(odd(n_aux_rest[to, :, 32 * j:32 * j + REST]), odd(by_unit(lo_rest, REST)))
                    go(odd(heads(n_top[to]))[:, :, 0:P], odd(by_unit(hi, P)))
                    go(odd(heads(n_top[to]))[:, :, P:KEYS], odd(by_unit(hi_rest, REST)))
                go(n_val_rest[32 * j:32 * j + REST, :, 32 * j:32 * j + 32], dr["nv_rest"][p, bass.ds(b * REST, REST)])
                if j == 0:
                    go(n_val[:], dr["nv"][p, bass.ds(b, 1)].rearrange("o p g d -> p (o g) d"))

            def load_x(t, b):
                sp.dma_start(x[:, t], dr["stream"][bass.ds(b, 1), t].rearrange("o p k n -> p (o k) n")).then_inc(x_loaded[t], 16)

            def load_early(t, b):
                sp.dma_start(xn[:], dr["stream"][bass.ds(b, 1), t].rearrange("o p k n -> p (o k) n")).then_inc(early_loaded.sem, 16)

            def store_x(t, it, b):
                wait(sp, dve_output.sem, dve_output.after(it, "output", 2 + t, 1))
                halves = dr["stream"].rearrange("b t p k n -> (b t) p k n")
                sp.dma_start(halves[bass.ds(2 * b + t, 1)].rearrange("o p k n -> p (o k) n"), x[:, t]).then_inc(x_stored[t], 16)
                wait(sp, x_stored[t], 16 * it + 16)

            def spread_inverses(c, batch):
                for q in range(4):
                    if c < 2:
                        dst = inv_b[64 * (q % 2):64 * (q % 2) + 64, q // 2, :]
                        row = 32 * q + 8 * batch
                        src = dr["sums"][row:row + 1, :].to_broadcast([64, TOK])
                    else:
                        dst = inv_b[32 * q:32 * q + 32, :, :]
                        row = 32 * q + DN + 8 * batch
                        src = dr["sums"][row:row + 8, :].rearrange("(u r) n -> r u n", r=4)[0:1].to_broadcast([32, 2, TOK])
                    sp.dma_start(dst, src).then_inc(inv_loaded.sem, 16)

            def one_turn(it, p, b):
                batch = {turn: sp.snap(it + turn) if not isinstance(it, int) else it + turn for turn in (-1, 0, 1)}
                switch = isinstance(it, int)
                if switch:
                    b_before, next_p, next_b = (b - 1) % B, p + (b + 1) // B, (b + 1) % B
                else:
                    b_before, next_p, next_b = sp.snap(b - 1), p, sp.snap(b + 1)
                more = not switch or it + 1 < ITER
                for what, c, k, turn in WINDOW:
                    if not present(it, turn):
                        continue
                    now = batch[turn]
                    if what == "inverse":
                        wait(sp, dve_invert.sem, dve_invert.after(now, what, c, 0))
                        sp.dma_start(dr["sums"], inv[:]).then_inc(sums_stored.sem, 16)
                        wait(sp, sums_stored.sem, sums_stored.after(now, what, c, 0))
                        spread_inverses(c, 0)
                    elif what == "scale" and k + 1 < OUT_BATCHES[c]:
                        wait(sp, pool_scale.sem, pool_scale.after(now, what, c, k))
                        spread_inverses(c, k + 1)
                    elif (what, c, k) == ("output", 3, 1):
                        store_x(1, now, b_before)
                        if not switch or 0 < it < ITER:
                            load_x(1, b)
                        if switch and it == B:
                            wait(sp, pe_output.sem, pe_output.after(now, what, c, k))
                            load_narrow(1)
                    elif what == "query" and (c, k) == (14, 0) and more:
                        wait(sp, act_split.sem, act_split.after(now, "rate", 3, 0))
                        wait(sp, pool_split.sem, pool_split.after(now, "rate", 3, 0))
                        if switch and it == B - 1:
                            sp.wait_ge(wide_loaded, 2 * WIDE)
                        load_early(0, next_b)
                    elif what == "split" and c == 0:
                        wait(sp, act_split.sem, act_split.after(now, what, c, k))
                        wait(sp, pool_split.sem, pool_split.after(now, what, c, k))
                        load_early(1, next_b)
                    elif turn == 1:
                        continue
                    elif what == "turn" and c in NARROW_KEYS_AT and (not switch or it > 0):
                        if c == NARROW_KEYS_AT[0]:
                            wait(sp, pe_value.sem, pe_value.after(batch[-1], "value", STEPS - 1, 1))
                        load_narrow_keys(p, b, NARROW_KEYS_AT.index(c))
                    elif what == "turn" and c in WIDE_KEYS_AT and more:
                        if c == WIDE_KEYS_AT[0]:
                            wait(sp, pe_value.sem, pe_value.after(now, "value", WSTEPS - 1, 1))
                        load_wide_keys(next_p, next_b, WIDE_KEYS_AT.index(c))
                    elif (what, c, k) == ("output", 1, 3) and switch and it == B - 1:
                        wait(sp, pe_output.sem, pe_output.after(now, what, c, k))
                        load_wide(1)
                    elif (what, c, k) == ("output", 2, 1):
                        store_x(0, now, b)
                        if more:
                            load_x(0, next_b)

            load_early(0, 0)
            load_wide(0)
            for t in range(2):
                for par in range(2):
                    a = 64 * (1 - par)
                    sp.dma_start(q_aux[a:a + 6, t].rearrange("p s (j two) n -> p (s j) two n", two=2)[:, :, par, :],
                                 dr["maskrows"][t][:, None, :].to_broadcast([6, 4, TOK])).then_inc(masks_loaded, 16)
            for part in range(3):
                load_wide_keys(0, 0, part)
            wait(sp, act_split.sem, act_split.after(0, "split", 0, 0))
            wait(sp, pool_split.sem, pool_split.after(0, "split", 0, 0))
            load_early(1, 0)
            load_x(0, 0)
            load_x(1, 0)
            load_narrow(0)
            for part in range(KVN):
                load_narrow_keys(0, 0, part)
            for p in range(2):
                one_turn(B * p, p, 0)
                with sp.Fori(1, B - 1) as b:
                    one_turn(sp.snap(b + B * p), p, sp.snap(b))
                one_turn(B * p + B - 1, p, B - 1)
            one_turn(ITER, 2, 0)

        @block.scalar
        def _(act):
            act.wait_ge(cleared, CLEARED)

            def do(it, what, n, k):
                if what == "split":
                    wait(act, early_loaded.sem, early_loaded.after(it, what, n, k))
                    wait(act, pe_query.sem, pe_query.before(it, 8 * n))
                    nc.scalar.activation(x_hi[:], xn[:], ACT.Copy).then_inc(act_split.sem, 1)
                elif what == "squares":
                    wait(act, dve_output.sem, dve_output.after(it, "output", n - 2, 3))
                    wait(act, act_split.sem, act_split.before(it, n))
                    wait(act, pool_split.sem, pool_split.before(it, n))
                    nc.scalar.activation(xn[:], x[:, n - 2], ACT.Square).then_inc(act_square.sem, 1)
                elif what == "rate":
                    wait(act, dve_rate.sem, dve_rate.after(it, what, n, k))
                    wait(act, pe_query.sem, pe_query.before(it, 16 + 2 * (n - 2)))
                    nc.scalar.activation(x_hi[:], xn[:], ACT.Copy).then_inc(act_split.sem, 1)
                elif what == "query":
                    wait(act, pe_query.sem, pe_query.after(it, what, n, k))
                    ps = bank_of((what, n, k, 0))
                    s, j = slot(n), 2 * k
                    nc.scalar.activation(q_pair[0:64, s, j, :], ps[0:64], ACT.Copy)
                    nc.scalar.activation(q_pair[64:P, s, j + 1, :], ps[64:P], ACT.Copy).then_inc(act_query.sem, 1)
                elif what in ("rest", "score"):
                    wait(act, pe_score.sem, pe_score.after(it, what, n, k))
                    number = pe_score.number[(what, n, k)]
                    if what == "rest":
                        wait(act, pe_value.sem, pe_value.before(it, pe_value.number[("value", n - 2, 1)] if n >= 2 else 0))
                        dst = probs_rest[:, n % 2, :]
                    else:
                        half = k // 2 if wide(n - 1) or n == 0 else 1
                        wait(act, pe_value.sem, pe_value.before(it, pe_value.number[("value", n - 1, half)] if n else 0))
                        dst = probs[:, k, :]
                    scale = (DW if wide(n) else DN) ** -0.5
                    nc.scalar.activation(dst, score_ps[:, number % 2, :], ACT.Exp, scale=scale).then_inc(act_exp.sem, 1)
                elif what == "turn":
                    wait(act, pe_turn.sem, pe_turn.after(it, what, n, k))
                    ps = bank_of((what, n, k, 0))
                    units = range(4) if wide(n) else (n % 2,)
                    for j in units:
                        a = 64 * (1 - j % 2) + ROW_M
                        last = nc.scalar.activation(q_aux[a:a + 4, half_of(n), slot(n), j, :], ps[0:4].bitcast(BF16)[:, 0:TOK], ACT.Copy, scale=-1.0)
                    last.then_inc(act_turn.sem, 1)
                elif what == "value":
                    wait(act, pe_value.sem, pe_value.after(it, what, n, k))
                    tile = first_tile(n) + (k if wide(n) else 0)
                    old, ago = last_in_place(tile)
                    c, i = chunk_of(old)
                    wait(act, dve_low.sem, dve_low.after(it - ago, "low", c, i // 2))
                    wait(act, act_norm.sem, act_norm.after(it - ago, "norm", c, i // 2))
                    nc.scalar.activation(kept[:, place(tile), :], out_ps[:, tile % 2, :], ACT.Copy).then_inc(act_keep.sem, 1)
                elif what == "norm":
                    wait(act, pool_scale.sem, pool_scale.after(it, "scale", n, k))
                    wait(act, pe_output.sem, pe_output.before(it, pe_output_before(n, k)))
                    for i in range(2):
                        tile = chunk_tile(n, 2 * k + i)
                        last = nc.scalar.activation(a_hi[:, i, :], kept[:, place(tile), :], ACT.Copy)
                    last.then_inc(act_norm.sem, 1)

            def pe_output_before(c, k):
                return pe_output.number[("output", c, k)] - 1

            each_batch(act, do)

        @block.gpsimd
        def _(pool):
            for buf in (w_pair, n_pair, w_pair_rest, n_pair_rest):
                nc.gpsimd.memset(buf[:].bitcast(F32), 0.0).then_inc(cleared, 1)
            nc.gpsimd.memset(ident[:], 0.0).then_inc(ident_ready, 1)
            pool.wait_ge(ident_ready, 1)
            nc.gpsimd.affine_select(out=ident[:], in_=ident[:], compare_op=ALU.not_equal, fill=1.0, base=0,
                                    pattern=[[-1, P]], channel_multiplier=1).then_inc(ident_ready, 1)
            nc.gpsimd.memset(power[:], -0.5).then_inc(ident_ready, 1)
            pool.wait_ge(ident_ready, 3)
            nc.gpsimd.tensor_copy(ident_bf[:], ident[:]).then_inc(ident_ready, 1)
            pool.wait_ge(ident_ready, 4)
            pool.wait_ge(cleared, CLEARED)

            done = [0]

            def diagonal(rows, pattern, first=0):
                if done[0]:
                    pool.wait_ge(rows_filled, done[0])
                done[0] += 1
                nc.gpsimd.affine_select(out=rows, in_=rows, compare_op=ALU.not_equal, fill=1.0, base=-first,
                                        pattern=pattern, channel_multiplier=1).then_inc(rows_filled, 1)

            for par in range(2):
                a = 64 * (1 - par) + ROW_M
                for j in (par, par + 2):
                    heads = w_aux[a:a + 4].rearrange("p (g j) k -> p g j k", j=4)
                    diagonal(heads[:, :, j, :], [[0, 4], [0, P]], first=j)
                    rests = w_aux_rest[a:a + 4].rearrange("p (g j) k -> p g j k", j=4)
                    diagonal(rests[:, :, j, 32 * j:32 * j + REST], [[0, 4], [0, REST]], first=j)
                for u in (par, par + 2):
                    diagonal(n_aux[a:a + 4, 4 * u:4 * u + 4, :], [[-1, 4], [0, P]])
                    rests = n_aux_rest[a:a + 4, u].rearrange("p (j k) -> p j k", j=4)
                    diagonal(rests[:, :, 0:REST], [[-1, 4], [0, REST]])
            pool.wait_ge(rows_filled, done[0])

            def do(it, what, n, k):
                if what in ("split", "rate"):
                    wait(pool, act_split.sem, act_split.after(it, what, n, k))
                    nc.gpsimd.tensor_tensor(x_lo[:], xn[:], x_hi[:], ALU.subtract).then_inc(pool_split.sem, 1)
                elif what == "square":
                    wait(pool, dve_square.sem, dve_square.after(it, what, n, k))
                    nc.gpsimd.tensor_tensor(rate[:], meansq[:], power[:], ALU.pow).then_inc(pool_rate.sem, 1)
                elif what == "add":
                    tile = first_tile(n)
                    wait(pool, act_keep.sem, act_keep.before(it, tile + 1))
                    if n % 4 == 1:
                        wait(pool, dve_invert.sem, dve_invert.before(it, 2 * (n // 4)))
                        other = kept[:, place(tile - 1), :]
                    else:
                        wait(pool, pool_add.sem, pool_add.after(it, what, n - 1, 0))
                        other = total[:]
                    nc.gpsimd.tensor_tensor(total[:], other, kept[:, place(tile), :], ALU.add).then_inc(pool_add.sem, 1)
                elif what == "scale":
                    wait(pool, inv_loaded.sem, inv_loaded.after(it, what, n, k))
                    wait(pool, act_keep.sem, act_keep.before(it, chunk_tile(n, 2 * k + 1) + 1))
                    for i in range(2):
                        tile = kept[:, place(chunk_tile(n, 2 * k + i)), :]
                        last = nc.gpsimd.tensor_tensor(tile, tile, inv_b[:, i, :], ALU.mult)
                    last.then_inc(pool_scale.sem, 1)

            each_batch(pool, do)

        @block.vector
        def _(dve):
            for buf in (w_aux, n_aux, w_top, n_top, w_aux_rest, n_aux_rest, w_val_rest, n_val_rest, q_aux, sel, sel_rest):
                nc.vector.memset(buf[:], 0.0).then_inc(cleared, 1)
            for i in range(2):
                nc.vector.memset(no[i][:].bitcast(F32), 0.0).then_inc(cleared, 1)
            dve.wait_ge(cleared, CLEARED)
            nc.vector.memset(ones[:], 1.0)
            for g in range(4):
                nc.vector.memset(sel[:, g, 8 * g:8 * g + 8], 1.0)
                for j in range(4):
                    last = nc.vector.memset(sel_rest[32 * j:32 * j + REST, g, 32 * j + 8 * g:32 * j + 8 * g + 8], 1.0)
            last.then_inc(filled, 1)

            dve.wait_ge(wide_loaded, WIDE)

            def do(it, what, n, k):
                if what == "query":
                    wait(dve, act_query.sem, act_query.after(it, what, n, k))
                    ps = bank_of((what, n, k, 0))
                    t, s, j = half_of(n), slot(n), 2 * k
                    nc.vector.tensor_copy(q_aux[0:64, t, s, j, :], q_pair[0:64, s, j, :])
                    nc.vector.tensor_copy(q_aux[64:P, t, s, j + 1, :], q_pair[64:P, s, j + 1, :]).then_inc(dve_aux.sem, 1)
                    nc.vector.tensor_tensor(q_pair[64:P, s, j, :], ps[0:64], q_pair[0:64, s, j, :], ALU.subtract)
                    last = nc.vector.tensor_tensor(q_pair[0:64, s, j + 1, :], ps[64:P], q_pair[64:P, s, j + 1, :], ALU.subtract)
                    last.then_inc(dve_query.sem, 1)
                elif what == "max":
                    wait(dve, pe_max.sem, pe_max.after(it, what, n, k))
                    if k == 0:
                        wait(dve, pe_turn.sem, pe_turn.before(it, n))
                    sub, pair = k % 4, k // 4
                    src = bank_of((what, n, k, 0))[:, 0:2 * KEYS].rearrange("p (h k) -> p h k", h=2)
                    last = nc.vector.tensor_reduce(tops[:, sub, 2 * pair:2 * pair + 2], src, AX_X, ALU.max)
                    last.then_inc(dve_max.sem, 1)
                elif what == "guard":
                    wait(dve, pool_add.sem, pool_add.after(it, "add", 4 * n + 3, 0))
                    wait(dve, sums_stored.sem, sums_stored.before(it, n))
                    nc.vector.tensor_scalar(inv[:], total[:], TINY, None, ALU.max).then_inc(dve_guard.sem, 1)
                elif what in ("invert", "inverse"):
                    if n < 2:
                        wait(dve, pe_value.sem, pe_value.after(it, "value", 4 * n + 3, 1))
                        wait(dve, sums_stored.sem, sums_stored.before(it, n))
                    else:
                        wait(dve, dve_guard.sem, dve_guard.after(it, "guard", n, 0))
                    half = slice(0, TOK // 2) if what == "invert" else slice(TOK // 2, TOK)
                    nc.vector.reciprocal(inv[:, half], (sum_ps if n < 2 else inv)[:, half]).then_inc(dve_invert.sem, 1)
                elif what == "low":
                    wait(dve, act_norm.sem, act_norm.after(it, "norm", n, k))
                    for i in range(2):
                        tile = chunk_tile(n, 2 * k + i)
                        last = nc.vector.tensor_tensor(a_lo[:, i, :], kept[:, place(tile), :], a_hi[:, i, :], ALU.subtract)
                    last.then_inc(dve_low.sem, 1)
                elif what == "output":
                    t = n % 2
                    if k == 0 and n < 2:
                        dve.wait_ge(x_loaded[t], it * 16 + 16)
                    else:
                        wait(dve, dve_output.sem, dve_output.after(it, what, *((n, k - 1) if k else (n - 2, 3))))
                        if k == 0:
                            wait(dve, dve_rate.sem, dve_rate.after(it, "rate", n, 0))
                    for m in range(KC):
                        wait(dve, pe_output.sem, pe_output.after(it, what, n, k) - (KC - 1 - m))
                        dst, ps = x[:, t, m, :], bank_of((what, n, k, m))
                        if n < 2 and k == 0:
                            last = nc.vector.scalar_tensor_tensor(out=dst, in0=ps, scalar=bias[:, m:m + 1], in1=dst, op0=ALU.add, op1=ALU.add)
                        else:
                            last = nc.vector.tensor_tensor(dst, ps, dst, ALU.add)
                        last.then_inc(dve_output.sem, 1)
                elif what == "square":
                    wait(dve, pe_square.sem, pe_square.after(it, what, n, k))
                    last = nc.vector.tensor_scalar(meansq[:], bank_of((what, n, k, 0))[:, 0:4], 1.0 / C, EPS, ALU.mult, ALU.add)
                    last.then_inc(dve_square.sem, 1)
                elif what == "rate":
                    wait(dve, pe_rate.sem, pe_rate.after(it, what, n, k))
                    ps = bank_of((what, n, k, 0))
                    for m in range(KC):
                        last = nc.vector.tensor_tensor(xn[:, m, :], ps, x[:, n - 2, m, :], ALU.mult)
                    last.then_inc(dve_rate.sem, 1)


            each_batch(dve, do)

        @block.tensor
        def _(pe):
            pe.wait_ge(ident_ready, 4)
            pe.wait_ge(filled, 1)
            pe.wait_ge(masks_loaded, 16 * 4)
            pe.wait_ge(rows_filled, 16)
            pe.wait_ge(wide_loaded, WIDE)

            def bank(it, use):
                at = [(*g[:3], g[4]) for g in GENERAL].index(use)
                turn = GENERAL[at][3]
                back = at - GB
                while isinstance(it, int) and back >= -len(GENERAL) * (ITER + 1):
                    if 0 <= it - turn + GENERAL[back % len(GENERAL)][3] + back // len(GENERAL) < ITER:
                        break
                    back -= GB
                what, n, k, of, m = GENERAL[back % len(GENERAL)]
                read = reader[what]
                wait(pe, read.sem, read.after(it - turn + of + back // len(GENERAL), what, n, k) - (read.times - 1 - m if what == "output" else 0))
                return general[:, BANK[use], :]

            def do(it, what, n, k):
                if what == "query":
                    if n == WSTEPS:
                        wait(pe, nkeys_loaded, (it + 1) * NKEYS)
                    if n % 4 == 0 and k == 0:
                        key = ("split", n // 4, 0) if wide(n) else ("rate", n // 4, 0)
                        wait(pe, pool_split.sem, pool_split.after(it, *key))
                    ps = bank(it, (what, n, k, 0))
                    w, at = (wq, 2 * (n % 4) + k) if wide(n) else (nq, (n % 4) // 2)
                    at = slice(at * P, at * P + P)
                    pairs = [q for c in range(KC) for q in split3(w[0][:, c, at], w[1][:, c, at], x_hi[:, c, :], x_lo[:, c, :])]
                    for i, (l, r) in enumerate(pairs):
                        last = nc.tensor.matmul(ps, l, r, start=(i == 0), stop=(i == len(pairs) - 1))
                    last.then_inc(pe_query.sem, 1)
                elif what == "max":
                    if k == 0 or k == 4 and wide(n):
                        wait(pe, dve_aux.sem, dve_aux.before(it, queries_for(n) - (k == 0 and wide(n))))
                        if n == 0:
                            wait(pe, wkeys_loaded, (it + 1) * WKEYS)
                    ps = bank(it, (what, n, k, 0))
                    sub, pair = slice(k % 4 * P, k % 4 * P + P), k // 4
                    q = q_aux[:, half_of(n), slot(n)]
                    if wide(n):
                        for i in range(2):
                            last = nc.tensor.matmul(ps[:, i * KEYS:(i + 1) * KEYS], q[:, 2 * pair + i, sub],
                                                    w_top[:, 4 * (n % 4) + 2 * pair + i, :], start=True, stop=True)
                    else:
                        h = 4 * (n % 4) + 2 * pair
                        last = nc.tensor.matmul(ps[:, 0:2 * KEYS], q[:, n % 2, sub],
                                                n_top[:, h:h + 2, :].rearrange("p h k -> p (h k)"), start=True, stop=True)
                    last.then_inc(pe_max.sem, 1)
                elif what == "turn":
                    wait(pe, dve_max.sem, dve_max.after(it, "max", n, 7))
                    ps = bank(it, (what, n, k, 0))
                    for sub in range(4):
                        last = nc.tensor.transpose(ps[0:4].bitcast(BF16)[:, sub * P:(sub + 1) * P], tops[:, sub, :], ident_bf[:])
                    last.then_inc(pe_turn.sem, 1)
                elif what in ("rest", "score"):
                    number = pe_score.number[(what, n, k)]
                    ps = score_ps[:, number % 2, :]
                    wait(pe, act_exp.sem, act_exp.before(it, number - 2))
                    if what == "rest":
                        wait(pe, dve_query.sem, dve_query.before(it, queries_for(n)))
                        wait(pe, act_turn.sem, act_turn.after(it, "turn", n, 0))
                    s, t, g = slot(n), half_of(n), n % 4
                    pairs = []
                    for j in (range(4) if what == "rest" else (k,)):
                        h = 4 * g + j
                        unit = j if wide(n) else n % 2
                        if what == "score":
                            keys = (w_pair[:, h], w_aux[:, h]) if wide(n) else (n_pair[:, h], n_aux[:, h])
                        elif wide(n):
                            keys = (w_pair_rest[:, h], w_aux_rest[:, h])
                        elif j == 0:
                            keys = (n_pair_rest[:, g], n_aux_rest[:, g])
                        else:
                            continue
                        pairs += [(keys[0], q_pair[:, s, unit, :]), (keys[1], q_aux[:, t, s, unit, :])]
                    for i, (l, r) in enumerate(pairs):
                        last = nc.tensor.matmul(ps, l, r, start=(i == 0), stop=(i == len(pairs) - 1))
                    last.then_inc(pe_score.sem, 1)
                elif what == "value":
                    wait(pe, act_exp.sem, act_exp.after(it, "score", n, 2 * k + 1))
                    tile, g = first_tile(n) + (k if wide(n) else 0), n % 4
                    wait(pe, act_keep.sem, act_keep.before(it, tile - 1))
                    if n in (0, 4) and k == 0:
                        wait(pe, dve_invert.sem, dve_invert.before(it, 2 * (n // 4)) - (4 if n == 0 else 0))
                    out = out_ps[:, tile % 2, :]
                    rest = probs_rest[:, n % 2, :]
                    heads = (2 * k, 2 * k + 1) if wide(n) else range(4)
                    for i, j in enumerate(heads):
                        h = 4 * g + j
                        if wide(n):
                            nc.tensor.matmul(out[64 * i:64 * i + 64], w_val[:, h * DW:(h + 1) * DW], probs[:, j, :],
                                             start=True, stop=False, skip_group_check=True)
                        else:
                            nc.tensor.matmul(out[32 * j:32 * j + 32], n_val[:, g, :], probs[:, j, :],
                                             start=True, stop=False, skip_group_check=True)
                    if wide(n):
                        for i, j in enumerate(heads):
                            h = 4 * g + j
                            nc.tensor.matmul(out[64 * i:64 * i + 64], w_val_rest[:, h * DW:(h + 1) * DW], rest,
                                             start=False, stop=True, skip_group_check=True)
                    else:
                        last = nc.tensor.matmul(out, n_val_rest[:, g, :], rest, start=False, stop=True, skip_group_check=True)
                    for j in heads if wide(n) else ():
                        last = nc.tensor.matmul(sum_ps[32 * j:32 * j + 32, :], sel[:, g, :], probs[:, j, :],
                                                start=(g == 0), stop=False, skip_group_check=True)
                    if k == 1 and wide(n):
                        last = nc.tensor.matmul(sum_ps[:], sel_rest[:, g, :], rest, start=False, stop=(g == 3), skip_group_check=True)
                    last.then_inc(pe_value.sem, 1)
                elif what == "output":
                    wait(pe, dve_low.sem, dve_low.after(it, "low", n, k))
                    w = wo if n < 2 else no
                    for m in range(KC):
                        ps = bank(it, (what, n, k, m))
                        rows = slice(m * P, m * P + P)
                        pairs = [q for i in range(2) for q in split3(w[0][:, 2 * k + i, rows], w[1][:, 2 * k + i, rows], a_hi[:, i, :], a_lo[:, i, :])]
                        for i, (l, r) in enumerate(pairs):
                            last = nc.tensor.matmul(ps, l, r, start=(i == 0), stop=(i == len(pairs) - 1))
                        last.then_inc(pe_output.sem, 1)
                elif what == "square":
                    wait(pe, act_square.sem, act_square.after(it, "squares", n, k))
                    ps = bank(it, (what, n, k, 0))
                    for sub in range(4):
                        for c in range(KC):
                            last = nc.tensor.matmul(ps[:, sub:sub + 1], xn[:, c, sub * P:(sub + 1) * P], ones[:],
                                                    start=(c == 0), stop=(c == KC - 1))
                    last.then_inc(pe_square.sem, 1)
                elif what == "rate":
                    wait(pe, pool_rate.sem, pool_rate.after(it, "square", n, k))
                    ps = bank(it, (what, n, k, 0))
                    for sub in range(4):
                        last = nc.tensor.transpose(ps[:, sub * P:(sub + 1) * P], rate[:, sub:sub + 1].to_broadcast([P, P]), ident[:])
                    last.then_inc(pe_rate.sem, 1)

            def queries_for(n):
                return 2 * (n + 1) if wide(n) else 2 * WSTEPS + (n - WSTEPS) // 2 + 1

            each_batch(pe, do)


def store_outputs(nc, dr, out):
    ctx = ExitStack()
    with ctx:
        def sem(name):
            return ctx.enter_context(nc.semaphore(name))

        ident = ctx.enter_context(nc.sbuf_tensor("o_ident", [P, P], F32))
        xt = ctx.enter_context(nc.sbuf_tensor("o_xt", [P, 2 * B, KC, TOK], F32))
        tokens = ctx.enter_context(nc.sbuf_tensor("o_tokens", [P, 2 * B, 4, C], F32))
        ps = ctx.enter_context(nc.psum_tensor("o_ps", [P, 8, 512], F32))
        ident_ready, made = sem("o_ident_ready"), sem("o_transposed")
        loaded = [sem(f"o_loaded{i}") for i in range(2 * B)]
        taken = [sem("o_taken_dve"), sem("o_taken_act")]
        stored = sem("o_stored")
        block = ctx.enter_context(nc.Block())

        @block.sync
        def _(sp):
            for i in range(2 * B):
                sp.dma_start(xt[:, i], dr["stream"][i // 2, i % 2]).then_inc(loaded[i], 16)
            for i in range(2 * B):
                for e in range(2):
                    sp.wait_ge(taken[e], i + 1)
                sp.dma_start(out.rearrange("b (c t p) d -> (b c) p t d", t=4, p=P)[i], tokens[:, i]).then_inc(stored, 16)
            sp.wait_ge(stored, 16 * 2 * B)

        @block.gpsimd
        def _(pool):
            nc.gpsimd.memset(ident[:], 0.0).then_inc(ident_ready, 1)
            pool.wait_ge(ident_ready, 1)
            nc.gpsimd.affine_select(out=ident[:], in_=ident[:], compare_op=ALU.not_equal, fill=1.0, base=0,
                                    pattern=[[-1, P]], channel_multiplier=1).then_inc(ident_ready, 1)

        @block.tensor
        def _(pe):
            pe.wait_ge(ident_ready, 2)
            for i in range(2 * B):
                pe.wait_ge(loaded[i], 16)
                if i >= 4:
                    for e in range(2):
                        pe.wait_ge(taken[e], i - 3)
                for t in range(4):
                    for k in range(KC):
                        col = (t % 2) * C + k * P
                        last = nc.tensor.transpose(ps[:, 2 * (i % 4) + t // 2, col:col + P], xt[:, i, k, t * P:(t + 1) * P], ident[:])
                last.then_inc(made, 1)

        def take(eng, copy, e):
            for i in range(2 * B):
                eng.wait_ge(made, i + 1)
                copy(tokens[:, i, 2 * e:2 * e + 2, :].rearrange("p t d -> p (t d)"), ps[:, 2 * (i % 4) + e, :]).then_inc(taken[e], 1)

        @block.vector
        def _(dve):
            take(dve, nc.vector.tensor_copy, 0)

        @block.scalar
        def _(act):
            take(act, lambda dst, src: nc.scalar.activation(dst, src, ACT.Copy), 1)


_INS = ["x", "ctx_2048", "mask_S_fk1", "mask_S_fk0"]
for _p in range(2):
    _INS += [f"L{2 * _p}_xattn_{_w}" for _w in ("Wq", "Wk", "Wv", "Wo", "bo", "token_indices_A", "token_indices_B")]
    _INS += [f"L{2 * _p + 1}_xattn_{_w}" for _w in ("wq", "wk", "wv", "wo", "norm_w")]


def build(nc, ins, out):
    dr = scratch_tensors(nc)
    prepare(nc, ins, dr)
    run_layers(nc, ins, dr)
    store_outputs(nc, dr, out)


def kernel(**inputs):
    import numpy as _np
    import concourse.bacc as _bacc
    from concourse import mybir as _mybir
    from concourse.bass_utils import run_bass_kernel_spmd as _run

    nc = _bacc.Bacc("TRN2", target_bir_lowering=False, num_devices=1)
    arrays, ins = {}, {}
    for name in _INS:
        a = _np.ascontiguousarray(inputs[name])
        arrays[f"in_{name}_dram"] = a
        ins[name] = nc.dram_tensor(f"in_{name}_dram", a.shape, _mybir.dt.from_np(a.dtype), kind="ExternalInput").ap()
    out = nc.dram_tensor("out_0_dram", (B, S, C), _mybir.dt.float32, kind="ExternalOutput").ap()
    build(nc, ins, out)
    r = _run(nc, [arrays], core_ids=[0])
    return r.results[0]["out_0_dram"]
```

```python
from contextlib import ExitStack

import concourse.bass as bass
from concourse import mybir

F32 = mybir.dt.float32
F32R = mybir.dt.float32r
BF16 = mybir.dt.bfloat16
I32 = mybir.dt.int32
ALU = mybir.AluOpType
ACT = mybir.ActivationFunctionType
AX_X = mybir.AxisListType.X

P = 128
B, S, C = 4, 1024, 256
KEYS, CT = 154, 512
REST = KEYS - P
H = 16
DW, DN = 64, 16
KVN = 4
TOK = 512
KC, KCT = C // P, CT // P
ALLK = B * KEYS
WI = H * DW
EPS = 1e-5
SUPPRESS = 20.0
ROW_M = 32
WSTEPS, STEPS = 8, 16


def split3(lhs_hi, lhs_lo, rhs_hi, rhs_lo):
    return ((lhs_hi, rhs_hi), (lhs_hi, rhs_lo), (lhs_lo, rhs_hi))


def scratch_tensors(nc):
    def d(name, shape, dt):
        return nc.dram_tensor("scratch_" + name, shape, dt).ap()

    return dict(
        stream=d("stream", (B, 2, P, KC, TOK), F32),
        maskrows=d("maskrows", (2, 6, TOK), BF16),
        keyrows=d("keyrows", (2, 6, KEYS), BF16),
        wq_hi=d("wq_hi", (2, P, KC, WI), F32), wq_lo=d("wq_lo", (2, P, KC, WI), F32),
        wo_hi=d("wo_hi", (2, P, H // 2, C), F32), wo_lo=d("wo_lo", (2, P, H // 2, C), F32),
        nq_hi=d("nq_hi", (2, P, KC, C), F32), nq_lo=d("nq_lo", (2, P, KC, C), F32),
        no_hi=d("no_hi", (2, P, KC, C), F32), no_lo=d("no_lo", (2, P, KC, C), F32),
        wk_hi=d("wk_hi", (2, P, H // 2, ALLK), F32),
        wk_lob=d("wk_lob", (2, P, H // 2, ALLK), BF16), wk_hib=d("wk_hib", (2, P, H // 2, ALLK), BF16),
        nk_hi=d("nk_hi", (2, KVN * DN, ALLK), F32),
        nk_lob=d("nk_lob", (2, KVN * DN, ALLK), BF16), nk_hib=d("nk_hib", (2, KVN * DN, ALLK), BF16),
        wv=d("wv", (2, B, P, WI), F32), wv_rest=d("wv_rest", (2, B * REST, WI), F32),
        nv=d("nv", (2, B, P, KVN, 32), F32), nv_rest=d("nv_rest", (2, B * REST, KVN, 32), F32),
        sums=d("sums", (P, TOK), F32),
    )


def prepare(nc, ins, dr):
    ctx = ExitStack()
    with ctx:
        def sb(name, shape, dt=F32):
            return ctx.enter_context(nc.sbuf_tensor(name, shape, dt))

        def sem(name):
            return ctx.enter_context(nc.semaphore(name))

        ident = sb("p_ident", [P, P])
        tokens_in = sb("p_tokens_in", [P, 2, 4, C])
        tokens_t = sb("p_tokens_t", [P, 2, KC, TOK])
        ctx_in = sb("p_ctx_in", [P, 5, CT])
        ctx_hi = sb("p_ctx_hi", [P, KCT, ALLK], F32R)
        ctx_lo = sb("p_ctx_lo", [P, KCT, ALLK], F32R)
        SETS, OUTS = 4, 4
        raw = sb("p_raw", [P, SETS * 2048])
        hi = sb("p_hi", [P, SETS * 2048], F32R)
        lo = sb("p_lo", [P, SETS * 2048], F32R)
        normw = sb("p_normw", [P, KC])
        kout_hi = sb("p_kout_hi", [P, OUTS, ALLK], F32R)
        kout_hib = sb("p_kout_hib", [P, OUTS, ALLK], BF16)
        kout_lob = sb("p_kout_lob", [P, OUTS, ALLK], BF16)
        vout = sb("p_vout", [P, OUTS, 512])
        nvout = sb("p_nvout", [P, OUTS, KVN, 32])
        idx = sb("p_idx", [1, 8], I32)
        idxf = sb("p_idxf", [1, 3, 8])
        keyno = sb("p_keyno", [1, KEYS], I32)
        keynof = sb("p_keynof", [1, KEYS])
        onehot = sb("p_onehot", [1, 5, KEYS])
        keyrow = sb("p_keyrow", [1, 2, 6, KEYS], BF16)
        mrow = sb("p_mrow", [1, 2, S])
        mtmp = sb("p_mtmp", [1, 2, S])
        mpart = sb("p_mpart", [1, 2, 3, S], BF16)
        ps = ctx.enter_context(nc.psum_tensor("p_ps", [P, 8, 512], F32))

        s_ident = sem("p_ident_ready")
        s_x = [sem(f"p_tokens_loaded{i}") for i in range(2)]
        s_xt = sem("p_tokens_transposed")
        s_xc = sem("p_tokens_copied")
        s_xs = [sem(f"p_tokens_stored{i}") for i in range(2)]
        s_c = sem("p_context_loaded")
        s_ct = sem("p_context_transposed")
        s_cs = sem("p_context_split")
        s_w = [sem(f"p_weights_loaded{i}") for i in range(SETS)]
        s_nw = sem("p_norm_weights_loaded")
        s_hi = sem("p_weights_hi")
        s_lo = sem("p_weights_lo")
        s_wst = [sem(f"p_weights_stored{i}") for i in range(4)]
        s_mm = sem("p_product_made")
        s_ev = sem("p_product_taken")
        s_evh = sem("p_hi_taken")
        s_st = [sem(f"p_product_stored{i}") for i in range(OUTS)]
        s_ones = sem("p_ones_ready")
        s_small = sem("p_small_loaded")
        s_rows = sem("p_rows_chain")
        s_rowst = sem("p_rows_stored")
        s_pool = sem("p_pool_chain")

        block = ctx.enter_context(nc.Block())
        NX = 2 * B

        def weight_pieces(p):
            wq, wk, wv, wo = ins[f"L{2 * p}_xattn_Wq"], ins[f"L{2 * p}_xattn_Wk"], ins[f"L{2 * p}_xattn_Wv"], ins[f"L{2 * p}_xattn_Wo"]
            nq, nk, nv, no = (ins[f"L{2 * p + 1}_xattn_{w}"] for w in ("wq", "wk", "wv", "wo"))
            r = lambda w: w.rearrange("(k p) n -> p k n", p=P)
            return [("wk0", r(wk)[:, :, 0:512], None),
                    ("wq", r(wq), (dr["wq_hi"][p], dr["wq_lo"][p])),
                    ("wk1", r(wk)[:, :, 512:1024], None), ("nk", r(nk), None),
                    ("wo", r(wo), (dr["wo_hi"][p], dr["wo_lo"][p])),
                    ("wv0", r(wv)[:, :, 0:512], None), ("nv", r(nv), None),
                    ("nq", r(nq), (dr["nq_hi"][p], dr["nq_lo"][p])),
                    ("wv1", r(wv)[:, :, 512:1024], None),
                    ("no", r(no), (dr["no_hi"][p], dr["no_lo"][p]))]

        pieces = [(p, *x) for p in range(2) for x in weight_pieces(p)]
        used = lambda i: pieces[i][3] is None

        def view(buf, i):
            k, n = pieces[i][2].shape[1:]
            return buf[:, (i % SETS) * 2048:(i % SETS) * 2048 + k * n].rearrange("p (k n) -> p k n", k=k)

        jobs = []
        for i, (p, name, src, st) in enumerate(pieces):
            if name in ("wk0", "wk1"):
                jobs += [(i, "k", 4 * int(name[2]) + m) for m in range(4)]
            elif name == "nk":
                jobs += [(i, "nk", 0)]
            elif name in ("wv0", "wv1"):
                jobs += [(i, "v", (int(name[2]), t)) for t in range(B + 1)]
            elif name == "nv":
                jobs += [(i, "nv", t) for t in range(B + 1)]
        last_job = {i: max(n for n, j in enumerate(jobs) if j[0] == i) for i in range(len(pieces)) if used(i)}

        def wait_piece_free(eng, i):
            j = i - SETS
            if j < 0:
                return
            if used(j):
                eng.wait_ge(s_mm, last_job[j] + 1)
            else:
                stored = sum(not used(k) for k in range(j))
                eng.wait_ge(s_wst[stored % 4], 32 * (stored // 4 + 1))

        def store_job(sp, n):
            i, kind, what = jobs[n]
            p, stored = pieces[i][0], s_st[n % OUTS]
            sp.wait_ge(s_ev, n + 1)
            if kind in ("k", "nk"):
                m = P if kind == "k" else KVN * DN
                for name, buf in (("hi", kout_hi), ("hib", kout_hib), ("lob", kout_lob)):
                    to = dr["wk_" + name][p, :, what, :] if kind == "k" else dr["nk_" + name][p]
                    of = buf[0:m, n % OUTS, :]
                    sp.dma_start(to, of.bitcast(F32) if name == "hi" else of).then_inc(stored, 16)
            elif kind == "v":
                half, t = what
                cols = slice(half * 512, half * 512 + 512)
                to = dr["wv"][p, t, :, cols] if t < B else dr["wv_rest"][p, :, cols]
                sp.dma_start(to, vout[0:P if t < B else B * REST, n % OUTS, :]).then_inc(stored, 48)
            else:
                to = dr["nv"][p, what] if what < B else dr["nv_rest"][p]
                sp.dma_start(to, nvout[0:P if what < B else B * REST, n % OUTS]).then_inc(stored, 48)

        rows_ready = []

        @block.vector
        def _(dve):
            for k in range(KCT):
                dve.wait_ge(s_ct, k + 1)
                for half, (a, z) in enumerate(((0, 512), (512, ALLK))):
                    bank = (k % 2) * 2 + half
                    nc.vector.tensor_copy(ctx_hi[:, k, a:z], ps[:, bank, 0:z - a]).then_inc(s_cs, 1)
                dve.wait_ge(s_cs, 4 * k + 2)
                for half, (a, z) in enumerate(((0, 512), (512, ALLK))):
                    bank = (k % 2) * 2 + half
                    nc.vector.tensor_tensor(ctx_lo[:, k, a:z], ps[:, bank, 0:z - a], ctx_hi[:, k, a:z], ALU.subtract).then_inc(s_cs, 1)
            def take_stream(x):
                dve.wait_ge(s_xt, x + 1)
                if x >= 2:
                    dve.wait_ge(s_xs[x % 2], 16 * (x // 2))
                for k in range(KC):
                    nc.vector.tensor_copy(tokens_t[:, x % 2, k, :], ps[:, 6 + k, :]).then_inc(s_xc, 1)

            chain = [0]

            def link(instruction):
                chain[0] += 1
                instruction.then_inc(s_rows, 1)
                dve.wait_ge(s_rows, chain[0])

            def make_rows():
                dve.wait_ge(s_small, 16 * 6)
                link(nc.vector.tensor_scalar(mtmp[:], mrow[:], -1.0, 1.0, ALU.mult, ALU.add))
                link(nc.vector.tensor_scalar(mrow[:], mtmp[:], -SUPPRESS * DW ** 0.5, None, ALU.mult))
                for part in range(3):
                    link(nc.vector.tensor_copy(mpart[:, :, part], mrow[:]))
                    if part < 2:
                        link(nc.vector.tensor_tensor(mrow[:], mrow[:], mpart[:, :, part], ALU.subtract))
                dve.wait_ge(s_ones, 1)
                link(nc.vector.tensor_copy(keynof[:], keyno[:]))
                link(nc.vector.tensor_copy(idxf[:, 0, :], idx[:]))
                link(nc.vector.tensor_scalar(idxf[:, 1, :], idxf[:, 0, :], 0.0, float(KEYS), ALU.is_lt, ALU.mult))
                link(nc.vector.tensor_tensor(idxf[:, 2, :], idxf[:, 0, :], idxf[:, 1, :], ALU.add))
                for p in range(2):
                    for j in range(4):
                        link(nc.vector.tensor_scalar(onehot[:, j, :], keynof[:], idxf[:, 2, 4 * p + j:4 * p + j + 1], None, ALU.is_equal))
                    link(nc.vector.tensor_tensor(onehot[:, 0, :], onehot[:, 0, :], onehot[:, 1, :], ALU.max))
                    link(nc.vector.tensor_tensor(onehot[:, 2, :], onehot[:, 2, :], onehot[:, 3, :], ALU.max))
                    link(nc.vector.tensor_scalar(onehot[:, 4, :], onehot[:, 2, :], -1.0, 1.0, ALU.mult, ALU.add))
                    link(nc.vector.tensor_tensor(onehot[:, 1, :], onehot[:, 0, :], onehot[:, 4, :], ALU.mult))
                    for r in range(6):
                        link(nc.vector.tensor_copy(keyrow[:, p, r, :], onehot[:, 1 if r < 3 else 2, :]))
                rows_ready.append(chain[0])

            def take_product(n, i, kind, what):
                dve.wait_ge(s_mm, n + 1)
                if n >= OUTS:
                    dve.wait_ge(s_st[n % OUTS], 48 * (n // OUTS))
                bank = 2 * (n % 3)
                if kind in ("k", "nk"):
                    m = P if kind == "k" else KVN * DN
                    parts = [(ps[0:m, bank + half, 0:z - a], a, z) for half, (a, z) in enumerate(((0, 512), (512, ALLK)))]
                    for src, a, z in parts:
                        nc.vector.tensor_copy(kout_hi[0:m, n % OUTS, a:z], src)
                        last = nc.vector.tensor_copy(kout_hib[0:m, n % OUTS, a:z], src)
                    link(last)
                    for src, a, z in parts:
                        last = nc.vector.tensor_tensor(kout_lob[0:m, n % OUTS, a:z], src, kout_hi[0:m, n % OUTS, a:z], ALU.subtract)
                elif kind == "v":
                    m = P if what[1] < B else B * REST
                    last = nc.vector.tensor_copy(vout[0:m, n % OUTS, :], ps[0:m, bank, :])
                else:
                    dve.wait_ge(s_ones, 1)
                    m = P if what < B else B * REST
                    last = nc.vector.tensor_copy(nvout[0:m, n % OUTS, :, 0:DN], ps[0:m, bank, 0:KVN * DN].rearrange("p (g d) -> p g d", g=KVN))
                last.then_inc(s_ev, 1)

            for i in range(len(pieces)):
                if i < NX:
                    take_stream(i)
                for n, job in enumerate(jobs):
                    if job[0] == i:
                        take_product(n, *job)
                if i == 4:
                    make_rows()

        @block.sync
        def _(sp):
            def load_piece(i):
                if i >= SETS:
                    sp.wait_ge(s_lo, i - SETS + 1)
                p, name, src, st = pieces[i]
                sp.dma_start(view(raw, i), src).then_inc(s_w[i % SETS], 16)
                if name == "nq":
                    if p:
                        sp.wait_ge(s_hi, len(pieces) // 2)
                    sp.dma_start(normw[:, :], ins[f"L{2 * p + 1}_xattn_norm_w"].rearrange("(k p) -> p k", p=P)).then_inc(s_nw, 16)

            with nc.allow_non_contiguous_dma(reason="columns of norm weights"):
                sp.dma_start(ctx_in[:, 0:B, :], ins["ctx_2048"][:, 0:P].rearrange("b p d -> p b d")).then_inc(s_c, 16)
                for b in range(B):
                    sp.dma_start(ctx_in[b * REST:(b + 1) * REST, B, :], ins["ctx_2048"][b, P:KEYS]).then_inc(s_c, 16)
                def load_stream(x):
                    if x >= 2:
                        sp.wait_ge(s_xt, x - 1)
                    sp.dma_start(tokens_in[:, x % 2], ins["x"].rearrange("b (c t p) d -> (b c) p t d", t=4, p=P)[x]).then_inc(s_x[x % 2], 16)

                load_piece(0)
                load_stream(0)
                load_piece(1)
                for i in range(2, SETS):
                    load_piece(i)
                load_stream(1)
                for a, name in enumerate(("mask_S_fk1", "mask_S_fk0")):
                    sp.dma_start(mrow[:, a, :], ins[name].rearrange("(a n) -> a n", a=1)).then_inc(s_small, 16)
                for p in range(2):
                    for a, name in enumerate("AB"):
                        at = 4 * p + 2 * a
                        sp.dma_start(idx[:, at:at + 2], ins[f"L{2 * p}_xattn_token_indices_{name}"].rearrange("(a n) -> a n", a=1)).then_inc(s_small, 16)
                for i in range(len(pieces)):
                    if i + SETS < len(pieces):
                        load_piece(i + SETS)
                    if i < NX:
                        if i + 2 < NX:
                            load_stream(i + 2)
                        sp.wait_ge(s_xc, KC * (i + 1))
                        sp.dma_start(dr["stream"][i // 2, i % 2], tokens_t[:, i % 2]).then_inc(s_xs[i % 2], 16)
                    for n, j in enumerate(jobs):
                        if j[0] == i:
                            store_job(sp, n)
                sp.wait_ge(s_rows, rows_ready[0])
                for t in range(2):
                    sp.dma_start(dr["maskrows"][t:t + 1].rearrange("o (a r) n -> o a r n", a=2),
                                 mpart[:, :, :, t * TOK:(t + 1) * TOK]).then_inc(s_rowst, 16)
                sp.dma_start(dr["keyrows"].rearrange("(o p) r n -> o p r n", o=1), keyrow[:]).then_inc(s_rowst, 16)
                sp.wait_ge(s_rowst, 48)
                for h in range(2):
                    sp.wait_ge(s_xs[h], 16 * (NX // 2))
                for h in range(OUTS):
                    sp.wait_ge(s_st[h], 48 * len(range(h, len(jobs), OUTS)))

        @block.scalar
        def _(act):
            for i, (p, name, src, st) in enumerate(pieces):
                act.wait_ge(s_w[i % SETS], 16 * (i // SETS + 1))
                wait_piece_free(act, i)
                if name == "nq":
                    act.wait_ge(s_nw, 16 * (p + 1))
                    for k in range(KC):
                        nc.scalar.activation(view(raw, i)[:, k], view(raw, i)[:, k], ACT.Copy,
                                             scale=normw[:, k:k + 1]).then_inc(s_evh, 1)
                    act.wait_ge(s_evh, KC * (p + 1))
                nc.scalar.activation(view(hi, i), view(raw, i), ACT.Copy).then_inc(s_hi, 1)
                if st is not None:
                    act.wait_ge(s_lo, i + 1)
                    stored = s_wst[sum(not used(k) for k in range(i)) % 4]
                    act.dma_start(st[0], view(hi, i).bitcast(F32)).then_inc(stored, 16)
                    act.dma_start(st[1], view(lo, i).bitcast(F32)).then_inc(stored, 16)
            for k in range(4):
                act.wait_ge(s_wst[k], 32 * 2)

        @block.gpsimd
        def _(pool):
            nc.gpsimd.memset(ident[:], 0.0).then_inc(s_pool, 1)
            pool.wait_ge(s_pool, 1)
            nc.gpsimd.affine_select(out=ident[:], in_=ident[:], compare_op=ALU.not_equal, fill=1.0, base=0,
                                    pattern=[[-1, P]], channel_multiplier=1).then_inc(s_ident, 1)
            nc.gpsimd.memset(nvout[:], 0.0).then_inc(s_pool, 1)
            pool.wait_ge(s_pool, 2)
            for u in range(KVN):
                nc.gpsimd.memset(nvout[:, :, u, DN + 4 * u:DN + 4 * u + 4], 1.0)
            nc.gpsimd.iota(keyno[:], pattern=[[1, KEYS]], base=0, channel_multiplier=0).then_inc(s_ones, 1)
            for i, (p, name, src, st) in enumerate(pieces):
                pool.wait_ge(s_hi, i + 1)
                wait_piece_free(pool, i)
                nc.gpsimd.tensor_tensor(view(lo, i), view(raw, i), view(hi, i), ALU.subtract).then_inc(s_lo, 1)

        @block.tensor
        def _(pe):
            pe.wait_ge(s_ident, 1)
            pe.wait_ge(s_c, 16 * (B + 1))
            for k in range(KCT):
                if k >= 1:
                    pe.wait_ge(s_cs, 4 * k)
                for t in range(5):
                    n = P if t < 4 else ALLK - 512
                    bank, col = (k % 2) * 2 + (t // 4), (t % 4) * P
                    last = nc.tensor.transpose(ps[:, bank, col:col + n], ctx_in[0:n, t, k * P:(k + 1) * P], ident[0:n, 0:n])
                last.then_inc(s_ct, 1)
            def turn_stream(x):
                pe.wait_ge(s_x[x % 2], 16 * (x // 2 + 1))
                if x:
                    pe.wait_ge(s_xc, KC * x)
                for k in range(KC):
                    for t in range(4):
                        last = nc.tensor.transpose(ps[:, 6 + k, t * P:(t + 1) * P], tokens_in[:, x % 2, t, k * P:(k + 1) * P], ident[:])
                last.then_inc(s_xt, 1)

            def make_product(n, i, kind, what):
                pe.wait_ge(s_lo, i + 1)
                if n >= 3:
                    pe.wait_ge(s_ev, n - 2)
                bank = 2 * (n % 3)
                wh, wl = view(hi, i), view(lo, i)
                if kind in ("k", "nk"):
                    cols = slice((what % 4) * P, (what % 4) * P + P) if kind == "k" else slice(0, KVN * DN)
                    m = P if kind == "k" else KVN * DN
                    for half, (a, z) in enumerate(((0, 512), (512, ALLK))):
                        pairs = [q for k in range(KCT) for q in split3(wh[:, k, cols], wl[:, k, cols], ctx_hi[:, k, a:z], ctx_lo[:, k, a:z])]
                        for j, (l, r) in enumerate(pairs):
                            last = nc.tensor.matmul(ps[0:m, bank + half, 0:z - a], l, r, start=(j == 0), stop=(j == len(pairs) - 1))
                else:
                    t = what[1] if kind == "v" else what
                    n_cols = 512 if kind == "v" else KVN * DN
                    m = P if t < B else B * REST

                    def tok(c, k):
                        return c[:, k, t * P:t * P + m]

                    pairs = [q for k in range(KCT) for q in split3(tok(ctx_hi, k), tok(ctx_lo, k), wh[:, k, :], wl[:, k, :])]
                    for j, (l, r) in enumerate(pairs):
                        last = nc.tensor.matmul(ps[0:m, bank, 0:n_cols], l, r, start=(j == 0), stop=(j == len(pairs) - 1))
                last.then_inc(s_mm, 1)

            pe.wait_ge(s_cs, 4 * KCT)
            for i in range(len(pieces)):
                if i < NX:
                    turn_stream(i)
                for n, job in enumerate(jobs):
                    if job[0] == i:
                        make_product(n, *job)


GB = 3
OUT_BATCHES = (4, 4, 2, 2)
KEPT = 10
PLACES = ((0, 1, 2, 3, 4, 5, 6, 7), (8, 9, 0, 1, 2, 3, 4, 5), (6, 7, 8, 9), (4, 5, 6, 7))
ITER = 2 * B
TINY = 1e-37
NARROW_KEYS_AT, WIDE_KEYS_AT = (2, 3, 4, 7), (12, 13, 14, 15)


def wide(n):
    return n < WSTEPS


def half_of(n):
    return (n // 4) % 2


def slot(n):
    return n % 2 if wide(n) else ((n - WSTEPS) // 2) % 2


def first_tile(n):
    return 2 * n if wide(n) else 2 * WSTEPS + (n - WSTEPS)


def chunk_tile(c, k):
    return first_tile(4 * c) + k


def chunk_of(tile):
    c = max(c for c in range(4) if chunk_tile(c, 0) <= tile)
    return c, tile - chunk_tile(c, 0)


def place(tile):
    c, k = chunk_of(tile)
    return PLACES[c][k]


def last_in_place(tile):
    for back in range(1, 25):
        old, ago = (tile - back) % 24, int(tile - back < 0)
        if place(old) == place(tile):
            return old, ago


ORDER = """
    rest 0, max 1 2, max 1 3, inverse 3-, query 1 1, score 0 0, score 0 1, max 1 4, scale 3- 0, max 1 5,
        max 1 6, score 0 2, max 1 7, score 0 3, query 2 0, turn 1, norm 3- 0, value 0 0, low 3- 0,
        value 0 1, max 2 0, max 2 1,
    rest 1, scale 3- 1, max 2 2, max 2 3, query 2 1, score 1 0, score 1 1, output 3- 0, norm 3- 1, max 2 4,
        max 2 5, max 2 6, score 1 2, max 2 7, value 1 0, low 3- 1, score 1 3, output 3- 1, query 3 0,
        turn 2, value 1 1, max 3 0, max 3 1,
    rest 2, max 3 2, max 3 3, query 3 1, score 2 0, score 2 1, split 1, max 3 4, score 2 2, max 3 5,
        value 2 0, max 3 6, max 3 7, score 2 3, query 4 0, turn 3, value 2 1, max 4 0, max 4 1,
    rest 3, max 4 2, max 4 3, query 4 1, score 3 0, score 3 1, max 4 4, max 4 5, value 3 0, max 4 6,
        score 3 2, max 4 7, score 3 3, query 5 0, turn 4, value 3 1, max 5 0, max 5 1, invert 0, max 5 2,
        inverse 0,
    rest 4, max 5 3, query 5 1, score 4 0, max 5 4, score 4 1, max 5 5, value 4 0, max 5 6, score 4 2,
        max 5 7, score 4 3, query 6 0, turn 5, value 4 1, scale 0 0, norm 0 0, max 6 0, max 6 1,
    rest 5, low 0 0, max 6 2, scale 0 1, max 6 3, query 6 1, score 5 0, score 5 1, output 0 0, norm 0 1,
        max 6 4, max 6 5, score 5 2, value 5 0, low 0 1, max 6 6, max 6 7, score 5 3, output 0 1, scale 0 2,
        norm 0 2, query 7 0, turn 6, value 5 1, low 0 2, max 7 0, max 7 1,
    rest 6, max 7 2, max 7 3, query 7 1, score 6 0, score 6 1, output 0 2, score 6 2, scale 0 3, norm 0 3,
        max 7 4, max 7 5, value 6 0, low 0 3, max 7 6, max 7 7, score 6 3, turn 7, output 0 3, squares 2,
        value 6 1, square 2,
    rest 7, score 7 0, score 7 1, rate 2, value 7 0, query 8 0, score 7 2, max 8 0, score 7 3, max 8 1,
        max 8 2, max 8 3, max 8 4, max 8 5, max 8 6, max 8 7, value 7 1, max 9 0, turn 8, max 9 1, invert 1,
    rest 8, inverse 1, max 9 2, max 9 3, score 8 0, score 8 1, max 9 4, max 9 5, score 8 2, max 9 6,
        score 8 3, max 9 7, scale 1 0, query 10 0, turn 9, value 8 1,
    rest 9, max 10 0, max 10 1, max 10 2, max 10 3, score 9 0, max 10 4, score 9 1, max 10 5, max 10 6,
        max 10 7, score 9 2, low 1 0, norm 1 0, score 9 3, scale 1 1, turn 10, value 9 1, output 1 0, add 9,
        max 11 0,
    rest 10, max 11 1, max 11 2, score 10 0, max 11 3, max 11 4, max 11 5, norm 1 1, score 10 1, max 11 6,
        scale 1 2, score 10 2, low 1 1, max 11 7, output 1 1, score 10 3, norm 1 2, value 10 1, scale 1 3,
        low 1 2, turn 11, output 1 2, add 10,
    rest 11, score 11 0, score 11 1, norm 1 3, score 11 2, low 1 3, score 11 3, output 1 3, squares 3,
        value 11 1, square 3, rate 3, add 11, query 12 0, max 12 0, max 12 1, max 12 2, max 12 3, max 12 4,
        max 12 5, max 12 6, max 12 7, turn 12, max 13 0, guard 2, invert 2, max 13 1,
    rest 12, max 13 2, max 13 3, score 12 0, inverse 2, score 12 1, max 13 4, max 13 5, max 13 6,
        score 12 2, max 13 7, score 12 3, query 14 0, turn 13, scale 2 0, max 14 0, max 14 1, value 12 1,
    rest 13, max 14 2, max 14 3, split 0+, score 13 0, score 13 1, max 14 4, norm 2 0, max 14 5, low 2 0,
        max 14 6, score 13 2, max 14 7, score 13 3, output 2 0, turn 14, scale 2 1, add 13, max 15 0,
        norm 2 1, value 13 1, max 15 1, max 15 2,
    rest 14, max 15 3, score 14 0, max 15 4, max 15 5, low 2 1, score 14 1, max 15 6, score 14 2, max 15 7,
        score 14 3, output 2 1, turn 15, query 0+ 0, value 14 1, add 14, max 0+ 0,
    rest 15, max 0+ 1, max 0+ 2, max 0+ 3, query 0+ 1, score 15 0, score 15 1, score 15 2, max 0+ 4,
        max 0+ 5, max 0+ 6, max 0+ 7, score 15 3, turn 0+, value 15 1, query 1+ 0, max 1+ 0, add 15,
        max 1+ 1, guard 3, invert 3
"""


def window():
    order = []
    for entry in ORDER.replace("\n", " ").split(","):
        what, n, k = (entry.split() + ["0"])[:3]
        turn = {"+": 1, "-": -1}.get(n[-1], 0)
        order.append((what, int(n.rstrip("+-")), int(k), turn))
    return order


WINDOW = window()


def present(it, turn):
    return not isinstance(it, int) or 0 <= it + turn < ITER


class Signal:

    def __init__(self, sem, kinds, times=1):
        self.sem, self.times = sem, times
        mine = [x for x in WINDOW if x[0] in kinds]
        mine = [x for t in (1, 0, -1) for x in mine if x[3] == t]
        self.number = {x[:3]: i + 1 for i, x in enumerate(mine)}
        self.per = len(self.number) * times

    def after(self, it, *key):
        return it * self.per + self.number[key] * self.times

    def before(self, it, number):
        return it * self.per + max(number, 0) * self.times


def wait(eng, sem, value):
    if not isinstance(value, int) or value > 0:
        eng.wait_ge(sem, value)


GENERAL = [(*x, m) for x in WINDOW if x[0] in ("query", "max", "turn", "output", "square", "rate")
           for m in range(KC if x[0] == "output" else 1)]
assert len(GENERAL) % GB == 0
BANK = {(*use[:3], use[4]): i % GB for i, use in enumerate(GENERAL)}


def run_layers(nc, ins, dr):
    ctx = ExitStack()
    with ctx:
        def sb(name, shape, dt=F32):
            return ctx.enter_context(nc.sbuf_tensor(name, shape, dt))

        def sem(name):
            return ctx.enter_context(nc.semaphore(name))

        def signal(name, *kinds, times=1):
            return Signal(sem(name), kinds, times)

        x = sb("x", [P, 2, KC, TOK])
        wq = [sb(f"wq_{a}", [P, KC, WI], F32R) for a in ("hi", "lo")]
        wo = [sb(f"wo_{a}", [P, H // 2, C], F32R) for a in ("hi", "lo")]
        nq = [sb(f"nq_{a}", [P, KC, C], F32R) for a in ("hi", "lo")]
        no = [sb(f"no_{a}", [P, KVN, C], F32R) for a in ("hi", "lo")]
        bias = sb("bias", [P, KC])
        w_pair, n_pair = (sb(a + "_pair", [P, H, P], F32R) for a in "wn")
        w_aux, n_aux = (sb(a + "_aux", [P, H, P], BF16) for a in "wn")
        w_top, n_top = (sb(a + "_top", [P, H, KEYS], BF16) for a in "wn")
        w_pair_rest, w_aux_rest = sb("w_pair_rest", [P, H, P], F32R), sb("w_aux_rest", [P, H, P], BF16)
        n_pair_rest, n_aux_rest = sb("n_pair_rest", [P, KVN, P], F32R), sb("n_aux_rest", [P, KVN, P], BF16)
        w_val, w_val_rest = sb("w_val", [P, WI]), sb("w_val_rest", [P, WI])
        n_val, n_val_rest = sb("n_val", [P, KVN, 32]), sb("n_val_rest", [P, KVN, P])
        x_hi, x_lo = sb("x_hi", [P, KC, TOK], F32R), sb("x_lo", [P, KC, TOK], F32R)
        xn = sb("xn", [P, KC, TOK])
        q_pair = sb("q_pair", [P, 2, 4, TOK], F32R)
        q_aux = sb("q_aux", [P, 2, 2, 4, TOK], BF16)
        probs = sb("probs", [P, 4, TOK])
        probs_rest = sb("probs_rest", [P, 2, TOK])
        kept = sb("kept", [P, KEPT, TOK])
        total = sb("total", [P, TOK])
        inv = sb("inv", [P, TOK])
        inv_b = sb("inv_b", [P, 2, TOK])
        a_hi, a_lo = sb("a_hi", [P, 2, TOK], F32R), sb("a_lo", [P, 2, TOK], F32R)
        tops = sb("tops", [P, 4, 4], BF16)
        meansq, rate, power = sb("meansq", [P, 4]), sb("rate", [P, 4]), sb("power", [P, 4])
        ident, ident_bf, ones = sb("ident", [P, P]), sb("ident_bf", [P, P], BF16), sb("ones", [P, 1])
        sel, sel_rest = sb("sel", [P, 4, 32]), sb("sel_rest", [P, 4, P])

        general = ctx.enter_context(nc.psum_tensor("general", [P, GB, 512], F32))
        score_ps = ctx.enter_context(nc.psum_tensor("score_ps", [P, 2, 512], F32))
        out_ps = ctx.enter_context(nc.psum_tensor("out_ps", [P, 2, 512], F32))
        sum_ps = ctx.enter_context(nc.psum_tensor("sum_ps", [P, 512], F32))

        ROWS_CLEARED, CLEARED = 6, 11
        WIDE_QUERY, WIDE, WIDE_OUT, NARROW = 16 * 2, 16 * 9, 16 * 2, 16 * 18
        WTOPS, WKEYS, NKEYS = 16 * 4, 16 * 23, 16 * 53

        cleared = sem("cleared")
        rows_cleared = sem("rows_cleared")
        filled, rows_filled = sem("filled"), sem("rows_filled")
        ident_ready = sem("ident_ready")
        masks_loaded = sem("masks_loaded")
        wide_query_loaded, wide_loaded, wide_out_loaded = sem("wide_query_loaded"), sem("wide_loaded"), sem("wide_out_loaded")
        narrow_loaded = sem("narrow_loaded")
        wtops_loaded, wkeys_loaded, nkeys_loaded = sem("wtops_loaded"), sem("wkeys_loaded"), sem("nkeys_loaded")
        early_loaded = signal("early_loaded", "split", times=16)
        x_loaded, x_stored = [sem(f"x_loaded{t}") for t in range(2)], [sem(f"x_stored{t}") for t in range(2)]
        sums_stored, inv_loaded = signal("sums_stored", "inverse", times=16), signal("inv_loaded", "scale", times=64)
        pe_query, pe_max, pe_turn = signal("pe_query", "query"), signal("pe_max", "max"), signal("pe_turn", "turn")
        pe_score, pe_value = signal("pe_score", "rest", "score"), signal("pe_value", "value")
        pe_output, pe_square, pe_rate = signal("pe_output", "output", times=KC), signal("pe_square", "square"), signal("pe_rate", "rate")
        act_split, act_query, act_exp = signal("act_split", "split", "rate"), signal("act_query", "query"), signal("act_exp", "rest", "score")
        act_turn, act_keep, act_norm = signal("act_turn", "turn"), signal("act_keep", "value"), signal("act_norm", "norm")
        act_square = signal("act_square", "squares")
        dve_aux, dve_query = signal("dve_aux", "query"), signal("dve_query", "query")
        dve_guard = signal("dve_guard", "guard")
        dve_max, dve_invert = signal("dve_max", "max"), signal("dve_invert", "invert", "inverse")
        dve_output = signal("dve_output", "output", times=KC)
        dve_square, dve_rate = signal("dve_square", "square"), signal("dve_rate", "rate")
        pool_split, pool_rate = signal("pool_split", "split", "rate"), signal("pool_rate", "square")
        pool_scale, dve_low = signal("pool_scale", "scale"), signal("dve_low", "low")
        pool_add = signal("pool_add", "add")
        reader = {"query": dve_query, "max": dve_max, "turn": act_turn, "output": dve_output,
                  "square": dve_square, "rate": dve_rate}

        block = ctx.enter_context(nc.Block())

        def each_batch(eng, do):
            def one_turn(it):
                loop = not isinstance(it, int)
                batch = {turn: eng.snap(it + turn) if loop else it + turn for turn in (-1, 0, 1)}
                for what, n, k, turn in WINDOW:
                    if present(it, turn):
                        do(batch[turn], what, n, k)

            one_turn(-1)
            one_turn(0)
            with eng.Fori(1, ITER - 1) as it:
                one_turn(it)
            one_turn(ITER - 1)
            one_turn(ITER)

        def bank_of(use):
            return general[:, BANK[use], :]

        @block.sync
        def _(sp):
            def load_wide(p):
                for i, a in enumerate(("hi", "lo")):
                    sp.dma_start(wq[i][:].bitcast(F32), dr["wq_" + a][p]).then_inc(wide_query_loaded, 16)
                sp.dma_start(bias[:], ins[f"L{2 * p}_xattn_bo"].rearrange("(k p) -> p k", p=P),
                             allow_slow_non_contiguous=True).then_inc(wide_loaded, 16)
                if p == 0:
                    sp.wait_ge(rows_cleared, ROWS_CLEARED)
                    load_masks()
                    load_wide_keys(0, 0, 0)
                for par in range(2):
                    a = 64 * (1 - par)
                    def every(buf):
                        return buf[a:a + 6].rearrange("p (h two) k -> p h two k", two=2)[:, :, par, :]
                    rows = dr["keyrows"][p]
                    sp.dma_start(every(w_aux), rows[:, None, 0:P].to_broadcast([6, 8, P])).then_inc(wide_loaded, 16)
                    sp.dma_start(every(w_top), rows[:, None, :].to_broadcast([6, 8, KEYS])).then_inc(wide_loaded, 16)
                for j in range(4):
                    a = 64 * (1 - j % 2)
                    rests = w_aux_rest[a:a + 6].rearrange("p (g j) k -> p g j k", j=4)
                    sp.dma_start(rests[:, :, j, 32 * j:32 * j + REST],
                                 dr["keyrows"][p][:, None, P:KEYS].to_broadcast([6, 4, REST])).then_inc(wide_loaded, 16)

                for i, a in enumerate(("hi", "lo")):
                    sp.dma_start(wo[i][:].bitcast(F32), dr["wo_" + a][p]).then_inc(wide_out_loaded, 16)

            def load_narrow(p):
                for i, a in enumerate(("hi", "lo")):
                    sp.dma_start(nq[i][:].bitcast(F32), dr["nq_" + a][p]).then_inc(narrow_loaded, 16)
                    for j in range(4):
                        src = dr["no_" + a][p].rearrange("(v j i) k n -> v j i k n", j=4, i=DN)
                        for v in range(2):
                            dst = no[i][32 * j:32 * j + DN].rearrange("p (k v) n -> p k v n", v=2)
                            sp.dma_start(dst[:, :, v, :].bitcast(F32), src[v, j]).then_inc(narrow_loaded, 16)
                sp.wait_ge(narrow_loaded, p * NARROW + NARROW)

            def cols(src, b):
                return src[..., bass.ds(b * P, P)], src[..., bass.ds(b * REST + B * P, REST)]

            def load_wide_keys(p, b, part):
                def go(dst, src, loaded=wkeys_loaded):
                    sp.dma_start(dst, src).then_inc(loaded, 16)

                def every(buf, par):
                    return buf.rearrange("p (h two) k -> p h two k", two=2)[:, :, par, :]

                if part == 0:
                    for par in range(2):
                        rows = slice(64 * par, 64 * par + 64)
                        main, rest = cols(dr["wk_hib"][p, rows], b)
                        go(every(w_top[rows], par)[:, :, 0:P], main, wtops_loaded)
                        go(every(w_top[rows], par)[:, :, P:KEYS], rest, wtops_loaded)
                elif part < 3:
                    par = part - 1
                    rows = slice(64 * par, 64 * par + 64)
                    main, rest = cols(dr["wk_hi"][p, rows], b)
                    for half in range(2):
                        to = slice(64 * half, 64 * half + 64)
                        go(every(w_pair[to], par).bitcast(F32), main)
                        for jj in (par, par + 2):
                            heads = w_pair_rest[to].rearrange("p (g j) k -> p g j k", j=4)
                            go(heads[:, :, jj, 32 * jj:32 * jj + REST].bitcast(F32),
                               rest.rearrange("p (g two) k -> p g two k", two=2)[:, :, jj // 2, :])
                    main, rest = cols(dr["wk_lob"][p, rows], b)
                    go(every(w_aux[rows], par), main)
                    for jj in (par, par + 2):
                        heads = w_aux_rest[rows].rearrange("p (g j) k -> p g j k", j=4)
                        go(heads[:, :, jj, 32 * jj:32 * jj + REST],
                           rest.rearrange("p (g two) k -> p g two k", two=2)[:, :, jj // 2, :])
                else:
                    go(w_val[:], dr["wv"][p, bass.ds(b, 1)].rearrange("o p n -> p (o n)"))
                    for j in range(4):
                        dst = w_val_rest[32 * j:32 * j + REST].rearrange("p (g j d) -> p g j d", j=4, d=DW)
                        src = dr["wv_rest"][p, bass.ds(b * REST, REST)].rearrange("p (g j d) -> p g j d", j=4, d=DW)
                        go(dst[:, :, j, :], src[:, :, j, :])

            def load_narrow_keys(p, b, j):
                def go(dst, src):
                    sp.dma_start(dst, src).then_inc(nkeys_loaded, 16)

                def by_unit(src, w):
                    return src.rearrange("(u i) k -> i u k", i=DN)

                heads = lambda buf: buf.rearrange("p (u j) k -> p u j k", j=4)[:, :, j, :]
                main, rest = cols(dr["nk_hi"][p], b)
                for half in range(2):
                    to = slice(64 * half + DN * j, 64 * half + DN * j + DN)
                    go(heads(n_pair[to]).bitcast(F32), by_unit(main, P))
                    go(n_pair_rest[to, :, 32 * j:32 * j + REST].bitcast(F32), by_unit(rest, REST))
                lo, lo_rest = cols(dr["nk_lob"][p], b)
                hi, hi_rest = cols(dr["nk_hib"][p], b)
                for par in range(2):
                    to = slice(64 * par + DN * j, 64 * par + DN * j + DN)
                    odd = lambda ap: ap.rearrange("p (v two) k -> p v two k", two=2)[:, :, par, :]
                    go(odd(heads(n_aux[to])), odd(by_unit(lo, P)))
                    go(odd(n_aux_rest[to, :, 32 * j:32 * j + REST]), odd(by_unit(lo_rest, REST)))
                    go(odd(heads(n_top[to]))[:, :, 0:P], odd(by_unit(hi, P)))
                    go(odd(heads(n_top[to]))[:, :, P:KEYS], odd(by_unit(hi_rest, REST)))
                go(n_val_rest[32 * j:32 * j + REST, :, 32 * j:32 * j + 32], dr["nv_rest"][p, bass.ds(b * REST, REST)])
                if j == 0:
                    go(n_val[:], dr["nv"][p, bass.ds(b, 1)].rearrange("o p g d -> p (o g) d"))

            def load_x(t, b):
                sp.dma_start(x[:, t], dr["stream"][bass.ds(b, 1), t].rearrange("o p k n -> p (o k) n")).then_inc(x_loaded[t], 16)

            def load_early(t, b):
                sp.dma_start(xn[:], dr["stream"][bass.ds(b, 1), t].rearrange("o p k n -> p (o k) n")).then_inc(early_loaded.sem, 16)

            def load_masks():
                for t in range(2):
                    for par in range(2):
                        a = 64 * (1 - par)
                        sp.dma_start(q_aux[a:a + 6, t].rearrange("p s (j two) n -> p (s j) two n", two=2)[:, :, par, :],
                                     dr["maskrows"][t][:, None, :].to_broadcast([6, 4, TOK])).then_inc(masks_loaded, 16)

            def store_x(t, it, b):
                wait(sp, dve_output.sem, dve_output.after(it, "output", 2 + t, 1))
                halves = dr["stream"].rearrange("b t p k n -> (b t) p k n")
                sp.dma_start(halves[bass.ds(2 * b + t, 1)].rearrange("o p k n -> p (o k) n"), x[:, t]).then_inc(x_stored[t], 16)
                wait(sp, x_stored[t], 16 * it + 16)

            def spread_inverses(c, batch):
                for h in range(2 if c < 2 else 4):
                    if c < 2:
                        dst = inv_b[64 * h:64 * h + 64, :, :]
                        src = dr["sums"].rearrange("(i h r) n -> r h i n", i=2, r=32)[8 * batch:8 * batch + 1, h]
                    else:
                        dst = inv_b[32 * h:32 * h + 32, :, :]
                        row = 32 * h + DN + 8 * batch
                        src = dr["sums"][row:row + 8, :].rearrange("(i r) n -> r i n", r=4)[0:1]
                    sp.dma_start(dst, src.to_broadcast([dst.shape[0], 2, TOK])).then_inc(inv_loaded.sem, 16 if c >= 2 else 32)

            def one_turn(it, p, b):
                batch = {turn: sp.snap(it + turn) if not isinstance(it, int) else it + turn for turn in (-1, 0, 1)}
                switch = isinstance(it, int)
                if switch:
                    b_before, next_p, next_b = (b - 1) % B, p + (b + 1) // B, (b + 1) % B
                else:
                    b_before, next_p, next_b = sp.snap(b - 1), p, sp.snap(b + 1)
                more = not switch or it + 1 < ITER
                for what, c, k, turn in WINDOW:
                    if not present(it, turn):
                        continue
                    now = batch[turn]
                    if what == "inverse":
                        wait(sp, dve_invert.sem, dve_invert.after(now, what, c, 0))
                        sp.dma_start(dr["sums"], inv[:]).then_inc(sums_stored.sem, 16)
                        wait(sp, sums_stored.sem, sums_stored.after(now, what, c, 0))
                        spread_inverses(c, 0)
                    elif what == "scale" and k + 1 < OUT_BATCHES[c]:
                        wait(sp, pool_scale.sem, pool_scale.after(now, what, c, k))
                        spread_inverses(c, k + 1)
                    elif (what, c, k) == ("output", 3, 1):
                        store_x(1, now, b_before)
                        if not switch or 0 < it < ITER:
                            load_x(1, b)
                        if switch and it == B:
                            wait(sp, pe_output.sem, pe_output.after(now, what, c, k))
                            load_narrow(1)
                    elif what == "query" and (c, k) == (14, 0) and more:
                        wait(sp, act_split.sem, act_split.after(now, "rate", 3, 0))
                        wait(sp, pool_split.sem, pool_split.after(now, "rate", 3, 0))
                        if switch and it == B - 1:
                            sp.wait_ge(wide_query_loaded, 2 * WIDE_QUERY)
                            sp.wait_ge(wide_out_loaded, 2 * WIDE_OUT)
                            sp.wait_ge(wide_loaded, 2 * WIDE)
                        load_early(0, next_b)
                    elif what == "split" and c == 0:
                        wait(sp, act_split.sem, act_split.after(now, what, c, k))
                        wait(sp, pool_split.sem, pool_split.after(now, what, c, k))
                        load_early(1, next_b)
                    elif turn == 1:
                        continue
                    elif what == "turn" and c in NARROW_KEYS_AT and (not switch or it > 0):
                        if c == NARROW_KEYS_AT[0]:
                            wait(sp, pe_value.sem, pe_value.after(batch[-1], "value", STEPS - 1, 1))
                        load_narrow_keys(p, b, NARROW_KEYS_AT.index(c))
                    elif what == "turn" and c in WIDE_KEYS_AT and more:
                        if c == WIDE_KEYS_AT[0]:
                            wait(sp, pe_value.sem, pe_value.after(now, "value", WSTEPS - 1, 1))
                        load_wide_keys(next_p, next_b, WIDE_KEYS_AT.index(c))
                    elif (what, c, k) == ("output", 1, 3) and switch and it == B - 1:
                        wait(sp, pe_output.sem, pe_output.after(now, what, c, k))
                        load_wide(1)
                    elif (what, c, k) == ("output", 2, 1):
                        store_x(0, now, b)
                        if more:
                            load_x(0, next_b)

            load_early(0, 0)
            load_wide(0)
            sp.wait_ge(cleared, CLEARED)
            for part in range(1, 4):
                load_wide_keys(0, 0, part)
            wait(sp, act_split.sem, act_split.after(0, "split", 0, 0))
            wait(sp, pool_split.sem, pool_split.after(0, "split", 0, 0))
            load_early(1, 0)
            load_x(0, 0)
            load_x(1, 0)
            load_narrow(0)
            for part in range(KVN):
                load_narrow_keys(0, 0, part)
            for p in range(2):
                one_turn(B * p, p, 0)
                with sp.Fori(1, B - 1) as b:
                    one_turn(sp.snap(b + B * p), p, sp.snap(b))
                one_turn(B * p + B - 1, p, B - 1)
            one_turn(ITER, 2, 0)

        @block.scalar
        def _(act):
            def do(it, what, n, k):
                if what == "split":
                    wait(act, early_loaded.sem, early_loaded.after(it, what, n, k))
                    wait(act, pe_query.sem, pe_query.before(it, 8 * n))
                    nc.scalar.activation(x_hi[:], xn[:], ACT.Copy).then_inc(act_split.sem, 1)
                elif what == "squares":
                    wait(act, dve_output.sem, dve_output.after(it, "output", n - 2, 3))
                    wait(act, act_split.sem, act_split.before(it, n))
                    wait(act, pool_split.sem, pool_split.before(it, n))
                    nc.scalar.activation(xn[:], x[:, n - 2], ACT.Square).then_inc(act_square.sem, 1)
                elif what == "rate":
                    wait(act, dve_rate.sem, dve_rate.after(it, what, n, k))
                    wait(act, pe_query.sem, pe_query.before(it, 16 + 2 * (n - 2)))
                    nc.scalar.activation(x_hi[:], xn[:], ACT.Copy).then_inc(act_split.sem, 1)
                elif what == "query":
                    wait(act, pe_query.sem, pe_query.after(it, what, n, k))
                    ps = bank_of((what, n, k, 0))
                    s, j = slot(n), 2 * k
                    nc.scalar.activation(q_pair[0:64, s, j, :], ps[0:64], ACT.Copy)
                    nc.scalar.activation(q_pair[64:P, s, j + 1, :], ps[64:P], ACT.Copy).then_inc(act_query.sem, 1)
                elif what in ("rest", "score"):
                    wait(act, pe_score.sem, pe_score.after(it, what, n, k))
                    number = pe_score.number[(what, n, k)]
                    if what == "rest":
                        wait(act, pe_value.sem, pe_value.before(it, pe_value.number[("value", n - 2, 1)] if n >= 2 else 0))
                        dst = probs_rest[:, n % 2, :]
                    else:
                        half = k // 2 if wide(n - 1) or n == 0 else 1
                        wait(act, pe_value.sem, pe_value.before(it, pe_value.number[("value", n - 1, half)] if n else 0))
                        dst = probs[:, k, :]
                    scale = (DW if wide(n) else DN) ** -0.5
                    nc.scalar.activation(dst, score_ps[:, number % 2, :], ACT.Exp, scale=scale).then_inc(act_exp.sem, 1)
                elif what == "turn":
                    if isinstance(it, int) and (it, n) == (0, 0):
                        wait(act, cleared, CLEARED)
                    wait(act, pe_turn.sem, pe_turn.after(it, what, n, k))
                    ps = bank_of((what, n, k, 0))
                    units = range(4) if wide(n) else (n % 2,)
                    for j in units:
                        a = 64 * (1 - j % 2) + ROW_M
                        last = nc.scalar.activation(q_aux[a:a + 4, half_of(n), slot(n), j, :], ps[0:4].bitcast(BF16)[:, 0:TOK], ACT.Copy, scale=-1.0)
                    last.then_inc(act_turn.sem, 1)
                elif what == "value":
                    wait(act, pe_value.sem, pe_value.after(it, what, n, k))
                    tile = first_tile(n) + (k if wide(n) else 0)
                    old, ago = last_in_place(tile)
                    c, i = chunk_of(old)
                    wait(act, dve_low.sem, dve_low.after(it - ago, "low", c, i // 2))
                    wait(act, act_norm.sem, act_norm.after(it - ago, "norm", c, i // 2))
                    nc.scalar.activation(kept[:, place(tile), :], out_ps[:, tile % 2, :], ACT.Copy).then_inc(act_keep.sem, 1)
                elif what == "norm":
                    wait(act, pool_scale.sem, pool_scale.after(it, "scale", n, k))
                    wait(act, pe_output.sem, pe_output.before(it, pe_output_before(n, k)))
                    for i in range(2):
                        tile = chunk_tile(n, 2 * k + i)
                        last = nc.scalar.activation(a_hi[:, i, :], kept[:, place(tile), :], ACT.Copy)
                    last.then_inc(act_norm.sem, 1)

            def pe_output_before(c, k):
                return pe_output.number[("output", c, k)] - 1

            each_batch(act, do)

        @block.gpsimd
        def _(pool):
            for buf in (w_pair, n_pair, w_pair_rest, n_pair_rest, no[0]):
                nc.gpsimd.memset(buf[:].bitcast(F32), 0.0).then_inc(cleared, 1)
            nc.gpsimd.memset(ident[:], 0.0).then_inc(ident_ready, 1)
            pool.wait_ge(ident_ready, 1)
            nc.gpsimd.affine_select(out=ident[:], in_=ident[:], compare_op=ALU.not_equal, fill=1.0, base=0,
                                    pattern=[[-1, P]], channel_multiplier=1).then_inc(ident_ready, 1)
            nc.gpsimd.memset(power[:], -0.5).then_inc(ident_ready, 1)
            pool.wait_ge(ident_ready, 3)
            nc.gpsimd.tensor_copy(ident_bf[:], ident[:]).then_inc(ident_ready, 1)
            pool.wait_ge(ident_ready, 4)
            def fill_rows():
                pool.wait_ge(rows_cleared, ROWS_CLEARED)
                wait(pool, pool_split.sem, pool_split.after(0, "split", 0, 0))
                done = [0]

                def diagonal(rows, pattern, first=0):
                    if done[0]:
                        pool.wait_ge(rows_filled, done[0])
                    done[0] += 1
                    nc.gpsimd.affine_select(out=rows, in_=rows, compare_op=ALU.not_equal, fill=1.0, base=-first,
                                            pattern=pattern, channel_multiplier=1).then_inc(rows_filled, 1)

                for par in range(2):
                    a = 64 * (1 - par) + ROW_M
                    for j in (par, par + 2):
                        heads = w_aux[a:a + 4].rearrange("p (g j) k -> p g j k", j=4)
                        diagonal(heads[:, :, j, :], [[0, 4], [0, P]], first=j)
                        rests = w_aux_rest[a:a + 4].rearrange("p (g j) k -> p g j k", j=4)
                        diagonal(rests[:, :, j, 32 * j:32 * j + REST], [[0, 4], [0, REST]], first=j)
                    for u in (par, par + 2):
                        diagonal(n_aux[a:a + 4, 4 * u:4 * u + 4, :], [[-1, 4], [0, P]])
                        rests = n_aux_rest[a:a + 4, u].rearrange("p (j k) -> p j k", j=4)
                        diagonal(rests[:, :, 0:REST], [[-1, 4], [0, REST]])
                pool.wait_ge(rows_filled, done[0])

            def do(it, what, n, k):
                if what in ("split", "rate"):
                    wait(pool, act_split.sem, act_split.after(it, what, n, k))
                    nc.gpsimd.tensor_tensor(x_lo[:], xn[:], x_hi[:], ALU.subtract).then_inc(pool_split.sem, 1)
                    if (what, n) == ("split", 0) and isinstance(it, int) and it == 0:
                        fill_rows()
                elif what == "square":
                    wait(pool, dve_square.sem, dve_square.after(it, what, n, k))
                    nc.gpsimd.tensor_tensor(rate[:], meansq[:], power[:], ALU.pow).then_inc(pool_rate.sem, 1)
                elif what == "add":
                    tile = first_tile(n)
                    wait(pool, act_keep.sem, act_keep.before(it, tile + 1))
                    if n % 4 == 1:
                        wait(pool, dve_invert.sem, dve_invert.before(it, 2 * (n // 4)))
                        other = kept[:, place(tile - 1), :]
                    else:
                        wait(pool, pool_add.sem, pool_add.after(it, what, n - 1, 0))
                        other = total[:]
                    nc.gpsimd.tensor_tensor(total[:], other, kept[:, place(tile), :], ALU.add).then_inc(pool_add.sem, 1)
                elif what == "scale":
                    wait(pool, inv_loaded.sem, inv_loaded.after(it, what, n, k))
                    wait(pool, act_keep.sem, act_keep.before(it, chunk_tile(n, 2 * k + 1) + 1))
                    for i in range(2):
                        tile = kept[:, place(chunk_tile(n, 2 * k + i)), :]
                        last = nc.gpsimd.tensor_tensor(tile, tile, inv_b[:, i, :], ALU.mult)
                    last.then_inc(pool_scale.sem, 1)

            each_batch(pool, do)

        @block.vector
        def _(dve):
            for buf in (w_top, q_aux, w_aux, w_aux_rest, n_aux, n_aux_rest):
                nc.vector.memset(buf[:].bitcast(F32), 0.0).then_inc(rows_cleared, 1)
            for buf in (n_top, w_val_rest, n_val_rest, sel, sel_rest, no[1]):
                nc.vector.memset(buf[:].bitcast(F32), 0.0).then_inc(cleared, 1)
            dve.wait_ge(rows_cleared, ROWS_CLEARED)
            dve.wait_ge(cleared, CLEARED)
            nc.vector.memset(ones[:], 1.0)
            for g in range(4):
                nc.vector.memset(sel[:, g, 8 * g:8 * g + 8], 1.0)
                for j in range(4):
                    last = nc.vector.memset(sel_rest[32 * j:32 * j + REST, g, 32 * j + 8 * g:32 * j + 8 * g + 8], 1.0)
            last.then_inc(filled, 1)

            def do(it, what, n, k):
                if what == "query":
                    wait(dve, act_query.sem, act_query.after(it, what, n, k))
                    ps = bank_of((what, n, k, 0))
                    t, s, j = half_of(n), slot(n), 2 * k
                    nc.vector.tensor_copy(q_aux[0:64, t, s, j, :], q_pair[0:64, s, j, :])
                    nc.vector.tensor_copy(q_aux[64:P, t, s, j + 1, :], q_pair[64:P, s, j + 1, :]).then_inc(dve_aux.sem, 1)
                    nc.vector.tensor_tensor(q_pair[64:P, s, j, :], ps[0:64], q_pair[0:64, s, j, :], ALU.subtract)
                    last = nc.vector.tensor_tensor(q_pair[0:64, s, j + 1, :], ps[64:P], q_pair[64:P, s, j + 1, :], ALU.subtract)
                    last.then_inc(dve_query.sem, 1)
                elif what == "max":
                    wait(dve, pe_max.sem, pe_max.after(it, what, n, k))
                    if k == 0:
                        wait(dve, pe_turn.sem, pe_turn.before(it, n))
                    sub, pair = k % 4, k // 4
                    src = bank_of((what, n, k, 0))[:, 0:2 * KEYS].rearrange("p (h k) -> p h k", h=2)
                    last = nc.vector.tensor_reduce(tops[:, sub, 2 * pair:2 * pair + 2], src, AX_X, ALU.max)
                    last.then_inc(dve_max.sem, 1)
                elif what == "guard":
                    wait(dve, pool_add.sem, pool_add.after(it, "add", 4 * n + 3, 0))
                    wait(dve, sums_stored.sem, sums_stored.before(it, n))
                    nc.vector.tensor_scalar(inv[:], total[:], TINY, None, ALU.max).then_inc(dve_guard.sem, 1)
                elif what in ("invert", "inverse"):
                    if n < 2:
                        wait(dve, pe_value.sem, pe_value.after(it, "value", 4 * n + 3, 1))
                        wait(dve, sums_stored.sem, sums_stored.before(it, n))
                    else:
                        wait(dve, dve_guard.sem, dve_guard.after(it, "guard", n, 0))
                    half = slice(0, TOK // 2) if what == "invert" else slice(TOK // 2, TOK)
                    nc.vector.reciprocal(inv[:, half], (sum_ps if n < 2 else inv)[:, half]).then_inc(dve_invert.sem, 1)
                elif what == "low":
                    wait(dve, act_norm.sem, act_norm.after(it, "norm", n, k))
                    for i in range(2):
                        tile = chunk_tile(n, 2 * k + i)
                        last = nc.vector.tensor_tensor(a_lo[:, i, :], kept[:, place(tile), :], a_hi[:, i, :], ALU.subtract)
                    last.then_inc(dve_low.sem, 1)
                elif what == "output":
                    t = n % 2
                    if (n, k) == (0, 0) and isinstance(it, int):
                        wait(dve, wide_loaded, WIDE)
                    if k == 0 and n < 2:
                        dve.wait_ge(x_loaded[t], it * 16 + 16)
                    else:
                        wait(dve, dve_output.sem, dve_output.after(it, what, *((n, k - 1) if k else (n - 2, 3))))
                        if k == 0:
                            wait(dve, dve_rate.sem, dve_rate.after(it, "rate", n, 0))
                    for m in range(KC):
                        wait(dve, pe_output.sem, pe_output.after(it, what, n, k) - (KC - 1 - m))
                        dst, ps = x[:, t, m, :], bank_of((what, n, k, m))
                        if n < 2 and k == 0:
                            last = nc.vector.scalar_tensor_tensor(out=dst, in0=ps, scalar=bias[:, m:m + 1], in1=dst, op0=ALU.add, op1=ALU.add)
                        else:
                            last = nc.vector.tensor_tensor(dst, ps, dst, ALU.add)
                        last.then_inc(dve_output.sem, 1)
                elif what == "square":
                    wait(dve, pe_square.sem, pe_square.after(it, what, n, k))
                    last = nc.vector.tensor_scalar(meansq[:], bank_of((what, n, k, 0))[:, 0:4], 1.0 / C, EPS, ALU.mult, ALU.add)
                    last.then_inc(dve_square.sem, 1)
                elif what == "rate":
                    wait(dve, pe_rate.sem, pe_rate.after(it, what, n, k))
                    ps = bank_of((what, n, k, 0))
                    for m in range(KC):
                        last = nc.vector.tensor_tensor(xn[:, m, :], ps, x[:, n - 2, m, :], ALU.mult)
                    last.then_inc(dve_rate.sem, 1)


            each_batch(dve, do)

        @block.tensor
        def _(pe):
            pe.wait_ge(ident_ready, 4)
            pe.wait_ge(wide_query_loaded, WIDE_QUERY)

            def bank(it, use):
                at = [(*g[:3], g[4]) for g in GENERAL].index(use)
                turn = GENERAL[at][3]
                back = at - GB
                while isinstance(it, int) and back >= -len(GENERAL) * (ITER + 1):
                    if 0 <= it - turn + GENERAL[back % len(GENERAL)][3] + back // len(GENERAL) < ITER:
                        break
                    back -= GB
                what, n, k, of, m = GENERAL[back % len(GENERAL)]
                read = reader[what]
                wait(pe, read.sem, read.after(it - turn + of + back // len(GENERAL), what, n, k) - (read.times - 1 - m if what == "output" else 0))
                return general[:, BANK[use], :]

            def do(it, what, n, k):
                if what == "query":
                    if n == WSTEPS:
                        wait(pe, nkeys_loaded, (it + 1) * NKEYS)
                    if n % 4 == 0 and k == 0:
                        key = ("split", n // 4, 0) if wide(n) else ("rate", n // 4, 0)
                        wait(pe, pool_split.sem, pool_split.after(it, *key))
                    ps = bank(it, (what, n, k, 0))
                    w, at = (wq, 2 * (n % 4) + k) if wide(n) else (nq, (n % 4) // 2)
                    at = slice(at * P, at * P + P)
                    pairs = [q for c in range(KC) for q in split3(w[0][:, c, at], w[1][:, c, at], x_hi[:, c, :], x_lo[:, c, :])]
                    for i, (l, r) in enumerate(pairs):
                        last = nc.tensor.matmul(ps, l, r, start=(i == 0), stop=(i == len(pairs) - 1))
                    last.then_inc(pe_query.sem, 1)
                elif what == "max":
                    if k == 0 or k == 4 and wide(n):
                        wait(pe, dve_aux.sem, dve_aux.before(it, queries_for(n) - (k == 0 and wide(n))))
                        if n == 0:
                            wait(pe, wtops_loaded, (it + 1) * WTOPS)
                            if isinstance(it, int):
                                wait(pe, masks_loaded, 16 * 4)
                                wait(pe, wide_loaded, WIDE)
                    ps = bank(it, (what, n, k, 0))
                    sub, pair = slice(k % 4 * P, k % 4 * P + P), k // 4
                    q = q_aux[:, half_of(n), slot(n)]
                    if wide(n):
                        for i in range(2):
                            last = nc.tensor.matmul(ps[:, i * KEYS:(i + 1) * KEYS], q[:, 2 * pair + i, sub],
                                                    w_top[:, 4 * (n % 4) + 2 * pair + i, :], start=True, stop=True)
                    else:
                        h = 4 * (n % 4) + 2 * pair
                        last = nc.tensor.matmul(ps[:, 0:2 * KEYS], q[:, n % 2, sub],
                                                n_top[:, h:h + 2, :].rearrange("p h k -> p (h k)"), start=True, stop=True)
                    last.then_inc(pe_max.sem, 1)
                elif what == "turn":
                    wait(pe, dve_max.sem, dve_max.after(it, "max", n, 7))
                    ps = bank(it, (what, n, k, 0))
                    for sub in range(4):
                        last = nc.tensor.transpose(ps[0:4].bitcast(BF16)[:, sub * P:(sub + 1) * P], tops[:, sub, :], ident_bf[:])
                    last.then_inc(pe_turn.sem, 1)
                elif what in ("rest", "score"):
                    number = pe_score.number[(what, n, k)]
                    ps = score_ps[:, number % 2, :]
                    wait(pe, act_exp.sem, act_exp.before(it, number - 2))
                    if (what, n) == ("rest", 0):
                        wait(pe, wkeys_loaded, (it + 1) * WKEYS)
                    if (what, n) == ("rest", 0) and isinstance(it, int):
                        wait(pe, rows_filled, 16)
                        wait(pe, filled, 1)
                    if what == "rest":
                        wait(pe, dve_query.sem, dve_query.before(it, queries_for(n)))
                        wait(pe, act_turn.sem, act_turn.after(it, "turn", n, 0))
                    s, t, g = slot(n), half_of(n), n % 4
                    pairs = []
                    for j in (range(4) if what == "rest" else (k,)):
                        h = 4 * g + j
                        unit = j if wide(n) else n % 2
                        if what == "score":
                            keys = (w_pair[:, h], w_aux[:, h]) if wide(n) else (n_pair[:, h], n_aux[:, h])
                        elif wide(n):
                            keys = (w_pair_rest[:, h], w_aux_rest[:, h])
                        elif j == 0:
                            keys = (n_pair_rest[:, g], n_aux_rest[:, g])
                        else:
                            continue
                        pairs += [(keys[0], q_pair[:, s, unit, :]), (keys[1], q_aux[:, t, s, unit, :])]
                    for i, (l, r) in enumerate(pairs):
                        last = nc.tensor.matmul(ps, l, r, start=(i == 0), stop=(i == len(pairs) - 1))
                    last.then_inc(pe_score.sem, 1)
                elif what == "value":
                    wait(pe, act_exp.sem, act_exp.after(it, "score", n, 2 * k + 1))
                    tile, g = first_tile(n) + (k if wide(n) else 0), n % 4
                    wait(pe, act_keep.sem, act_keep.before(it, tile - 1))
                    if n in (0, 4) and k == 0:
                        wait(pe, dve_invert.sem, dve_invert.before(it, 2 * (n // 4)) - (4 if n == 0 else 0))
                    out = out_ps[:, tile % 2, :]
                    rest = probs_rest[:, n % 2, :]
                    heads = (2 * k, 2 * k + 1) if wide(n) else range(4)
                    for i, j in enumerate(heads):
                        h = 4 * g + j
                        if wide(n):
                            nc.tensor.matmul(out[64 * i:64 * i + 64], w_val[:, h * DW:(h + 1) * DW], probs[:, j, :],
                                             start=True, stop=False, skip_group_check=True)
                        else:
                            nc.tensor.matmul(out[32 * j:32 * j + 32], n_val[:, g, :], probs[:, j, :],
                                             start=True, stop=False, skip_group_check=True)
                    if wide(n):
                        for i, j in enumerate(heads):
                            h = 4 * g + j
                            nc.tensor.matmul(out[64 * i:64 * i + 64], w_val_rest[:, h * DW:(h + 1) * DW], rest,
                                             start=False, stop=True, skip_group_check=True)
                    else:
                        last = nc.tensor.matmul(out, n_val_rest[:, g, :], rest, start=False, stop=True, skip_group_check=True)
                    for j in heads if wide(n) else ():
                        last = nc.tensor.matmul(sum_ps[32 * j:32 * j + 32, :], sel[:, g, :], probs[:, j, :],
                                                start=(g == 0), stop=False, skip_group_check=True)
                    if k == 1 and wide(n):
                        last = nc.tensor.matmul(sum_ps[:], sel_rest[:, g, :], rest, start=False, stop=(g == 3), skip_group_check=True)
                    last.then_inc(pe_value.sem, 1)
                elif what == "output":
                    if isinstance(it, int) and (n, k) == (0, 0):
                        wait(pe, wide_out_loaded, WIDE_OUT)
                    wait(pe, dve_low.sem, dve_low.after(it, "low", n, k))
                    w = wo if n < 2 else no
                    for m in range(KC):
                        ps = bank(it, (what, n, k, m))
                        rows = slice(m * P, m * P + P)
                        pairs = [q for i in range(2) for q in split3(w[0][:, 2 * k + i, rows], w[1][:, 2 * k + i, rows], a_hi[:, i, :], a_lo[:, i, :])]
                        for i, (l, r) in enumerate(pairs):
                            last = nc.tensor.matmul(ps, l, r, start=(i == 0), stop=(i == len(pairs) - 1))
                        last.then_inc(pe_output.sem, 1)
                elif what == "square":
                    wait(pe, act_square.sem, act_square.after(it, "squares", n, k))
                    ps = bank(it, (what, n, k, 0))
                    for sub in range(4):
                        for c in range(KC):
                            last = nc.tensor.matmul(ps[:, sub:sub + 1], xn[:, c, sub * P:(sub + 1) * P], ones[:],
                                                    start=(c == 0), stop=(c == KC - 1))
                    last.then_inc(pe_square.sem, 1)
                elif what == "rate":
                    wait(pe, pool_rate.sem, pool_rate.after(it, "square", n, k))
                    ps = bank(it, (what, n, k, 0))
                    for sub in range(4):
                        last = nc.tensor.transpose(ps[:, sub * P:(sub + 1) * P], rate[:, sub:sub + 1].to_broadcast([P, P]), ident[:])
                    last.then_inc(pe_rate.sem, 1)

            def queries_for(n):
                return 2 * (n + 1) if wide(n) else 2 * WSTEPS + (n - WSTEPS) // 2 + 1

            each_batch(pe, do)


def store_outputs(nc, dr, out):
    ctx = ExitStack()
    with ctx:
        def sem(name):
            return ctx.enter_context(nc.semaphore(name))

        ident = ctx.enter_context(nc.sbuf_tensor("o_ident", [P, P], F32))
        xt = ctx.enter_context(nc.sbuf_tensor("o_xt", [P, 2 * B, KC, TOK], F32))
        tokens = ctx.enter_context(nc.sbuf_tensor("o_tokens", [P, 2 * B, 4, C], F32))
        ps = ctx.enter_context(nc.psum_tensor("o_ps", [P, 8, 512], F32))
        ident_ready, made = sem("o_ident_ready"), sem("o_transposed")
        loaded = [sem(f"o_loaded{i}") for i in range(2 * B)]
        taken = [sem("o_taken_dve"), sem("o_taken_act")]
        stored = sem("o_stored")
        block = ctx.enter_context(nc.Block())

        @block.sync
        def _(sp):
            for i in range(2 * B):
                sp.dma_start(xt[:, i], dr["stream"][i // 2, i % 2]).then_inc(loaded[i], 16)
            for i in range(2 * B):
                for e in range(2):
                    sp.wait_ge(taken[e], i + 1)
                sp.dma_start(out.rearrange("b (c t p) d -> (b c) p t d", t=4, p=P)[i], tokens[:, i]).then_inc(stored, 16)
            sp.wait_ge(stored, 16 * 2 * B)

        @block.gpsimd
        def _(pool):
            nc.gpsimd.memset(ident[:], 0.0).then_inc(ident_ready, 1)
            pool.wait_ge(ident_ready, 1)
            nc.gpsimd.affine_select(out=ident[:], in_=ident[:], compare_op=ALU.not_equal, fill=1.0, base=0,
                                    pattern=[[-1, P]], channel_multiplier=1).then_inc(ident_ready, 1)

        @block.tensor
        def _(pe):
            pe.wait_ge(ident_ready, 2)
            for i in range(2 * B):
                pe.wait_ge(loaded[i], 16)
                if i >= 4:
                    for e in range(2):
                        pe.wait_ge(taken[e], i - 3)
                for t in range(4):
                    for k in range(KC):
                        col = (t % 2) * C + k * P
                        last = nc.tensor.transpose(ps[:, 2 * (i % 4) + t // 2, col:col + P], xt[:, i, k, t * P:(t + 1) * P], ident[:])
                last.then_inc(made, 1)

        def take(eng, copy, e):
            for i in range(2 * B):
                eng.wait_ge(made, i + 1)
                copy(tokens[:, i, 2 * e:2 * e + 2, :].rearrange("p t d -> p (t d)"), ps[:, 2 * (i % 4) + e, :]).then_inc(taken[e], 1)

        @block.vector
        def _(dve):
            take(dve, nc.vector.tensor_copy, 0)

        @block.scalar
        def _(act):
            take(act, lambda dst, src: nc.scalar.activation(dst, src, ACT.Copy), 1)


_INS = ["x", "ctx_2048", "mask_S_fk1", "mask_S_fk0"]
for _p in range(2):
    _INS += [f"L{2 * _p}_xattn_{_w}" for _w in ("Wq", "Wk", "Wv", "Wo", "bo", "token_indices_A", "token_indices_B")]
    _INS += [f"L{2 * _p + 1}_xattn_{_w}" for _w in ("wq", "wk", "wv", "wo", "norm_w")]


def build(nc, ins, out):
    dr = scratch_tensors(nc)
    prepare(nc, ins, dr)
    run_layers(nc, ins, dr)
    store_outputs(nc, dr, out)


def kernel(**inputs):
    import numpy as _np
    import concourse.bacc as _bacc
    from concourse import mybir as _mybir
    from concourse.bass_utils import run_bass_kernel_spmd as _run

    nc = _bacc.Bacc("TRN2", target_bir_lowering=False, num_devices=1)
    arrays, ins = {}, {}
    for name in _INS:
        a = _np.ascontiguousarray(inputs[name])
        arrays[f"in_{name}_dram"] = a
        ins[name] = nc.dram_tensor(f"in_{name}_dram", a.shape, _mybir.dt.from_np(a.dtype), kind="ExternalInput").ap()
    out = nc.dram_tensor("out_0_dram", (B, S, C), _mybir.dt.float32, kind="ExternalOutput").ap()
    build(nc, ins, out)
    r = _run(nc, [arrays], core_ids=[0])
    return r.results[0]["out_0_dram"]
```
